# Optimizing a Trainium2 kernel written in Bass

```python
import numpy as np
import jax
import jax.numpy as jnp

def _softmax(x, axis=-1):
    return jax.nn.softmax(x, axis=axis)

def _gelu(x):
    return jax.nn.gelu(x, approximate=True)

def _silu(x):
    return jax.nn.silu(x)

def _sigmoid(x):
    return jax.nn.sigmoid(x)

def _layernorm(x, axis=-1, eps=1e-05):
    m = jnp.mean(x, axis=axis, keepdims=True)
    v = jnp.var(x, axis=axis, keepdims=True)
    return (x - m) / jnp.sqrt(v + eps)

def _scatter_add(tgt, idx, src, axis=0):
    return tgt.at[idx].add(src)

def _segment_sum(src, seg, n):
    return jax.ops.segment_sum(src, seg, n)
kernel_name = 'mk_seq_postln_d2_jaxref_r8_20961e'

def setup_inputs(seed: int=0):
    np.random.seed(seed)
    _w = jnp.asarray

    def _L0_attn_setup():
        import jax, jax.numpy as jnp
        import numpy as np
        KEY_DIM = 128
        SCALE = KEY_DIM ** (-0.5)
        key = jax.random.key(seed)
        k1, k2, k3, k4 = jax.random.split(key, 4)
        B, S, E = (4, 256, 128)
        x = jax.random.normal(k1, (B, S, E), dtype=jnp.float32)
        WQ = jax.random.normal(k2, (KEY_DIM, E), dtype=jnp.float32) * E ** (-0.5)
        WK = jax.random.normal(k3, (KEY_DIM, E), dtype=jnp.float32) * E ** (-0.5)
        WV = jax.random.normal(k4, (KEY_DIM, E), dtype=jnp.float32) * E ** (-0.5)
        return {'x': x, 'WQ': WQ, 'WK': WK, 'WV': WV}
    _L0_attn_in = _L0_attn_setup()

    def _L0_ffn_setup():
        import jax, jax.numpy as jnp
        import numpy as np
        DIM = 128
        NQ = 16
        NKV = 4
        HD = DIM // NQ
        HID = 256
        E = 8
        B, S = (1, 128)
        EPS = 1e-06

        def rmsnorm(x, w):
            ms = jnp.mean(x * x, axis=-1, keepdims=True)
            return w * (x * jax.lax.rsqrt(ms + EPS))

        def rope_tables(seq_len, head_dim):
            inv_freq = 1.0 / 10000.0 ** (jnp.arange(0, head_dim, 2, dtype=jnp.float32) / head_dim)
            t = jnp.arange(seq_len, dtype=jnp.float32)
            freqs = jnp.einsum('i,j->ij', t, inv_freq)
            return (jnp.cos(freqs), jnp.sin(freqs))

        def apply_rope(x, cos, sin):
            c = cos[None, :, None, :]
            s = sin[None, :, None, :]
            half = x.shape[-1] // 2
            x1, x2 = (x[..., :half], x[..., half:])
            return jnp.concatenate([x1 * c - x2 * s, x1 * s + x2 * c], axis=-1)

        def _forward(x, ln1_w, ln2_w, Wq, bq, Wk, bk, Wv, bv, qn_w, kn_w, Wg, bg, Wo, bo, Wr, br, W1, b1, W2, b2):
            batch, seq, _ = x.shape
            cos, sin = rope_tables(seq, HD)
            h = rmsnorm(x, ln1_w)
            q = (h @ Wq + bq).reshape(batch, seq, NQ, HD)
            k = (h @ Wk + bk).reshape(batch, seq, NKV, HD)
            v = (h @ Wv + bv).reshape(batch, seq, NKV, HD)
            q = rmsnorm(apply_rope(q, cos, sin), qn_w)
            k = rmsnorm(apply_rope(k, cos, sin), kn_w)
            rep = NQ // NKV
            k = jnp.repeat(k, rep, axis=2)
            v = jnp.repeat(v, rep, axis=2)
            scores = jnp.einsum('bthd,bshd->bhts', q, k) / np.sqrt(HD)
            causal = jnp.tril(jnp.ones((seq, seq), dtype=bool))
            scores = jnp.where(causal[None, None], scores, -jnp.inf)
            attn = jax.nn.softmax(scores, axis=-1)
            out = jnp.einsum('bhts,bshd->bthd', attn, v)
            gate = jax.nn.sigmoid(out @ Wg + bg)
            out = (out * gate).reshape(batch, seq, DIM)
            x = x + out @ Wo + bo
            h2 = rmsnorm(x, ln2_w)
            logits = h2 @ Wr + br
            top1 = jnp.argmax(logits, axis=-1).reshape(-1)
            xt = h2.reshape(-1, DIM)
            u = jnp.einsum('td,edf->tef', xt, W1) + b1
            u1, u2 = (u[..., :HID], u[..., HID:])
            act = u1 * jax.nn.sigmoid(u2)
            y_all = jnp.einsum('teh,ehd->ted', act, W2) + b2
            y = jnp.take_along_axis(y_all, top1[:, None, None], axis=1)[:, 0, :]
            return x + y.reshape(batch, seq, DIM)
        key = jax.random.key(seed)
        ks = jax.random.split(key, 20)
        sc = lambda fan_in: 1.0 / np.sqrt(fan_in)
        d = {}
        d['x'] = jax.random.normal(ks[0], (B, S, DIM), dtype=jnp.float32)
        d['ln1_w'] = jnp.ones((DIM,), jnp.float32)
        d['ln2_w'] = jnp.ones((DIM,), jnp.float32)
        d['Wq'] = jax.random.normal(ks[1], (DIM, DIM), jnp.float32) * sc(DIM)
        d['bq'] = jnp.zeros((DIM,), jnp.float32)
        d['Wk'] = jax.random.normal(ks[2], (DIM, HD * NKV), jnp.float32) * sc(DIM)
        d['bk'] = jnp.zeros((HD * NKV,), jnp.float32)
        d['Wv'] = jax.random.normal(ks[3], (DIM, HD * NKV), jnp.float32) * sc(DIM)
        d['bv'] = jnp.zeros((HD * NKV,), jnp.float32)
        d['qn_w'] = jnp.ones((HD,), jnp.float32)
        d['kn_w'] = jnp.ones((HD,), jnp.float32)
        d['Wg'] = jax.random.normal(ks[4], (HD, HD), jnp.float32) * sc(HD)
        d['bg'] = jnp.zeros((HD,), jnp.float32)
        d['Wo'] = jax.random.normal(ks[5], (DIM, DIM), jnp.float32) * sc(DIM)
        d['bo'] = jnp.zeros((DIM,), jnp.float32)
        d['Wr'] = jax.random.normal(ks[6], (DIM, E), jnp.float32) * sc(DIM)
        d['br'] = jnp.zeros((E,), jnp.float32)
        d['W1'] = jax.random.normal(ks[7], (E, DIM, 2 * HID), jnp.float32) * sc(DIM)
        d['b1'] = jnp.zeros((E, 2 * HID), jnp.float32)
        d['W2'] = jax.random.normal(ks[8], (E, HID, DIM), jnp.float32) * sc(HID)
        d['b2'] = jnp.zeros((E, DIM), jnp.float32)
        return d
    _L0_ffn_in = _L0_ffn_setup()

    def _L1_attn_setup():
        import jax, jax.numpy as jnp
        import numpy as np
        B, T, C, NH = (32, 64, 128, 16)
        DH = C // NH

        def _rope_tables(seq_len, dim):
            inv = 1.0 / 10000.0 ** (np.arange(0, dim, 2, dtype=np.float32) / dim)
            freqs = np.arange(seq_len, dtype=np.float32)[:, None] * inv[None, :]
            return (jnp.asarray(np.cos(freqs)), jnp.asarray(np.sin(freqs)))

        def _apply_rope(x, cos, sin):
            b, t, h, d = x.shape
            d2 = d // 2
            xv = x.reshape(b, t, h, d2, 2)
            x0, x1 = (xv[..., 0], xv[..., 1])
            c = cos[None, :t, None, :]
            s = sin[None, :t, None, :]
            o0 = x0 * c - x1 * s
            o1 = x0 * s + x1 * c
            return jnp.stack([o0, o1], axis=-1).reshape(b, t, h, d)
        key = jax.random.key(seed)
        ks = jax.random.split(key, 5)
        scale = 0.02
        return {'x': jax.random.normal(ks[0], (B, T, C), dtype=jnp.float32), 'Wq': jax.random.normal(ks[1], (C, C), dtype=jnp.float32) * scale, 'Wk': jax.random.normal(ks[2], (C, C), dtype=jnp.float32) * scale, 'Wv': jax.random.normal(ks[3], (C, C), dtype=jnp.float32) * scale, 'Wo': jax.random.normal(ks[4], (C, C), dtype=jnp.float32) * scale}
    _L1_attn_in = _L1_attn_setup()

    def _L1_ffn_setup():
        import jax, jax.numpy as jnp
        import numpy as np
        DIM = 128
        DEPTH = 2
        HEADS = 8
        DIM_HEAD = 64
        WINDOW = 64
        INNER = HEADS * DIM_HEAD
        HID = int(DIM * 4 * 2 / 3)
        B, N = (2, 1024)
        QK_SCALE = 8.0

        def shift_token(t):
            t1, t2 = jnp.split(t, 2, axis=-1)
            t2 = jnp.pad(t2, ((0, 0), (1, 0), (0, 0)))[:, :-1]
            return jnp.concatenate([t1, t2], axis=-1)

        def l2norm(t):
            return t / jnp.clip(jnp.linalg.norm(t, axis=-1, keepdims=True), 1e-12)

        def rotate_half(x):
            x1, x2 = jnp.split(x, 2, axis=-1)
            return jnp.concatenate([-x2, x1], axis=-1)

        def rotary_xpos(q, k):
            n = q.shape[-2]
            half_idx = jnp.arange(0, DIM_HEAD, 2, dtype=jnp.float32)
            inv_freq = 1.0 / 10000.0 ** (half_idx / DIM_HEAD)
            t = jnp.arange(n, dtype=jnp.float32)
            freqs = t[:, None] * inv_freq[None, :]
            freqs = jnp.concatenate([freqs, freqs], axis=-1)
            base = (half_idx + 0.4 * DIM_HEAD) / (1.4 * DIM_HEAD)
            power = (t - n // 2) / float(WINDOW // 2)
            scale = base[None, :] ** power[:, None]
            scale = jnp.concatenate([scale, scale], axis=-1)
            cos, sin = (jnp.cos(freqs), jnp.sin(freqs))
            q = q * cos * scale + rotate_half(q) * sin * scale
            k = k * cos / scale + rotate_half(k) * sin / scale
            return (q, k)

        def local_attention(q, k, v):
            b, h, n, d = q.shape
            w = n // WINDOW
            bq = q.reshape(b, h, w, WINDOW, d) * QK_SCALE
            bk = k.reshape(b, h, w, WINDOW, d)
            bv = v.reshape(b, h, w, WINDOW, d)

            def look_around(t):
                p = jnp.pad(t, ((0, 0), (0, 0), (1, 0), (0, 0), (0, 0)))
                return jnp.concatenate([p[:, :, :w], p[:, :, 1:]], axis=3)
            bk, bv = (look_around(bk), look_around(bv))
            bt = jnp.arange(n).reshape(w, WINDOW)
            btp = jnp.pad(bt, ((1, 0), (0, 0)), constant_values=-1)
            btk = jnp.concatenate([btp[:w], btp[1:]], axis=1)
            sim = jnp.einsum('bhwid,bhwjd->bhwij', bq, bk)
            i = bt[:, :, None]
            j = btk[:, None, :]
            mask = (i < j) | (i > j + WINDOW) | (j == -1)
            sim = jnp.where(mask, -jnp.finfo(sim.dtype).max, sim)
            attn = jax.nn.softmax(sim, axis=-1)
            out = jnp.einsum('bhwij,bhwjd->bhwid', attn, bv)
            return out.reshape(b, h, n, d)

        def _layer(x, wqkv, qs, ksc, wo, lg, lb, w1, b1, w2, b2):
            b, n, _ = x.shape
            h = shift_token(x)
            qkv = h @ wqkv
            q, k, v = jnp.split(qkv, 3, axis=-1)
            to_heads = lambda t: t.reshape(b, n, HEADS, DIM_HEAD).transpose(0, 2, 1, 3)
            q, k, v = (to_heads(q), to_heads(k), to_heads(v))
            q = l2norm(q) * qs
            k = l2norm(k) * ksc
            q, k = rotary_xpos(q, k)
            o = local_attention(q, k, v)
            o = o.transpose(0, 2, 1, 3).reshape(b, n, INNER)
            x = x + o @ wo
            h = shift_token(x)
            mu = h.mean(-1, keepdims=True)
            var = h.var(-1, keepdims=True)
            h = (h - mu) / jnp.sqrt(var + 1e-05) * lg + lb
            h = h @ w1 + b1
            a, g = jnp.split(h, 2, axis=-1)
            h = a * jax.nn.gelu(g, approximate=False)
            x = x + h @ w2 + b2
            return x
        key = jax.random.key(seed)
        ks = jax.random.split(key, 6)
        return {'x': jax.random.normal(ks[0], (B, N, DIM), jnp.float32), 'wqkv': jax.random.normal(ks[1], (DEPTH, DIM, 3 * INNER), jnp.float32) * 0.02, 'q_scale': jnp.ones((DEPTH, DIM_HEAD), jnp.float32), 'k_scale': jnp.ones((DEPTH, DIM_HEAD), jnp.float32), 'wo': jax.random.normal(ks[2], (DEPTH, INNER, DIM), jnp.float32) * 0.02, 'ln_g': jnp.ones((DEPTH, DIM), jnp.float32), 'ln_b': jnp.zeros((DEPTH, DIM), jnp.float32), 'w1': jax.random.normal(ks[3], (DEPTH, DIM, 2 * HID), jnp.float32) * 0.02, 'b1': jnp.zeros((DEPTH, 2 * HID), jnp.float32), 'w2': jax.random.normal(ks[4], (DEPTH, HID, DIM), jnp.float32) * 0.02, 'b2': jnp.zeros((DEPTH, DIM), jnp.float32)}
    _L1_ffn_in = _L1_ffn_setup()
    _d = {'L0_attn_x': _L0_attn_in['x'], 'L0_attn_WQ': _L0_attn_in['WQ'], 'L0_attn_WK': _L0_attn_in['WK'], 'L0_attn_WV': _L0_attn_in['WV'], 'L0_ffn_ln1_w': _L0_ffn_in['ln1_w'], 'L0_ffn_ln2_w': _L0_ffn_in['ln2_w'], 'L0_ffn_Wq': _L0_ffn_in['Wq'], 'L0_ffn_bq': _L0_ffn_in['bq'], 'L0_ffn_Wk': _L0_ffn_in['Wk'], 'L0_ffn_bk': _L0_ffn_in['bk'], 'L0_ffn_Wv': _L0_ffn_in['Wv'], 'L0_ffn_bv': _L0_ffn_in['bv'], 'L0_ffn_qn_w': _L0_ffn_in['qn_w'], 'L0_ffn_kn_w': _L0_ffn_in['kn_w'], 'L0_ffn_Wg': _L0_ffn_in['Wg'], 'L0_ffn_bg': _L0_ffn_in['bg'], 'L0_ffn_Wo': _L0_ffn_in['Wo'], 'L0_ffn_bo': _L0_ffn_in['bo'], 'L0_ffn_Wr': _L0_ffn_in['Wr'], 'L0_ffn_br': _L0_ffn_in['br'], 'L0_ffn_W1': _L0_ffn_in['W1'], 'L0_ffn_b1': _L0_ffn_in['b1'], 'L0_ffn_W2': _L0_ffn_in['W2'], 'L0_ffn_b2': _L0_ffn_in['b2'], 'L1_attn_Wq': _L1_attn_in['Wq'], 'L1_attn_Wk': _L1_attn_in['Wk'], 'L1_attn_Wv': _L1_attn_in['Wv'], 'L1_attn_Wo': _L1_attn_in['Wo'], 'L1_ffn_wqkv': _L1_ffn_in['wqkv'], 'L1_ffn_q_scale': _L1_ffn_in['q_scale'], 'L1_ffn_k_scale': _L1_ffn_in['k_scale'], 'L1_ffn_wo': _L1_ffn_in['wo'], 'L1_ffn_ln_g': _L1_ffn_in['ln_g'], 'L1_ffn_ln_b': _L1_ffn_in['ln_b'], 'L1_ffn_w1': _L1_ffn_in['w1'], 'L1_ffn_b1': _L1_ffn_in['b1'], 'L1_ffn_w2': _L1_ffn_in['w2'], 'L1_ffn_b2': _L1_ffn_in['b2']}
    _x0 = _d['L0_attn_x']
    _d['L0_attn_x'] = jax.random.normal(jax.random.fold_in(jax.random.key(seed), 1), (32, 256, 128), dtype=_x0.dtype)
    del _x0
    return _d

def reference(L0_attn_x, L0_attn_WQ, L0_attn_WK, L0_attn_WV, L0_ffn_ln1_w, L0_ffn_ln2_w, L0_ffn_Wq, L0_ffn_bq, L0_ffn_Wk, L0_ffn_bk, L0_ffn_Wv, L0_ffn_bv, L0_ffn_qn_w, L0_ffn_kn_w, L0_ffn_Wg, L0_ffn_bg, L0_ffn_Wo, L0_ffn_bo, L0_ffn_Wr, L0_ffn_br, L0_ffn_W1, L0_ffn_b1, L0_ffn_W2, L0_ffn_b2, L1_attn_Wq, L1_attn_Wk, L1_attn_Wv, L1_attn_Wo, L1_ffn_wqkv, L1_ffn_q_scale, L1_ffn_k_scale, L1_ffn_wo, L1_ffn_ln_g, L1_ffn_ln_b, L1_ffn_w1, L1_ffn_b1, L1_ffn_w2, L1_ffn_b2):

    def _L0_attn_ref(x, WQ, WK, WV):
        import jax, jax.numpy as jnp
        import numpy as np
        KEY_DIM = 128
        SCALE = KEY_DIM ** (-0.5)
        q = jnp.einsum('bse,ke->bsk', x, WQ)
        k = jnp.einsum('bse,ke->bsk', x, WK)
        v = jnp.einsum('bse,ve->bsv', x, WV)
        scores = jnp.einsum('bsk,btk->bst', q, k) * SCALE
        masked = jnp.where(jnp.tril(scores) == 0, -jnp.inf, scores)
        attn = jax.nn.softmax(masked, axis=-1)
        return jnp.einsum('bst,btv->bsv', attn, v)

    def _L0_ffn_ref(x, ln1_w, ln2_w, Wq, bq, Wk, bk, Wv, bv, qn_w, kn_w, Wg, bg, Wo, bo, Wr, br, W1, b1, W2, b2):
        import jax, jax.numpy as jnp
        import numpy as np
        DIM = 128
        NQ = 16
        NKV = 4
        HD = DIM // NQ
        HID = 256
        E = 8
        B, S = (1, 128)
        EPS = 1e-06

        def rmsnorm(x, w):
            ms = jnp.mean(x * x, axis=-1, keepdims=True)
            return w * (x * jax.lax.rsqrt(ms + EPS))

        def rope_tables(seq_len, head_dim):
            inv_freq = 1.0 / 10000.0 ** (jnp.arange(0, head_dim, 2, dtype=jnp.float32) / head_dim)
            t = jnp.arange(seq_len, dtype=jnp.float32)
            freqs = jnp.einsum('i,j->ij', t, inv_freq)
            return (jnp.cos(freqs), jnp.sin(freqs))

        def apply_rope(x, cos, sin):
            c = cos[None, :, None, :]
            s = sin[None, :, None, :]
            half = x.shape[-1] // 2
            x1, x2 = (x[..., :half], x[..., half:])
            return jnp.concatenate([x1 * c - x2 * s, x1 * s + x2 * c], axis=-1)

        def _forward(x, ln1_w, ln2_w, Wq, bq, Wk, bk, Wv, bv, qn_w, kn_w, Wg, bg, Wo, bo, Wr, br, W1, b1, W2, b2):
            batch, seq, _ = x.shape
            cos, sin = rope_tables(seq, HD)
            h = rmsnorm(x, ln1_w)
            q = (h @ Wq + bq).reshape(batch, seq, NQ, HD)
            k = (h @ Wk + bk).reshape(batch, seq, NKV, HD)
            v = (h @ Wv + bv).reshape(batch, seq, NKV, HD)
            q = rmsnorm(apply_rope(q, cos, sin), qn_w)
            k = rmsnorm(apply_rope(k, cos, sin), kn_w)
            rep = NQ // NKV
            k = jnp.repeat(k, rep, axis=2)
            v = jnp.repeat(v, rep, axis=2)
            scores = jnp.einsum('bthd,bshd->bhts', q, k) / np.sqrt(HD)
            causal = jnp.tril(jnp.ones((seq, seq), dtype=bool))
            scores = jnp.where(causal[None, None], scores, -jnp.inf)
            attn = jax.nn.softmax(scores, axis=-1)
            out = jnp.einsum('bhts,bshd->bthd', attn, v)
            gate = jax.nn.sigmoid(out @ Wg + bg)
            out = (out * gate).reshape(batch, seq, DIM)
            x = x + out @ Wo + bo
            h2 = rmsnorm(x, ln2_w)
            logits = h2 @ Wr + br
            top1 = jnp.argmax(logits, axis=-1).reshape(-1)
            xt = h2.reshape(-1, DIM)
            u = jnp.einsum('td,edf->tef', xt, W1) + b1
            u1, u2 = (u[..., :HID], u[..., HID:])
            act = u1 * jax.nn.sigmoid(u2)
            y_all = jnp.einsum('teh,ehd->ted', act, W2) + b2
            y = jnp.take_along_axis(y_all, top1[:, None, None], axis=1)[:, 0, :]
            return x + y.reshape(batch, seq, DIM)
        return _forward(x, ln1_w, ln2_w, Wq, bq, Wk, bk, Wv, bv, qn_w, kn_w, Wg, bg, Wo, bo, Wr, br, W1, b1, W2, b2)

    def _L1_attn_ref(x, Wq, Wk, Wv, Wo):
        import jax, jax.numpy as jnp
        import numpy as np
        B, T, C, NH = (32, 64, 128, 16)
        DH = C // NH

        def _rope_tables(seq_len, dim):
            inv = 1.0 / 10000.0 ** (np.arange(0, dim, 2, dtype=np.float32) / dim)
            freqs = np.arange(seq_len, dtype=np.float32)[:, None] * inv[None, :]
            return (jnp.asarray(np.cos(freqs)), jnp.asarray(np.sin(freqs)))

        def _apply_rope(x, cos, sin):
            b, t, h, d = x.shape
            d2 = d // 2
            xv = x.reshape(b, t, h, d2, 2)
            x0, x1 = (xv[..., 0], xv[..., 1])
            c = cos[None, :t, None, :]
            s = sin[None, :t, None, :]
            o0 = x0 * c - x1 * s
            o1 = x0 * s + x1 * c
            return jnp.stack([o0, o1], axis=-1).reshape(b, t, h, d)
        b, t, c = x.shape
        cos, sin = _rope_tables(t, DH)
        q = (x @ Wq.T).reshape(b, t, NH, DH)
        k = (x @ Wk.T).reshape(b, t, NH, DH)
        v = (x @ Wv.T).reshape(b, t, NH, DH)
        q = _apply_rope(q, cos, sin)
        k = _apply_rope(k, cos, sin)
        q = q.transpose(0, 2, 1, 3)
        k = k.transpose(0, 2, 1, 3)
        v = v.transpose(0, 2, 1, 3)
        att = jnp.einsum('bhqd,bhkd->bhqk', q.astype(jnp.float32), k.astype(jnp.float32))
        att = att * DH ** (-0.5)
        att = jax.nn.softmax(att, axis=-1).astype(v.dtype)
        out = jnp.einsum('bhqk,bhkd->bhqd', att, v)
        out = out.transpose(0, 2, 1, 3).reshape(b, t, c)
        return out @ Wo.T

    def _L1_ffn_ref(x, wqkv, q_scale, k_scale, wo, ln_g, ln_b, w1, b1, w2, b2):
        import jax, jax.numpy as jnp
        import numpy as np
        DIM = 128
        DEPTH = 2
        HEADS = 8
        DIM_HEAD = 64
        WINDOW = 64
        INNER = HEADS * DIM_HEAD
        HID = int(DIM * 4 * 2 / 3)
        B, N = (2, 1024)
        QK_SCALE = 8.0

        def shift_token(t):
            t1, t2 = jnp.split(t, 2, axis=-1)
            t2 = jnp.pad(t2, ((0, 0), (1, 0), (0, 0)))[:, :-1]
            return jnp.concatenate([t1, t2], axis=-1)

        def l2norm(t):
            return t / jnp.clip(jnp.linalg.norm(t, axis=-1, keepdims=True), 1e-12)

        def rotate_half(x):
            x1, x2 = jnp.split(x, 2, axis=-1)
            return jnp.concatenate([-x2, x1], axis=-1)

        def rotary_xpos(q, k):
            n = q.shape[-2]
            half_idx = jnp.arange(0, DIM_HEAD, 2, dtype=jnp.float32)
            inv_freq = 1.0 / 10000.0 ** (half_idx / DIM_HEAD)
            t = jnp.arange(n, dtype=jnp.float32)
            freqs = t[:, None] * inv_freq[None, :]
            freqs = jnp.concatenate([freqs, freqs], axis=-1)
            base = (half_idx + 0.4 * DIM_HEAD) / (1.4 * DIM_HEAD)
            power = (t - n // 2) / float(WINDOW // 2)
            scale = base[None, :] ** power[:, None]
            scale = jnp.concatenate([scale, scale], axis=-1)
            cos, sin = (jnp.cos(freqs), jnp.sin(freqs))
            q = q * cos * scale + rotate_half(q) * sin * scale
            k = k * cos / scale + rotate_half(k) * sin / scale
            return (q, k)

        def local_attention(q, k, v):
            b, h, n, d = q.shape
            w = n // WINDOW
            bq = q.reshape(b, h, w, WINDOW, d) * QK_SCALE
            bk = k.reshape(b, h, w, WINDOW, d)
            bv = v.reshape(b, h, w, WINDOW, d)

            def look_around(t):
                p = jnp.pad(t, ((0, 0), (0, 0), (1, 0), (0, 0), (0, 0)))
                return jnp.concatenate([p[:, :, :w], p[:, :, 1:]], axis=3)
            bk, bv = (look_around(bk), look_around(bv))
            bt = jnp.arange(n).reshape(w, WINDOW)
            btp = jnp.pad(bt, ((1, 0), (0, 0)), constant_values=-1)
            btk = jnp.concatenate([btp[:w], btp[1:]], axis=1)
            sim = jnp.einsum('bhwid,bhwjd->bhwij', bq, bk)
            i = bt[:, :, None]
            j = btk[:, None, :]
            mask = (i < j) | (i > j + WINDOW) | (j == -1)
            sim = jnp.where(mask, -jnp.finfo(sim.dtype).max, sim)
            attn = jax.nn.softmax(sim, axis=-1)
            out = jnp.einsum('bhwij,bhwjd->bhwid', attn, bv)
            return out.reshape(b, h, n, d)

        def _layer(x, wqkv, qs, ksc, wo, lg, lb, w1, b1, w2, b2):
            b, n, _ = x.shape
            h = shift_token(x)
            qkv = h @ wqkv
            q, k, v = jnp.split(qkv, 3, axis=-1)
            to_heads = lambda t: t.reshape(b, n, HEADS, DIM_HEAD).transpose(0, 2, 1, 3)
            q, k, v = (to_heads(q), to_heads(k), to_heads(v))
            q = l2norm(q) * qs
            k = l2norm(k) * ksc
            q, k = rotary_xpos(q, k)
            o = local_attention(q, k, v)
            o = o.transpose(0, 2, 1, 3).reshape(b, n, INNER)
            x = x + o @ wo
            h = shift_token(x)
            mu = h.mean(-1, keepdims=True)
            var = h.var(-1, keepdims=True)
            h = (h - mu) / jnp.sqrt(var + 1e-05) * lg + lb
            h = h @ w1 + b1
            a, g = jnp.split(h, 2, axis=-1)
            h = a * jax.nn.gelu(g, approximate=False)
            x = x + h @ w2 + b2
            return x
        for l in range(DEPTH):
            x = _layer(x, wqkv[l], q_scale[l], k_scale[l], wo[l], ln_g[l], ln_b[l], w1[l], b1[l], w2[l], b2[l])
        return x
    x = L0_attn_x
    x = _layernorm(x + _L0_attn_ref(x, L0_attn_WQ, L0_attn_WK, L0_attn_WV), axis=-1)
    x = _layernorm(x + _L0_ffn_ref(x, L0_ffn_ln1_w, L0_ffn_ln2_w, L0_ffn_Wq, L0_ffn_bq, L0_ffn_Wk, L0_ffn_bk, L0_ffn_Wv, L0_ffn_bv, L0_ffn_qn_w, L0_ffn_kn_w, L0_ffn_Wg, L0_ffn_bg, L0_ffn_Wo, L0_ffn_bo, L0_ffn_Wr, L0_ffn_br, L0_ffn_W1, L0_ffn_b1, L0_ffn_W2, L0_ffn_b2), axis=-1)
    x = _layernorm(x + _L1_attn_ref(x, L1_attn_Wq, L1_attn_Wk, L1_attn_Wv, L1_attn_Wo), axis=-1)
    x = _layernorm(x + _L1_ffn_ref(x, L1_ffn_wqkv, L1_ffn_q_scale, L1_ffn_k_scale, L1_ffn_wo, L1_ffn_ln_g, L1_ffn_ln_b, L1_ffn_w1, L1_ffn_b1, L1_ffn_w2, L1_ffn_b2), axis=-1)
    return x

_drawn_inputs = setup_inputs


def setup_inputs(seed=0):
    import zlib

    import numpy as np

    out = dict(_drawn_inputs(seed))
    spreads = {'L0_ffn_ln1_w': (1.0, 0.2),
     'L0_ffn_ln2_w': (1.0, 0.2),
     'L0_ffn_bq': (0.0, 0.1),
     'L0_ffn_bk': (0.0, 0.1),
     'L0_ffn_bv': (0.0, 0.1),
     'L0_ffn_qn_w': (1.0, 0.2),
     'L0_ffn_kn_w': (1.0, 0.2),
     'L0_ffn_bg': (0.0, 0.352),
     'L0_ffn_bo': (0.0, 0.1),
     'L0_ffn_br': (0.0, 0.1),
     'L0_ffn_b1': (0.0, 0.286),
     'L0_ffn_b2': (0.0, 0.1),
     'L1_ffn_q_scale': (1.0, 0.6),
     'L1_ffn_k_scale': (1.0, 0.6),
     'L1_ffn_ln_g': (1.0, 0.6),
     'L1_ffn_ln_b': (0.0, 0.8),
     'L1_ffn_b1': (0.0, 0.8),
     'L1_ffn_b2': (0.0, 0.558)}
    factors = {'L1_attn_Wq': 8.0,
     'L1_attn_Wk': 8.0,
     'L1_attn_Wv': 8.0,
     'L1_attn_Wo': 8.0,
     'L1_ffn_wqkv': 2.81,
     'L1_ffn_wo': 2.818,
     'L1_ffn_w1': 6.627,
     'L1_ffn_w2': 6.474}
    for name, (base, spread) in spreads.items():
        noise = np.random.default_rng([zlib.crc32(name.encode()), seed]).standard_normal(out[name].shape)
        drawn = base * np.exp(spread * noise) if base else spread * noise
        out[name] = jnp.asarray(drawn.astype(out[name].dtype))
    for name, factor in factors.items():
        out[name] = (out[name] * factor).astype(out[name].dtype)
    return out
```

```python
from contextlib import ExitStack

import numpy as np
import concourse.bass as bass
from concourse import mybir

F32 = mybir.dt.float32
BF16 = mybir.dt.bfloat16
U32 = mybir.dt.uint32
ALU = mybir.AluOpType
ACT = mybir.ActivationFunctionType
AX_X = mybir.AxisListType.X

P = 128
D = 128
S = 256
TILES = S // P
LN_EPS = 1e-5
RMS_EPS = 1e-6
MASKED = -1e30


class Room:

    def __init__(self, nc, stack, stage):
        self.nc, self.stack, self.stage, self.sems = nc, stack, stage, []

    def sb(self, name, shape, dt=F32):
        return self.stack.enter_context(self.nc.sbuf_tensor(f"{self.stage}_{name}", shape, dt))

    def psum(self, name, shape, dt=F32):
        return self.stack.enter_context(self.nc.psum_tensor(f"{self.stage}_{name}", shape, dt))

    def sem(self, name):
        made = self.stack.enter_context(self.nc.semaphore(f"{self.stage}_{name}"))
        self.sems.append(made)
        return made

    def block(self):
        self.stack.callback(self.clear)
        return self.stack.enter_context(self.nc.Block())

    def clear(self):
        numbers = sorted(s.num for s in self.sems)
        starts = [a for a in numbers if a - 1 not in numbers]
        ends = [a + 1 for a in numbers if a + 1 not in numbers]
        with self.nc.Block() as block:
            @block.gpsimd
            def _(pool):
                for start, end in zip(starts, ends):
                    pool.sem_clear(range(start, end))


def seq(x_res, n):
    return x_res[:, bass.ds(n * (TILES * D), TILES * D)].rearrange("p (t d) -> p t d", t=TILES)


def tile(x_res, n, t):
    return x_res[:, bass.ds(n * (TILES * D) + t * D, D)]


def single_head_attention(nc, x_res, x_dram, wq_t, wk_t, wv_t, ident, neg_half, ln_eps, tril):
    n_seq = x_dram.shape[0]
    x_tiles = x_dram.rearrange("b (t p) d -> b p t d", p=P)
    scale = float(D) ** -0.5
    with ExitStack() as stack:
        room = Room(nc, stack, "sha")
        w = room.sb("w", [D, 3, D])
        x_in = [room.sb(f"x_in{s}", [P, TILES, D]) for s in range(2)]
        x_t = [room.sb(f"x_t{s}", [D, S]) for s in range(2)]
        qk_t = [room.sb(f"qk_t{s}", [D, 2, S]) for s in range(2)]
        v = [room.sb(f"v{s}", [P, TILES, D]) for s in range(2)]
        scores = [room.sb(f"scores{s}", [P, 3 * P]) for s in range(2)]
        dead = [room.sb(f"dead{s}", [P, 3 * P]) for s in range(2)]
        probs = [room.sb(f"probs{s}", [P, 3 * P]) for s in range(2)]
        probs_t = [room.sb(f"probs_t{s}", [P, 3 * P]) for s in range(2)]
        top = [room.sb(f"top{s}", [P, TILES]) for s in range(2)]
        bias = [room.sb(f"bias{s}", [P, TILES]) for s in range(2)]
        total = [room.sb(f"total{s}", [P, TILES]) for s in range(2)]
        inv = [room.sb(f"inv{s}", [P, TILES]) for s in range(2)]
        y = [room.sb(f"y{s}", [P, TILES, D]) for s in range(2)]
        stats = [room.sb(f"stats{s}", [P, TILES, 6]) for s in range(2)]
        mean_var = [room.sb(f"mean_var{s}", [P, TILES, 2]) for s in range(2)]
        veps = [room.sb(f"veps{s}", [P, TILES]) for s in range(2)]
        rstd = [room.sb(f"rstd{s}", [P, TILES]) for s in range(2)]
        ps_a = [room.psum(f"ps_a{s}", [P, 512]) for s in range(2)]
        ps_qk = [room.psum(f"ps_qk{s}", [P, 2, S]) for s in range(2)]
        ps_v = [room.psum(f"ps_v{s}", [P, TILES, D]) for s in range(2)]
        ps_p = [room.psum(f"ps_p{s}", [P, 512]) for s in range(2)]
        w_loaded = room.sem("w_loaded")
        x_loaded = [room.sem(f"x_loaded{s}") for s in range(2)]
        xt_done = room.sem("xt_done")
        xt_copied = room.sem("xt_copied")
        qk_done = room.sem("qk_done")
        qk_copied = room.sem("qk_copied")
        v_done = room.sem("v_done")
        v_copied = room.sem("v_copied")
        scores_done = room.sem("scores_done")
        bias_ready = room.sem("bias_ready")
        probs_ready = room.sem("probs_ready")
        pt_done = room.sem("pt_done")
        pt_copied = room.sem("pt_copied")
        out_done = room.sem("out_done")
        var_ready = room.sem("var_ready")
        rstd_ready = room.sem("rstd_ready")
        x_free = room.sem("x_free")
        row = [slice(0, P), slice(P, 3 * P)]
        block = room.block()

        @block.sync
        def _(sp):
            for c, src in enumerate((wq_t, wk_t, wv_t)):
                sp.dma_start(w[:, c, :], src).then_inc(w_loaded, 16)
            with sp.Fori(0, n_seq // 2) as i:
                for s in range(2):
                    n = i * 2 + s
                    sp.wait_ge(x_free, n + 1)
                    src = x_tiles[bass.ds(n, 1)].rearrange("b p t d -> (b p) t d")
                    sp.dma_start(x_in[s][:, :, :], src).then_inc(x_loaded[s], 16)

        @block.tensor
        def _(pe):
            pe.wait_ge(w_loaded, 48)
            with pe.Fori(0, n_seq // 2) as i:
                for s in range(2):
                    n = i * 2 + s
                    pe.wait_ge(x_loaded[s], i * 16 + 16)
                    for t in range(TILES):
                        last = pe.transpose(ps_a[s][:, t * P:(t + 1) * P], x_in[s][:, t, :], ident[:, :])
                    last.then_inc(xt_done, 1)
                for s in range(2):
                    n = i * 2 + s
                    pe.wait_ge(xt_copied, n + 1)
                    for c in range(2):
                        last = pe.matmul(ps_qk[s][:, c, :], w[:, c, :], x_t[s][:, :], start=True, stop=True)
                    last.then_inc(qk_done, 1)
                    for t in range(TILES):
                        last = pe.matmul(ps_v[s][:, t, :], x_t[s][:, t * P:(t + 1) * P], w[:, 2, :],
                                         start=True, stop=True)
                    last.then_inc(v_done, 1)
                for s in range(2):
                    n = i * 2 + s
                    pe.wait_ge(qk_copied, n + 1)
                    pe.matmul(ps_a[s][:, row[0]], qk_t[s][:, 0, 0:P], qk_t[s][:, 1, 0:P], start=True, stop=True)
                    pe.matmul(ps_a[s][:, row[1]], qk_t[s][:, 0, P:S], qk_t[s][:, 1, :],
                              start=True, stop=True).then_inc(scores_done, 1)
                for s in range(2):
                    n = i * 2 + s
                    pe.wait_ge(probs_ready, n + 1)
                    for b in range(3):
                        last = pe.transpose(ps_p[s][:, b * P:(b + 1) * P], probs[s][:, b * P:(b + 1) * P],
                                            ident[:, :])
                    last.then_inc(pt_done, 1)
                for s in range(2):
                    n = i * 2 + s
                    pe.wait_ge(pt_copied, n + 1)
                    pe.wait_ge(v_copied, n + 1)
                    pe.matmul(ps_p[s][:, 0:D], probs_t[s][:, 0:P], v[s][:, 0, :], start=True, stop=True)
                    for t in range(TILES):
                        last = pe.matmul(ps_p[s][:, D:2 * D], probs_t[s][:, (1 + t) * P:(2 + t) * P],
                                         v[s][:, t, :], start=t == 0, stop=t == 1)
                    last.then_inc(out_done, 1)

        @block.scalar
        def _(act):
            with act.Fori(0, n_seq // 2) as i:
                for s in range(2):
                    n = i * 2 + s
                    act.wait_ge(xt_done, n + 1)
                    act.copy(x_t[s][:, :], ps_a[s][:, 0:S]).then_inc(xt_copied, 1)
                for s in range(2):
                    n = i * 2 + s
                    act.wait_ge(v_done, n + 1)
                    act.copy(v[s][:, :, :], ps_v[s][:, :, :]).then_inc(v_copied, 1)
                for s in range(2):
                    n = i * 2 + s
                    act.wait_ge(bias_ready, n + 1)
                    for t in range(TILES):
                        last = act.activation(probs[s][:, row[t]], scores[s][:, row[t]], ACT.Exp,
                                              bias=bias[s][:, t:t + 1], scale=scale,
                                              accum_out=total[s][:, t:t + 1])
                    last.then_inc(probs_ready, 1)

        @block.gpsimd
        def _(pool):
            with pool.Fori(0, n_seq // 2) as i:
                for s in range(2):
                    pool.wait_ge(var_ready, i * 2 + (s + 1))
                    pool.tensor_tensor(veps[s][:, :], mean_var[s][:, :, 1], ln_eps[:, 0:TILES], ALU.add)
                    pool.drain()
                    pool.tensor_tensor(rstd[s][:, :], veps[s][:, :], neg_half[:, 0:TILES],
                                       ALU.pow).then_inc(rstd_ready, 1)

        @block.vector
        def _(dve):
            dve.sem_inc(x_free, 2)
            with dve.Fori(0, n_seq // 2) as i:
                for s in range(2):
                    n = i * 2 + s
                    dve.wait_ge(qk_done, n + 1)
                    dve.tensor_copy(qk_t[s][:, :, :], ps_qk[s][:, :, :]).then_inc(qk_copied, 1)
                for s in range(2):
                    n = i * 2 + s
                    dve.wait_ge(scores_done, n + 1)
                    dve.tensor_tensor(scores[s][:, :], ps_a[s][:, 0:3 * P], tril[:, :], ALU.mult)
                    dve.drain()
                    dve.tensor_scalar(dead[s][:, :], scores[s][:, :], 0.0, MASKED, ALU.is_equal, ALU.mult)
                    dve.drain()
                    for t in range(TILES):
                        dve.tensor_tensor_reduce(scores[s][:, row[t]], scores[s][:, row[t]], dead[s][:, row[t]],
                                                 1.0, -3e38, ALU.add, ALU.max, top[s][:, t:t + 1])
                    dve.drain()
                    dve.tensor_scalar(bias[s][:, :], top[s][:, :], -scale, None, ALU.mult).then_inc(bias_ready, 1)
                for s in range(2):
                    n = i * 2 + s
                    dve.wait_ge(pt_done, n + 1)
                    dve.tensor_copy(probs_t[s][:, :], ps_p[s][:, 0:3 * P]).then_inc(pt_copied, 1)
                    dve.reciprocal(inv[s][:, :], total[s][:, :])
                for s in range(2):
                    n = i * 2 + s
                    dve.drain()
                    dve.wait_ge(out_done, n + 1)
                    for t in range(TILES):
                        last = dve.scalar_tensor_tensor(y[s][:, t, :], ps_p[s][:, t * D:(t + 1) * D],
                                                        inv[s][:, t:t + 1], x_in[s][:, t, :], ALU.mult, ALU.add)
                    last.then_inc(x_free, 1)
                    dve.drain()
                    for t in range(TILES):
                        dve.bn_stats(stats[s][:, t, :], y[s][:, t, :])
                    dve.drain()
                    for t in range(TILES):
                        last = dve.bn_aggr(mean_var[s][:, t, :], stats[s][:, t, :])
                    last.then_inc(var_ready, 1)
                for s in range(2):
                    n = i * 2 + s
                    dve.drain()
                    dve.wait_ge(rstd_ready, n + 1)
                    for t in range(TILES):
                        dve.tensor_scalar(tile(x_res, n, t), y[s][:, t, :], mean_var[s][:, t, 0:1],
                                          rstd[s][:, t:t + 1], ALU.subtract, ALU.mult)


HEADS = 16
HD = 8
ROWS = 64
QUADS = HEADS // 4


class Step:

    def __init__(self, third, offset):
        self.third, self.offset = third, offset
        self.n = third * 3 + offset
        self.slot = offset % 3
        self.turn = third + offset // 3

    def __add__(self, k):
        return Step(self.third, self.offset + k)

    def __sub__(self, k):
        return Step(self.third, self.offset - k)


def run_steps(eng, n_seq, step):
    step(Step(0, 0), True, False, False, True)
    step(Step(0, 1), True, True, False, True)
    assert (n_seq - 5) % 3 == 0
    with eng.Fori(0, (n_seq - 5) // 3) as i:
        for c in range(3):
            step(Step(i, 2 + c), True, True, True, True)
    step(Step(0, n_seq - 3), True, True, True, True)
    step(Step(0, n_seq - 2), True, True, True, True)
    step(Step(0, n_seq - 1), True, True, True, False)
    step(Step(0, n_seq), False, True, True, False)
    step(Step(0, n_seq + 1), False, False, True, False)


def many_head_attention(nc, n_seq, x_res, out_res, consts, w, gated):
    ident, ident_bf, neg_half, eps_ln, eps_rms = (consts[k] for k in ("ident", "ident_bf", "neg_half", "ln_eps", "rms_eps"))
    NK = 8 if gated else 16
    NV = 4 if gated else 16
    NQK = HEADS + NK
    W = NQK * HD + NV * HD
    scale = float(HD) ** -0.5
    with ExitStack() as stack:
        room = Room(nc, stack, "gqa" if gated else "mha")
        x_in = [room.sb(f"x_in{r}", [P, TILES, D]) for r in range(3)]
        x_t = [room.sb(f"x_t{r}", [D, S]) for r in range(3)]
        qk = room.sb("qk", [P, TILES * NQK, HD])
        turned = room.sb("turned", [P, TILES * NQK, HD])
        swapped = room.sb("swapped", [P, TILES * NQK, HD])
        sq_sum = room.sb("sq_sum", [P, TILES * NQK])
        sq_eps = room.sb("sq_eps", [P, TILES * NQK])
        head_rms = room.sb("head_rms", [P, TILES * NQK])
        rest_q = room.sb("rest_q", [P, TILES * HEADS, HD])
        rest_k = room.sb("rest_k", [P, TILES * NK, HD])
        q_rows = room.sb("q_rows", [P, TILES * HEADS, ROWS], BF16)
        k_rows = room.sb("k_rows", [P, TILES * NK, ROWS], BF16)
        q_t = [room.sb(f"q_t{r}", [P, HEADS // 2, S], BF16) for r in range(3)]
        k_t = [room.sb(f"k_t{r}", [P, NK // 2, S], BF16) for r in range(3)]
        v_ext = [room.sb(f"v_ext{r}", [P, TILES, NV, 32]) for r in range(3)]
        neg_top = room.sb("neg_top", [P, TILES, HEADS])
        m_rows = room.sb("m_rows", [P, TILES, P], BF16)
        m_t = [room.sb(f"m_t{r}", [P, S], BF16) for r in range(3)]
        probs = room.sb("probs", [P, 8, 2 * S])
        o_t = room.sb("o_t", [P, QUADS, S])
        inv = room.sb("inv", [P, TILES, HEADS])
        attn = room.sb("attn", [P, TILES, D])
        attn_t = room.sb("attn_t", [D, S])
        gate_t = room.sb("gate_t", [D, S])
        x_ms = room.sb("x_ms", [P, TILES])
        x_ms_eps = room.sb("x_ms_eps", [P, TILES])
        x_rms = room.sb("x_rms", [P, TILES])
        sq = room.sb("sq", [P, D])
        y = room.sb("y", [P, TILES, D])
        stats = room.sb("stats", [P, TILES, 6])
        mean_var = room.sb("mean_var", [P, TILES, 2])
        rstd = room.sb("rstd", [P, TILES])
        ps_s = [room.psum(f"ps_s{r}", [P, 2 * S]) for r in range(2)]
        ps_st = [room.psum(f"ps_st{r}", [P, 2 * S]) for r in range(2)]
        ps_pv = room.psum("ps_pv", [P, QUADS, S])
        front = [room.psum(f"front{r}", [P, 512]) for r in range(2)]
        front_bf = [f[:, :].bitcast(BF16) for f in front]

        names = ("w_loaded xt_done xt_copied x_ms_ready x_rms_ready qkv_done qkv_taken sq_ready head_rms_ready "
                 "q_rows_ready k_rows_ready qt_done qt_copied kt_done kt_copied v_ready s_done max_done "
                 "m_rows_ready mt_done mt_copied st_done exp_done pv_done ot_copied ot_done attn_ready at_done "
                 "at_copied z_done z_exp_ready gated_ready y_done y_taken var_ready rstd_ready zeroed")
        sem = {k: room.sem(k) for k in names.split()}
        x_loaded = [room.sem(f"x_loaded{r}") for r in range(3)]
        block = room.block()

        def kgroup(h):
            return (h // 2) * NK // HEADS

        def vhead(h):
            return h * NV // HEADS

        @block.sync
        def _(sp):
            def load(s):
                sp.dma_start(x_in[s.slot][:, :, :], seq(x_res, s.n)).then_inc(x_loaded[s.slot], 16)

            for to, of in w["loads"]:
                sp.dma_start(to, of).then_inc(sem["w_loaded"], 16)
            for n in range(3):
                load(Step(0, n))
            with sp.Fori(0, (n_seq - 5) // 3) as i:
                for c in range(3):
                    s = Step(i, 3 + c)
                    sp.wait_ge(sem["xt_done"], (s - 2).n)
                    if gated:
                        sp.wait_ge(sem["x_ms_ready"], (s - 2).n)
                    load(s)
            for n in range(n_seq - 2, n_seq):
                sp.wait_ge(sem["xt_done"], n - 2)
                if gated:
                    sp.wait_ge(sem["x_ms_ready"], n - 2)
                load(Step(0, n))

        @block.tensor
        def _(pe):
            def turn_x(s):
                pe.wait_ge(x_loaded[s.slot], s.turn * 16 + 16)
                for t in range(TILES):
                    last = pe.transpose(front[1][:, t * P:(t + 1) * P], x_in[s.slot][:, t, :], ident[:, :])
                last.then_inc(sem["xt_done"], 1)

            def project_qkv(s):
                pe.wait_ge(sem["xt_copied"], s.n + 1)
                for t in range(TILES):
                    pe.matmul(front[t][:, 0:W], x_t[s.slot][:, t * P:(t + 1) * P], w["qkv"][:, 0:W],
                              start=True, stop=True).then_inc(sem["qkv_done"], 1)

            def turn_rows(s, rows, heads, ready, copied, done):
                pe.wait_ge(sem[ready], s.n + 1)
                if rows is q_rows:
                    pe.wait_ge(sem["qkv_taken"], s.n + 1)
                for t in range(TILES):
                    if rows is k_rows:
                        pe.wait_ge(sem["qt_copied"], s.n * 2 + (t + 1))
                    for j in range(heads // 2):
                        last = pe.transpose(front_bf[t][:, j * P:(j + 1) * P],
                                            rows[:, t * heads + 2 * j:t * heads + 2 * j + 2, :],
                                            ident_bf[:, :])
                    last.then_inc(sem[done], 1)

            def turn_m(s):
                pe.wait_ge(sem["m_rows_ready"], s.n + 1)
                for t in range(TILES):
                    last = pe.transpose(front_bf[0][:, t * P:(t + 1) * P], m_rows[:, t, :], ident_bf[:, :])
                last.then_inc(sem["mt_done"], 1)

            def scores(s, h):
                half = slice(ROWS * (h % 2), ROWS * (h % 2) + ROWS)
                q, k, out = q_t[s.slot][half, h // 2, :], k_t[s.slot][half, kgroup(h), :], ps_s[h % 2]
                if gated:
                    pe.matmul(out[:, 0:P], q[:, 0:P], k[:, 0:P], start=True, stop=False)
                    pe.matmul(out[:, P:3 * P], q[:, P:S], k[:, :], start=False, stop=False)
                    diagonal = out[:, :].rearrange("p (b c) -> p b c", c=S)[:, :, 0:P]
                    last = pe.matmul(diagonal, ident_bf[:, :], consts["mask_qk"][:, :, :], start=False, stop=True)
                else:
                    pe.matmul(out[:, 0:S], q[:, 0:P], k[:, :], start=True, stop=True)
                    last = pe.matmul(out[:, S:2 * S], q[:, P:S], k[:, :], start=True, stop=True)
                last.then_inc(sem["s_done"], 1)

            def scores_t(s, h):
                half = slice(ROWS * (h % 2), ROWS * (h % 2) + ROWS)
                q, k, out = q_t[s.slot][half, h // 2, :], k_t[s.slot][half, kgroup(h), :], ps_st[h % 2]
                pick, m = consts["pick"][half, h // 2, :], m_t[s.slot][half, :]
                pe.matmul(out[:, 0:S], pick, m, start=True, stop=False)
                if gated:
                    pe.matmul(out[:, S:3 * P], pick, m[:, P:S], start=False, stop=False)
                    pe.matmul(out[:, 0:S], k[:, 0:P], q, start=False, stop=False)
                    pe.matmul(out[:, S:3 * P], k[:, P:S], q[:, P:S], start=False, stop=False)
                    diagonal = out[:, :].rearrange("p (b c) -> p b c", c=S)[:, :, 0:P]
                    last = pe.matmul(diagonal, ident_bf[:, :], consts["mask_kq"][:, :, :], start=False, stop=True)
                else:
                    pe.matmul(out[:, S:2 * S], pick, m, start=False, stop=False)
                    pe.matmul(out[:, 0:S], k[:, 0:P], q, start=False, stop=False)
                    last = pe.matmul(out[:, S:2 * S], k[:, P:S], q, start=False, stop=True)
                last.then_inc(sem["st_done"], 1)

            def weigh_values(s, g):
                pe.wait_ge(sem["exp_done"], s.n * HEADS + 4 * (g + 1))
                for t in range(TILES):
                    for c in range(4):
                        h = 4 * g + c
                        slot = probs[:, h % 8, :]
                        if t == 0:
                            out, p = ps_pv[32 * c:32 * c + 32, g, :], slot[:, 0:S]
                        elif gated:
                            out, p = ps_pv[32 * c:32 * c + 32, g, P:S], slot[:, S:3 * P]
                        else:
                            out, p = ps_pv[32 * c:32 * c + 32, g, :], slot[:, S:2 * S]
                        last = pe.matmul(out, v_ext[s.slot][:, t, vhead(h), :], p, start=t == 0, stop=t == 1)
                last.then_inc(sem["pv_done"], 1)

            def turn_outputs(s):
                pe.wait_ge(sem["ot_copied"], s.n + 1)
                pe.wait_ge(sem["y_taken"], s.n)
                for t in range(TILES):
                    for g in range(QUADS):
                        last = pe.transpose(front[t][:, g * P:(g + 1) * P], o_t[:, g, t * P:(t + 1) * P], ident[:, :])
                last.then_inc(sem["ot_done"], 1)

            def turn_attn(s):
                pe.wait_ge(sem["attn_ready"], s.n + 1)
                for t in range(TILES):
                    last = pe.transpose(front[0][:, t * P:(t + 1) * P], attn[:, t, :], ident[:, :])
                last.then_inc(sem["at_done"], 1)

            def gate_logits(s):
                pe.wait_ge(sem["at_copied"], s.n + 1)
                pe.matmul(front[1][:, 0:S], w["gate"][:, :], attn_t[:, :], start=True, stop=True)\
                  .then_inc(sem["z_done"], 1)

            def project_out(s):
                pe.wait_ge(sem["gated_ready" if gated else "at_copied"], s.n + 1)
                for t in range(TILES):
                    last = pe.matmul(front[0][:, t * D:(t + 1) * D], attn_t[:, t * P:(t + 1) * P], w["out"][:, :],
                                     start=True, stop=True)
                last.then_inc(sem["y_done"], 1)

            def step(s, do_scores, attend, finish, do_front):
                if attend:
                    pe.wait_ge(sem["mt_copied"], s.n)
                for h in range(HEADS):
                    if do_scores:
                        if h == 0:
                            pe.wait_ge(sem["kt_copied"], s.n * 2 + 2)
                        if not (isinstance(s.n, int) and s.n == 0 and h < 2):
                            pe.wait_ge(sem["max_done"], s.n * HEADS + (h - 1))
                        scores(s, h)
                    if attend:
                        if not (isinstance(s.n, int) and s.n == 1 and h < 2):
                            pe.wait_ge(sem["exp_done"], (s - 1).n * HEADS + (h - 1))
                        scores_t(s - 1, h)
                    if h == 1 and finish:
                        weigh_values(s - 2, 3)
                    if attend and h in (5, 9, 13):
                        if h == 5 and finish:
                            pe.wait_ge(sem["ot_copied"], (s - 1).n)
                        weigh_values(s - 1, (h - 5) // 4)
                    if finish:
                        if h == 3:
                            turn_outputs(s - 2)
                        if h == 5:
                            turn_attn(s - 2)
                        if h == 6 and gated:
                            gate_logits(s - 2)
                        if h == 7:
                            project_out(s - 2)
                    if do_front:
                        if h == 8:
                            turn_x(s + 1)
                        if h == 9:
                            if finish:
                                pe.wait_ge(sem["y_taken"], (s - 1).n)
                            project_qkv(s + 1)
                        if h == 14:
                            turn_rows(s + 1, q_rows, HEADS, "q_rows_ready", None, "qt_done")
                        if h == 15:
                            turn_rows(s + 1, k_rows, NK, "k_rows_ready", None, "kt_done")
                if do_scores:
                    if do_front:
                        pe.wait_ge(sem["kt_copied"], (s + 1).n * 2 + 1)
                    else:
                        pe.wait_ge(sem["y_taken"], (s - 1).n)
                    turn_m(s)

            pe.wait_ge(sem["w_loaded"], 16 * w["count"])
            pe.wait_ge(sem["zeroed"], 1)
            turn_x(Step(0, 0))
            project_qkv(Step(0, 0))
            turn_rows(Step(0, 0), q_rows, HEADS, "q_rows_ready", None, "qt_done")
            turn_rows(Step(0, 0), k_rows, NK, "k_rows_ready", None, "kt_done")
            run_steps(pe, n_seq, step)

        @block.scalar
        def _(act):
            def take_x(s):
                act.wait_ge(sem["xt_done"], s.n + 1)
                if gated:
                    ins = act.activation(x_t[s.slot][:, :], front[1][:, 0:S], ACT.Copy, scale=w["ln1"][:, 0:1])
                else:
                    ins = act.copy(x_t[s.slot][:, :], front[1][:, 0:S])
                ins.then_inc(sem["xt_copied"], 1)

            def take_qkv(s):
                for t in range(TILES):
                    if t == 0:
                        act.wait_ge(sem["qkv_done"], s.n * 2 + 1)
                    else:
                        act.wait_ge(sem["qkv_done"], s.n * 2 + 2)
                    act.copy(qk[:, t * NQK:(t + 1) * NQK, :],
                             front[t][:, 0:NQK * HD].rearrange("p (h d) -> p h d", d=HD))
                    last = act.copy(v_ext[s.slot][:, t, :, 0:HD],
                                    front[t][:, NQK * HD:W].rearrange("p (h d) -> p h d", d=HD))
                last.then_inc(sem["qkv_taken"], 1)

            def take_rows(s, t, done, dst, heads, copied):
                act.wait_ge(sem[done], s.n * 2 + (t + 1))
                act.copy(dst[s.slot][:, :, t * P:(t + 1) * P],
                         front_bf[t][:, 0:heads // 2 * P].rearrange("p (j c) -> p j c", c=P))\
                   .then_inc(sem[copied], 1)

            def take_outputs(s):
                act.wait_ge(sem["pv_done"], s.n * QUADS + QUADS)
                for g in range(0, QUADS, 2):
                    last = act.copy(o_t[:, g:g + 2, :], ps_pv[:, g:g + 2, :])
                last.then_inc(sem["ot_copied"], 1)

            def take_attn(s):
                act.wait_ge(sem["at_done"], s.n + 1)
                act.copy(attn_t[:, :], front[0][:, 0:S]).then_inc(sem["at_copied"], 1)

            def gate_exp(s):
                act.wait_ge(sem["z_done"], s.n + 1)
                act.activation(gate_t[:, :], front[1][:, 0:S], ACT.Exp, bias=w["neg_bg"][:, 0:1], scale=-1.0)\
                   .then_inc(sem["z_exp_ready"], 1)

            def step(s, do_scores, attend, finish, do_front):
                for h in range(HEADS):
                    if attend:
                        a = s - 1
                        act.wait_ge(sem["st_done"], a.n * HEADS + (h + 1))
                        if not (isinstance(s.n, int) and s.n == 1 and h < 8):
                            act.wait_ge(sem["pv_done"], a.n * QUADS + (h // 4 - 1))
                        n_cols = 3 * P if gated else 4 * P
                        act.activation(probs[:, h % 8, 0:n_cols], ps_st[h % 2][:, 0:n_cols], ACT.Exp, scale=scale)\
                           .then_inc(sem["exp_done"], 1)
                    if finish:
                        if h == 1:
                            take_outputs(s - 2)
                        if h == 5:
                            take_attn(s - 2)
                        if h == 6 and gated:
                            gate_exp(s - 2)
                    if do_front:
                        if h == 8:
                            take_x(s + 1)
                        if h == 9 and not gated:
                            take_qkv(s + 1)
                        if h == 15:
                            take_rows(s + 1, 0, "qt_done", q_t, HEADS, "qt_copied")
                            take_rows(s + 1, 1, "qt_done", q_t, HEADS, "qt_copied")
                            take_rows(s + 1, 0, "kt_done", k_t, NK, "kt_copied")
                            take_rows(s + 1, 1, "kt_done", k_t, NK, "kt_copied")

            take_x(Step(0, 0))
            if not gated:
                take_qkv(Step(0, 0))
            for t in range(TILES):
                take_rows(Step(0, 0), t, "qt_done", q_t, HEADS, "qt_copied")
            for t in range(TILES):
                take_rows(Step(0, 0), t, "kt_done", k_t, NK, "kt_copied")
            run_steps(act, n_seq, step)

        @block.gpsimd
        def _(pool):
            def x_norm(s):
                pool.wait_ge(sem["x_ms_ready"], s.n + 1)
                pool.tensor_tensor(x_ms_eps[:, :], x_ms[:, :], eps_rms[:, 0:TILES], ALU.add)
                pool.drain()
                pool.tensor_tensor(x_rms[:, :], x_ms_eps[:, :], neg_half[:, 0:TILES], ALU.pow)\
                    .then_inc(sem["x_rms_ready"], 1)

            def head_norm(s):
                pool.wait_ge(sem["sq_ready"], s.n + 1)
                pool.tensor_tensor(sq_eps[:, :], sq_sum[:, :], w["eighth"][:, 0:TILES * NQK], ALU.mult)
                pool.drain()
                pool.tensor_tensor(sq_eps[:, :], sq_eps[:, :], eps_rms[:, 0:TILES * NQK], ALU.add)
                pool.drain()
                pool.tensor_tensor(head_rms[:, :], sq_eps[:, :], neg_half[:, 0:TILES * NQK], ALU.pow)\
                    .then_inc(sem["head_rms_ready"], 1)

            def layer_norm(s):
                pool.wait_ge(sem["var_ready"], s.n + 1)
                pool.tensor_tensor(x_ms_eps[:, :], mean_var[:, :, 1], eps_ln[:, 0:TILES], ALU.add)
                pool.drain()
                pool.tensor_tensor(rstd[:, :], x_ms_eps[:, :], neg_half[:, 0:TILES], ALU.pow)\
                    .then_inc(sem["rstd_ready"], 1)

            def step(s, do_scores, attend, finish, do_front):
                if finish and not gated:
                    layer_norm(s - 2)
                if do_front and gated:
                    x_norm(s + 1)
                    head_norm(s + 1)

            if gated:
                x_norm(Step(0, 0))
                head_norm(Step(0, 0))
            run_steps(pool, n_seq, step)

        @block.vector
        def _(dve):
            cos, sin = consts["cos"], consts["sin"]

            def by_tile(t):
                return t[:, :, :].rearrange("p (t h) d -> p t h d", t=TILES)

            def x_squares(s):
                dve.wait_ge(x_loaded[s.slot], s.turn * 16 + 16)
                for t in range(TILES):
                    x = x_in[s.slot][:, t, :]
                    last = dve.tensor_tensor_reduce(sq[:, :], x, x, 1.0 / D, 0.0, ALU.mult, ALU.add, x_ms[:, t:t + 1])
                    dve.drain()
                last.then_inc(sem["x_ms_ready"], 1)

            def take_qkv(s):
                dve.wait_ge(sem["x_rms_ready"], s.n + 1)
                for t in range(TILES):
                    dve.wait_ge(sem["qkv_done"], s.n * 2 + (t + 1))
                    dve.scalar_tensor_tensor(qk[:, t * NQK:(t + 1) * NQK, :].rearrange("p h d -> p (h d)"),
                                             front[t][:, 0:NQK * HD], x_rms[:, t:t + 1], w["b_qkv"][:, 0:NQK * HD],
                                             ALU.mult, ALU.add)
                    last = dve.scalar_tensor_tensor(
                        v_ext[s.slot][:, t, :, 0:HD], front[t][:, NQK * HD:W].rearrange("p (h d) -> p h d", d=HD),
                        x_rms[:, t:t + 1], w["b_qkv"][:, NQK * HD:W].rearrange("p (h d) -> p h d", d=HD),
                        ALU.mult, ALU.add)
                last.then_inc(sem["qkv_taken"], 1)
                dve.drain()

            def rotate(s):
                x, a, b = by_tile(qk), by_tile(turned), by_tile(swapped)
                shape = [P, TILES, NQK, HD]
                dve.tensor_tensor(a, x, cos[:, :, :].unsqueeze(2).broadcast_to(shape), ALU.mult)
                half = [P, TILES, NQK, HD // 2]
                dve.tensor_tensor(b[:, :, :, 0:4], x[:, :, :, 4:8],
                                  sin[:, :, 0:4].unsqueeze(2).broadcast_to(half), ALU.mult)
                dve.tensor_tensor(b[:, :, :, 4:8], x[:, :, :, 0:4],
                                  sin[:, :, 4:8].unsqueeze(2).broadcast_to(half), ALU.mult)
                dve.drain()
                dve.tensor_tensor(turned[:, :, :], turned[:, :, :], swapped[:, :, :], ALU.add)
                dve.drain()

            def norm_heads_a(s):
                dve.tensor_tensor(swapped[:, :, :], turned[:, :, :], turned[:, :, :], ALU.mult)
                dve.drain()
                dve.tensor_reduce(sq_sum[:, :], swapped[:, :, :], AX_X, ALU.add).then_inc(sem["sq_ready"], 1)

            def norm_heads_b(s):
                dve.wait_ge(sem["head_rms_ready"], s.n + 1)
                dve.tensor_tensor(turned[:, :, :], turned[:, :, :],
                                  head_rms[:, :].unsqueeze(2).broadcast_to([P, TILES * NQK, HD]), ALU.mult)
                dve.drain()
                dve.tensor_tensor(turned[:, :, :].rearrange("p (t h) d -> p t (h d)", t=TILES),
                                  turned[:, :, :].rearrange("p (t h) d -> p t (h d)", t=TILES),
                                  w["qk_norm"][:, :].unsqueeze(1).broadcast_to([P, TILES, NQK * HD]), ALU.mult)
                dve.drain()

            def split_rows(s):
                def pieces(rows, heads, first, rest, h_slots, m_slots, l_slot):
                    r = by_tile(rows)
                    flat = rows[:, :, :]
                    x = by_tile(turned)[:, :, first:first + heads, :]
                    slot = lambda k: flat[:, :, k * HD:(k + 1) * HD]
                    tiles = lambda a: a.rearrange("p (t h) d -> p t h d", t=TILES)
                    for k in h_slots:
                        dve.tensor_copy(tiles(slot(k)), x)
                    dve.drain()
                    dve.tensor_tensor(tiles(rest[:, :, :]), x, tiles(slot(h_slots[0])), ALU.subtract)
                    dve.drain()
                    for k in m_slots:
                        dve.tensor_copy(slot(k), rest[:, :, :])
                    dve.drain()
                    return dve.tensor_tensor(slot(l_slot), rest[:, :, :], slot(m_slots[0]), ALU.subtract)

                pieces(q_rows, HEADS, 0, rest_q, (0, 1, 2), (3, 5), 4).then_inc(sem["q_rows_ready"], 1)
                pieces(k_rows, NK, HEADS, rest_k, (0, 3, 4), (1, 5), 2).then_inc(sem["k_rows_ready"], 1)

            def split_max(s):
                top = neg_top[:, :, :].rearrange("p t (j c) -> p t c j", c=2)
                m = m_rows[:, :, :].rearrange("p t (c r) -> p t c r", c=2)
                high, low = m[:, :, :, 0:HEADS // 2], m[:, :, :, HEADS // 2:HEADS]
                dve.tensor_copy(high, top)
                dve.drain()
                dve.tensor_tensor(low, top, high, ALU.subtract).then_inc(sem["m_rows_ready"], 1)

            def take_m(s):
                dve.wait_ge(sem["mt_done"], s.n + 1)
                dve.tensor_copy(m_t[s.slot][:, :], front_bf[0][:, 0:S]).then_inc(sem["mt_copied"], 1)

            def maximum(s, h):
                dve.wait_ge(sem["s_done"], s.n * HEADS + (h + 1))
                if gated:
                    dve.tensor_reduce(neg_top[:, 0, h:h + 1], ps_s[h % 2][:, 0:P], AX_X, ALU.max, negate=True)
                    last = dve.tensor_reduce(neg_top[:, 1, h:h + 1], ps_s[h % 2][:, P:3 * P], AX_X, ALU.max, negate=True)
                else:
                    last = dve.tensor_reduce(neg_top[:, :, h:h + 1],
                                             ps_s[h % 2][:, :].rearrange("p (t c) -> p t c", t=TILES),
                                             AX_X, ALU.max, negate=True)
                last.then_inc(sem["max_done"], 1)

            def normalise(s):
                dve.wait_ge(sem["ot_done"], s.n + 1)
                for t in range(TILES):
                    o = front[t][:, :].rearrange("p (h c) -> p h c", c=32)
                    dve.reciprocal(inv[:, t, :], o[:, :, HD])
                dve.drain()
                for t in range(TILES):
                    o = front[t][:, :].rearrange("p (h c) -> p h c", c=32)
                    last = dve.tensor_tensor(attn[:, t, :].rearrange("p (h d) -> p h d", d=HD), o[:, :, 0:HD],
                                             inv[:, t, :].unsqueeze(2).broadcast_to([P, HEADS, HD]), ALU.mult)
                last.then_inc(sem["attn_ready"], 1)

            def gate(s):
                dve.wait_ge(sem["z_exp_ready"], s.n + 1)
                dve.tensor_scalar(gate_t[:, :], gate_t[:, :], 1.0, None, ALU.add)
                dve.drain()
                dve.reciprocal(gate_t[:, :], gate_t[:, :])
                dve.drain()
                dve.tensor_tensor(attn_t[:, :], attn_t[:, :], gate_t[:, :], ALU.mult).then_inc(sem["gated_ready"], 1)

            def residual(s):
                dve.wait_ge(sem["y_done"], s.n + 1)
                dve.tensor_tensor(y[:, :, :], front[0][:, 0:S].rearrange("p (t d) -> p t d", t=TILES),
                                  seq(x_res, s.n), ALU.add).then_inc(sem["y_taken"], 1)
                dve.drain()
                if gated:
                    dve.tensor_tensor(seq(out_res, s.n), y[:, :, :],
                                      w["bo"][:, :].unsqueeze(1).broadcast_to([P, TILES, D]), ALU.add)
                else:
                    for t in range(TILES):
                        dve.bn_stats(stats[:, t, :], y[:, t, :])
                    dve.drain()
                    for t in range(TILES):
                        last = dve.bn_aggr(mean_var[:, t, :], stats[:, t, :])
                    last.then_inc(sem["var_ready"], 1)

            def layer_norm(s):
                dve.wait_ge(sem["rstd_ready"], s.n + 1)
                for t in range(TILES):
                    dve.tensor_scalar(tile(out_res, s.n, t), y[:, t, :], mean_var[:, t, 0:1],
                                      rstd[:, t:t + 1], ALU.subtract, ALU.mult)

            def front_a(s):
                if gated:
                    take_qkv(s)
                else:
                    dve.wait_ge(sem["qkv_taken"], s.n + 1)

            def step(s, do_scores, attend, finish, do_front):
                for h in range(HEADS):
                    if do_scores:
                        maximum(s, h)
                    if finish:
                        if h == 4:
                            normalise(s - 2)
                        if h == 6 and gated:
                            gate(s - 2)
                        if h == 8:
                            residual(s - 2)
                        if h == 10 and not gated:
                            layer_norm(s - 2)
                    if do_front:
                        if h == 8 and gated:
                            x_squares(s + 1)
                        if h == 10:
                            front_a(s + 1)
                            rotate(s + 1)
                            if gated:
                                norm_heads_a(s + 1)
                        if h == 12:
                            if gated:
                                norm_heads_b(s + 1)
                            split_rows(s + 1)
                if do_scores:
                    dve.drain()
                    split_max(s)
                    take_m(s)

            dve.memset(q_rows[:, :, :].bitcast(U32), 0)
            dve.memset(k_rows[:, :, :].bitcast(U32), 0)
            dve.memset(m_rows[:, :, :].bitcast(U32), 0)
            for r in range(3):
                dve.memset(v_ext[r][:, :, :, :], 0.0)
            dve.drain()
            for r in range(3):
                last = dve.memset(v_ext[r][:, :, :, HD:HD + 1], 1.0)
            dve.drain()
            last.then_inc(sem["zeroed"], 1)
            dve.wait_ge(sem["w_loaded"], 16 * w["count"])
            if gated:
                x_squares(Step(0, 0))
            front_a(Step(0, 0))
            rotate(Step(0, 0))
            if gated:
                norm_heads_a(Step(0, 0))
                norm_heads_b(Step(0, 0))
            split_rows(Step(0, 0))
            run_steps(dve, n_seq, step)



class Turn:

    def __init__(self, half, offset):
        self.half, self.offset = half, offset
        self.n = half * 2 + offset
        self.slot = offset % 2
        self.turn = half + offset // 2

    def __add__(self, k):
        return Turn(self.half, self.offset + k)

    def __sub__(self, k):
        return Turn(self.half, self.offset - k)


def run_turns(eng, count, step):
    step(Turn(0, 0), False, True)
    assert count % 2 == 0
    with eng.Fori(0, (count - 2) // 2) as i:
        for c in range(2):
            step(Turn(i, 1 + c), True, True)
    step(Turn(0, count - 1), True, False)


GROUP = 4
COLS = GROUP * P
EXPERTS = 8
HID = 256
CHUNKS = HID // P


def group_of(x_res, n):
    return x_res[:, bass.ds(n * COLS, COLS)].rearrange("p (t d) -> p t d", t=GROUP)


def group_tile(x_res, n, t):
    return x_res[:, bass.ds(n * COLS + t * D, D)]


def mixture_of_experts(nc, n_groups, x_res, x1_res, consts, w):
    ident, neg_half, eps_ln, eps_rms = (consts[k] for k in ("ident", "neg_half", "ln_eps", "rms_eps"))
    UNITS = EXPERTS * CHUNKS
    with ExitStack() as stack:
        room = Room(nc, stack, "moe")
        w1 = room.sb("w1", [D, EXPERTS, 2 * HID])
        w2 = room.sb("w2", [P, EXPERTS, CHUNKS, D])
        b1 = room.sb("b1", [P, EXPERTS, 2 * CHUNKS])
        b2 = room.sb("b2", [EXPERTS, D])
        wr = room.sb("wr", [D, EXPERTS])
        br = room.sb("br", [P, EXPERTS])
        ln2 = room.sb("ln2", [D, 1])
        experts = room.sb("experts", [P, EXPERTS])
        x_in = [room.sb(f"x_in{r}", [P, GROUP, D]) for r in range(2)]
        h_t = [room.sb(f"h_t{r}", [D, COLS]) for r in range(2)]
        mask = [room.sb(f"mask{r}", [P, GROUP, EXPERTS]) for r in range(2)]
        mask_t = [room.sb(f"mask_t{r}", [EXPERTS, COLS]) for r in range(2)]
        acc = [room.sb(f"acc{r}", [P, GROUP, D]) for r in range(2)]
        h = room.sb("h", [P, GROUP, D])
        sq = room.sb("sq", [P, D])
        ms = room.sb("ms", [P, GROUP])
        ms_eps = room.sb("ms_eps", [P, GROUP])
        rms = room.sb("rms", [P, GROUP])
        logits = room.sb("logits", [P, GROUP, EXPERTS])
        best = room.sb("best", [P, GROUP, 8])
        index = room.sb("index", [P, GROUP, 8], U32)
        chosen = room.sb("chosen", [P, GROUP])
        sig = [room.sb(f"sig{r}", [P, COLS]) for r in range(2)]
        hidden = [room.sb(f"hidden{r}", [P, COLS]) for r in range(2)]
        stats = room.sb("stats", [P, GROUP, 6])
        mean_var = room.sb("mean_var", [P, GROUP, 2])
        var_eps = room.sb("var_eps", [P, GROUP])
        rstd = room.sb("rstd", [P, GROUP])
        ps_value = [room.psum(f"ps_value{r}", [P, COLS]) for r in range(2)]
        ps_gate = [room.psum(f"ps_gate{r}", [P, COLS]) for r in range(2)]
        ps_y = [room.psum(f"ps_y{r}", [P, GROUP, D]) for r in range(2)]
        ps_h = room.psum("ps_h", [P, COLS])
        ps_r = room.psum("ps_r", [P, COLS])
        names = ("w_loaded ms_ready rms_ready h_ready ht_done ht_copied logits_done logits_taken mask_ready "
                 "mask_turned mask_copied acc_ready value_done gate_done sig_ready hidden_ready y_done y_taken "
                 "var_ready rstd_ready finished")
        sem = {k: room.sem(k) for k in names.split()}
        x_loaded = [room.sem(f"x_loaded{r}") for r in range(2)]
        loads = [(w1[:, :, :], w["W1"]), (w2[:, :, :, :], w["W2"]), (b1[:, :, :], w["b1"]),
                 (b2[:, :], w["b2"]), (wr[:, :], w["Wr"]), (br[:, :], w["br"]), (ln2[:, :], w["ln2"]),
                 (experts[:, :], w["experts"])]
        block = room.block()
        YS = EXPERTS + 1

        @block.sync
        def _(sp):
            def load(s):
                sp.dma_start(x_in[s.slot][:, :, :], group_of(x1_res, s.n)).then_inc(x_loaded[s.slot], 16)

            for dst, src in loads:
                sp.dma_start(dst, src).then_inc(sem["w_loaded"], 16)
            load(Turn(0, 0))
            load(Turn(0, 1))
            with sp.Fori(0, (n_groups - 2) // 2) as i:
                for c in range(2):
                    s = Turn(i, 2 + c)
                    sp.wait_ge(sem["h_ready"], (s - 1).n)
                    sp.wait_ge(sem["acc_ready"], (s - 1).n)
                    load(s)

        @block.tensor
        def _(pe):
            def turn_h(s):
                pe.wait_ge(sem["h_ready"], s.n + 1)
                for t in range(GROUP):
                    last = pe.transpose(ps_h[:, t * P:(t + 1) * P], h[:, t, :], ident[:, :])
                last.then_inc(sem["ht_done"], 1)

            def route(s):
                pe.wait_ge(sem["ht_copied"], s.n + 1)
                for t in range(GROUP):
                    last = pe.matmul(ps_r[:, t * EXPERTS:(t + 1) * EXPERTS], h_t[s.slot][:, t * P:(t + 1) * P],
                                     wr[:, :], start=True, stop=True)
                last.then_inc(sem["logits_done"], 1)

            def turn_mask(s):
                pe.wait_ge(sem["mask_ready"], s.n + 1)
                for t in range(GROUP):
                    last = pe.transpose(ps_r[0:EXPERTS, t * P:(t + 1) * P], mask[s.slot][:, t, :], ident[:, :])
                last.then_inc(sem["mask_turned"], 1)

            def biases(s):
                pe.wait_ge(sem["mask_copied"], s.n + 1)
                bank(s, 0)
                for t in range(GROUP):
                    last = pe.matmul(y_bank(s, 0)[:, t, :], mask_t[s.slot][:, t * P:(t + 1) * P], b2[:, :],
                                     start=True, stop=True)
                last.then_inc(sem["y_done"], 1)

            def y_bank(s, k):
                return ps_y[(s.slot * YS + k) % 2]

            def bank(s, k):
                if not (isinstance(s.n, int) and s.n * YS + k < 2):
                    pe.wait_ge(sem["y_taken"], s.n * YS + (k - 1))

            def up(s, k):
                e, c = k // CHUNKS, k % CHUNKS
                if not (isinstance(s.n, int) and s.n * UNITS + k < 2):
                    pe.wait_ge(sem["hidden_ready"], s.n * UNITS + (k - 1))
                pe.matmul(ps_gate[k % 2][:, :], w1[:, e, HID + c * P:HID + (c + 1) * P], h_t[s.slot][:, :],
                          start=True, stop=True).then_inc(sem["gate_done"], 1)
                pe.matmul(ps_value[k % 2][:, :], w1[:, e, c * P:(c + 1) * P], h_t[s.slot][:, :],
                          start=True, stop=True).then_inc(sem["value_done"], 1)

            def down(s, k):
                e, c = k // CHUNKS, k % CHUNKS
                pe.wait_ge(sem["hidden_ready"], s.n * UNITS + (k + 1))
                if c == 0:
                    bank(s, 1 + e)
                for t in range(GROUP):
                    last = pe.matmul(y_bank(s, 1 + e)[:, t, :], hidden[k % 2][:, t * P:(t + 1) * P],
                                     w2[:, e, c, :], start=c == 0 and t == 0, stop=c == CHUNKS - 1 and t == GROUP - 1)
                if c == CHUNKS - 1:
                    last.then_inc(sem["y_done"], 1)

            def step(s, finish, front):
                biases(s)
                for k in range(UNITS + 1):
                    if k < UNITS:
                        up(s, k)
                    if k >= 1:
                        down(s, k - 1)
                    if front:
                        if k == 5:
                            turn_h(s + 1)
                        if k == 7:
                            route(s + 1)
                        if k == 10:
                            turn_mask(s + 1)

            pe.wait_ge(sem["w_loaded"], 16 * len(loads))
            turn_h(Turn(0, 0))
            route(Turn(0, 0))
            turn_mask(Turn(0, 0))
            run_turns(pe, n_groups, step)

        @block.scalar
        def _(act):
            def take_h(s):
                act.wait_ge(sem["ht_done"], s.n + 1)
                act.activation(h_t[s.slot][:, :], ps_h[:, :], ACT.Copy, scale=ln2[:, 0:1])\
                   .then_inc(sem["ht_copied"], 1)

            def take_mask(s):
                act.wait_ge(sem["mask_turned"], s.n + 1)
                act.copy(mask_t[s.slot][:, :], ps_r[0:EXPERTS, :]).then_inc(sem["mask_copied"], 1)

            def step(s, finish, front):
                for k in range(UNITS):
                    e, c = k // CHUNKS, k % CHUNKS
                    act.wait_ge(sem["gate_done"], s.n * UNITS + (k + 1))
                    if not (isinstance(s.n, int) and s.n * UNITS + k < 2):
                        act.wait_ge(sem["hidden_ready"], s.n * UNITS + (k - 1))
                    act.activation(sig[k % 2][:, :], ps_gate[k % 2][:, :], ACT.Sigmoid,
                                   bias=b1[:, e, CHUNKS + c:CHUNKS + c + 1]).then_inc(sem["sig_ready"], 1)
                    if front:
                        if k == 6:
                            take_h(s + 1)
                        if k == 11:
                            take_mask(s + 1)

            take_h(Turn(0, 0))
            take_mask(Turn(0, 0))
            run_turns(act, n_groups, step)

        @block.gpsimd
        def _(pool):
            def x_norm(s):
                pool.wait_ge(sem["ms_ready"], s.n + 1)
                pool.tensor_tensor(ms_eps[:, :], ms[:, :], eps_rms[:, 0:GROUP], ALU.add)
                pool.drain()
                pool.tensor_tensor(rms[:, :], ms_eps[:, :], neg_half[:, 0:GROUP], ALU.pow)\
                    .then_inc(sem["rms_ready"], 1)

            def start_sum(s):
                pool.wait_ge(x_loaded[s.slot], s.turn * 16 + 16)
                if not (isinstance(s.n, int) and s.n < 2):
                    pool.wait_ge(sem["finished"], (s - 1).n)
                pool.tensor_tensor(acc[s.slot][:, :, :], x_in[s.slot][:, :, :], group_of(x_res, s.n), ALU.add)\
                    .then_inc(sem["acc_ready"], 1)

            def layer_norm(s):
                pool.wait_ge(sem["var_ready"], s.n + 1)
                pool.tensor_tensor(var_eps[:, :], mean_var[:, :, 1], eps_ln[:, 0:GROUP], ALU.add)
                pool.drain()
                pool.tensor_tensor(rstd[:, :], var_eps[:, :], neg_half[:, 0:GROUP], ALU.pow)\
                    .then_inc(sem["rstd_ready"], 1)

            def step(s, finish, front):
                if finish:
                    layer_norm(s - 1)
                if front:
                    x_norm(s + 1)
                    start_sum(s + 1)

            x_norm(Turn(0, 0))
            start_sum(Turn(0, 0))
            run_turns(pool, n_groups, step)
            layer_norm(Turn(0, n_groups - 1))

        @block.vector
        def _(dve):
            def squares(s):
                dve.wait_ge(x_loaded[s.slot], s.turn * 16 + 16)
                for t in range(GROUP):
                    x = x_in[s.slot][:, t, :]
                    last = dve.tensor_tensor_reduce(sq[:, :], x, x, 1.0 / D, 0.0, ALU.mult, ALU.add, ms[:, t:t + 1])
                    dve.drain()
                last.then_inc(sem["ms_ready"], 1)

            def scale_h(s):
                dve.wait_ge(sem["rms_ready"], s.n + 1)
                for t in range(GROUP):
                    last = dve.tensor_scalar(h[:, t, :], x_in[s.slot][:, t, :], rms[:, t:t + 1], None, ALU.mult)
                last.then_inc(sem["h_ready"], 1)

            def choose(s):
                dve.wait_ge(sem["logits_done"], s.n + 1)
                dve.tensor_tensor(logits[:, :, :], ps_r[:, 0:GROUP * EXPERTS].rearrange("p (t e) -> p t e", t=GROUP),
                                  br[:, :].unsqueeze(1).broadcast_to([P, GROUP, EXPERTS]), ALU.add)
                dve.drain()
                for t in range(GROUP):
                    dve.max(best[:, t, :], logits[:, t, :])
                dve.drain()
                for t in range(GROUP):
                    dve.max_index(index[:, t, :], best[:, t, :], logits[:, t, :])
                dve.drain()
                dve.tensor_copy(chosen[:, :], index[:, :, 0])
                dve.drain()
                for t in range(GROUP):
                    last = dve.tensor_scalar(mask[s.slot][:, t, :], experts[:, :], chosen[:, t:t + 1], None, ALU.is_equal)
                last.then_inc(sem["mask_ready"], 1)

            def take_biases(s):
                dve.wait_ge(sem["y_done"], s.n * YS + 1)
                dve.wait_ge(sem["acc_ready"], s.n + 1)
                a, y = acc[s.slot], ps_y[(s.slot * YS) % 2]
                dve.tensor_tensor(a[:, :, :], y[:, :, :], a[:, :, :], ALU.add).then_inc(sem["y_taken"], 1)

            def take(s, e):
                dve.drain()
                dve.wait_ge(sem["y_done"], s.n * YS + (e + 2))
                a, y = acc[s.slot], ps_y[(s.slot * YS + 1 + e) % 2]
                for t in range(GROUP):
                    last = dve.scalar_tensor_tensor(a[:, t, :], y[:, t, :], mask[s.slot][:, t, e:e + 1], a[:, t, :],
                                                    ALU.mult, ALU.add)
                last.then_inc(sem["y_taken"], 1)

            def statistics(s):
                dve.drain()
                for t in range(GROUP):
                    dve.bn_stats(stats[:, t, :], acc[s.slot][:, t, :])
                dve.drain()
                for t in range(GROUP):
                    last = dve.bn_aggr(mean_var[:, t, :], stats[:, t, :])
                last.then_inc(sem["var_ready"], 1)

            def normalise(s):
                dve.wait_ge(sem["rstd_ready"], s.n + 1)
                for t in range(GROUP):
                    last = dve.tensor_scalar(group_tile(x_res, s.n, t), acc[s.slot][:, t, :], mean_var[:, t, 0:1],
                                             rstd[:, t:t + 1], ALU.subtract, ALU.mult)
                last.then_inc(sem["finished"], 1)

            def step(s, finish, front):
                take_biases(s)
                for k in range(UNITS):
                    e, c = k // CHUNKS, k % CHUNKS
                    dve.wait_ge(sem["sig_ready"], s.n * UNITS + (k + 1))
                    dve.wait_ge(sem["value_done"], s.n * UNITS + (k + 1))
                    dve.scalar_tensor_tensor(hidden[k % 2][:, :], ps_value[k % 2][:, :], b1[:, e, c:c + 1],
                                             sig[k % 2][:, :], ALU.add, ALU.mult).then_inc(sem["hidden_ready"], 1)
                    if k >= 2 and k % 2 == 0:
                        take(s, k // 2 - 1)
                    if finish and k == 1:
                        normalise(s - 1)
                    if front:
                        if k == 3:
                            squares(s + 1)
                        if k == 5:
                            scale_h(s + 1)
                        if k == 9:
                            choose(s + 1)
                take(s, EXPERTS - 1)
                statistics(s)

            dve.wait_ge(sem["w_loaded"], 16 * len(loads))
            squares(Turn(0, 0))
            scale_h(Turn(0, 0))
            choose(Turn(0, 0))
            run_turns(dve, n_groups, step)
            normalise(Turn(0, n_groups - 1))


def shift_loads(eng, src, dst, n, count, done):
    half = D // 2
    v = src[:, bass.ds(n * count * D, count * D)].rearrange("p (t d) -> p t d", t=count)
    eng.dma_start(dst[:, :, 0:half], v[:, :, 0:half]).then_inc(done, 16)
    eng.dma_start(dst[1:P, :, half:D], v[0:P - 1, :, half:D]).then_inc(done, 16)
    eng.dma_start(dst[0:1, 1:count:2, half:D], v[P - 1:P, 0:count:2, half:D]).then_inc(done, 16)


FF = 341
FF_CHUNKS = [(c, min(P, FF - c)) for c in range(0, FF, P)]


def gated_feed_forward(nc, n_groups, layer, x_res, consts, w, first=None, out_dram=None):
    ident, neg_half, eps_ln = (consts[k] for k in ("ident", "neg_half", "ln_eps"))
    N = len(FF_CHUNKS)
    final = out_dram is not None
    with ExitStack() as stack:
        room = Room(nc, stack, f"ffn{layer}")
        w1 = room.sb("w1", [D, 2 * FF])
        w2 = room.sb("w2", [P, N, D])
        b1 = room.sb("b1", [P, 2 * N])
        b2 = room.sb("b2", [P, D])
        ln_g = room.sb("ln_g", [D, 1])
        ln_b = room.sb("ln_b", [D, 1])
        shifted = [room.sb(f"shifted{r}", [P, GROUP, D]) for r in range(2)]
        h_t = [room.sb(f"h_t{r}", [D, COLS]) for r in range(2)]
        h = room.sb("h", [P, GROUP, D])
        x_b = [room.sb(f"x_b{r}", [P, GROUP, D]) for r in range(2)]
        result = [room.sb(f"result{r}", [P, GROUP, D]) for r in range(2)]
        gelu = [room.sb(f"gelu{r}", [P, COLS]) for r in range(3)]
        hidden = [room.sb(f"hidden{r}", [P, COLS]) for r in range(3)]
        stats = room.sb("stats", [P, GROUP, 6])
        mean_var = room.sb("mean_var", [P, GROUP, 2])
        var_eps = room.sb("var_eps", [P, GROUP])
        rstd = room.sb("rstd", [P, GROUP])
        stats2 = room.sb("stats2", [P, GROUP, 6])
        mean_var2 = room.sb("mean_var2", [P, GROUP, 2])
        rstd2 = room.sb("rstd2", [P, GROUP])
        ps_value = [room.psum(f"ps_value{r}", [P, COLS]) for r in range(2)]
        ps_gate = [room.psum(f"ps_gate{r}", [P, COLS]) for r in range(2)]
        ps_y = [room.psum(f"ps_y{r}", [P, GROUP, D]) for r in range(2)]
        ps_h = room.psum("ps_h", [P, COLS])
        names = ("w_loaded zeroed var_ready rstd_ready h_ready ht_done ht_copied xb_ready value_done gate_done "
                 "gelu_ready hidden_ready y_done y_taken var2_ready rstd2_ready result_ready")
        sem = {k: room.sem(k) for k in names.split()}
        loaded = [room.sem(f"loaded{r}") for r in range(2)]
        stored = [room.sem(f"stored{r}") for r in range(2)]
        loads = [(w1[:, :], w["w1"]), (b2[:, :], w["b2"]),
                 (ln_g[:, :], w["ln_g"]), (ln_b[:, :], w["ln_b"])]
        for k, (c, m) in enumerate(FF_CHUNKS):
            loads += [(w2[0:m, k, :], w["w2"][c:c + m, :]), (b1[0:m, k:k + 1], w["b1"][c:c + m, :]),
                      (b1[0:m, N + k:N + k + 1], w["b1"][FF + c:FF + c + m, :])]
        block = room.block()

        @block.sync
        def _(sp):
            def load(s):
                shift_loads(sp, x_res, shifted[s.slot], s.n, GROUP, loaded[s.slot])

            def store(s):
                sp.wait_ge(sem["result_ready"], s.n + 1)
                sp.dma_start(out_dram[bass.ds(s.n * 2, 2)].rearrange("b (t p) d -> p (b t) d", p=P),
                             result[s.slot][:, :, :]).then_inc(stored[s.slot], 16)

            for dst, src in loads:
                sp.dma_start(dst, src).then_inc(sem["w_loaded"], 16)
            sp.wait_ge(sem["zeroed"], 1)
            load(Turn(0, 0))
            load(Turn(0, 1))
            with sp.Fori(0, (n_groups - 2) // 2) as i:
                for c in range(2):
                    s = Turn(i, 2 + c)
                    sp.wait_ge(sem["h_ready"], (s - 1).n)
                    load(s)
                    if final:
                        store(s - 2)
            if final:
                store(Turn(0, n_groups - 2))
                store(Turn(0, n_groups - 1))
                for r in range(2):
                    sp.wait_ge(stored[r], 16 * (n_groups // 2))

        @block.tensor
        def _(pe):
            def turn_h(s):
                pe.wait_ge(sem["h_ready"], s.n + 1)
                for t in range(GROUP):
                    last = pe.transpose(ps_h[:, t * P:(t + 1) * P], h[:, t, :], ident[:, :])
                last.then_inc(sem["ht_done"], 1)

            def up(s, k):
                c, m = FF_CHUNKS[k]
                r = (s.slot * N + k) % 2
                if k == 0:
                    pe.wait_ge(sem["ht_copied"], s.n + 1)
                if not (isinstance(s.n, int) and s.n * N + k < 2):
                    pe.wait_ge(sem["hidden_ready"], s.n * N + (k - 1))
                pe.matmul(ps_gate[r][0:m, :], w1[:, FF + c:FF + c + m], h_t[s.slot][:, :],
                          start=True, stop=True).then_inc(sem["gate_done"], 1)
                pe.matmul(ps_value[r][0:m, :], w1[:, c:c + m], h_t[s.slot][:, :],
                          start=True, stop=True).then_inc(sem["value_done"], 1)

            def down(s, k):
                c, m = FF_CHUNKS[k]
                pe.wait_ge(sem["hidden_ready"], s.n * N + (k + 1))
                if k == 0 and not (isinstance(s.n, int) and s.n < 2):
                    pe.wait_ge(sem["y_taken"], (s - 1).n)
                for t in range(GROUP):
                    last = pe.matmul(ps_y[s.slot][:, t, :], hidden[k][0:m, t * P:(t + 1) * P], w2[0:m, k, :],
                                     start=k == 0 and t == 0, stop=k == N - 1 and t == GROUP - 1)
                if k == N - 1:
                    last.then_inc(sem["y_done"], 1)

            def step(s, finish, front):
                for k in range(N):
                    up(s, k)
                    if k == 0 and finish:
                        down(s - 1, N - 1)
                    if k >= 1:
                        down(s, k - 1)
                    if front and k == 1:
                        turn_h(s + 1)

            pe.wait_ge(sem["w_loaded"], 16 * len(loads))
            turn_h(Turn(0, 0))
            run_turns(pe, n_groups, step)
            down(Turn(0, n_groups - 1), N - 1)

        @block.scalar
        def _(act):
            def take_h(s):
                act.wait_ge(sem["ht_done"], s.n + 1)
                act.activation(h_t[s.slot][:, :], ps_h[:, :], ACT.Identity, bias=ln_b[:, 0:1], scale=ln_g[:, 0:1])\
                   .then_inc(sem["ht_copied"], 1)

            def step(s, finish, front):
                for k, (c, m) in enumerate(FF_CHUNKS):
                    r = (s.slot * N + k) % 2
                    act.wait_ge(sem["gate_done"], s.n * N + (k + 1))
                    if not (isinstance(s.n, int) and s.n == 0):
                        act.wait_ge(sem["hidden_ready"], s.n * N + (k + 1 - N))
                    act.activation(gelu[k][0:m, :], ps_gate[r][0:m, :], ACT.Gelu,
                                   bias=b1[0:m, N + k:N + k + 1]).then_inc(sem["gelu_ready"], 1)
                    if front and k == 1:
                        take_h(s + 1)

            take_h(Turn(0, 0))
            run_turns(act, n_groups, step)

        @block.gpsimd
        def _(pool):
            def layer_norm(s):
                pool.wait_ge(sem["var_ready"], s.n + 1)
                pool.tensor_tensor(var_eps[:, :], mean_var[:, :, 1], eps_ln[:, 0:GROUP], ALU.add)
                pool.drain()
                pool.tensor_tensor(rstd[:, :], var_eps[:, :], neg_half[:, 0:GROUP], ALU.pow)\
                    .then_inc(sem["rstd_ready"], 1)

            def last_norm(s):
                pool.wait_ge(sem["var2_ready"], s.n + 1)
                pool.tensor_tensor(var_eps[:, :], mean_var2[:, :, 1], eps_ln[:, 0:GROUP], ALU.add)
                pool.drain()
                pool.tensor_tensor(rstd2[:, :], var_eps[:, :], neg_half[:, 0:GROUP], ALU.pow)\
                    .then_inc(sem["rstd2_ready"], 1)

            def add_bias(s):
                if not (isinstance(s.n, int) and s.n < 2):
                    pool.wait_ge(sem["y_taken"], (s - 1).n)
                pool.tensor_tensor(x_b[s.slot][:, :, :], group_of(x_res, s.n),
                                   b2[:, :].unsqueeze(1).broadcast_to([P, GROUP, D]), ALU.add)\
                    .then_inc(sem["xb_ready"], 1)
                if final:
                    pool.wait_ge(sem["xb_ready"], s.n * 2 + 1)
                    pool.tensor_tensor(x_b[s.slot][:, :, :], x_b[s.slot][:, :, :], group_of(first, s.n), ALU.add)\
                        .then_inc(sem["xb_ready"], 1)

            def step(s, finish, front):
                add_bias(s)
                if front:
                    layer_norm(s + 1)
                if finish and final:
                    last_norm(s - 1)

            pool.wait_ge(sem["w_loaded"], 16 * len(loads))
            layer_norm(Turn(0, 0))
            run_turns(pool, n_groups, step)
            if final:
                last_norm(Turn(0, n_groups - 1))

        @block.vector
        def _(dve):
            def statistics(s):
                dve.wait_ge(loaded[s.slot], s.turn * 48 + 48)
                for t in range(GROUP):
                    dve.bn_stats(stats[:, t, :], shifted[s.slot][:, t, :])
                dve.drain()
                for t in range(GROUP):
                    last = dve.bn_aggr(mean_var[:, t, :], stats[:, t, :])
                last.then_inc(sem["var_ready"], 1)

            def normalise(s):
                dve.wait_ge(sem["rstd_ready"], s.n + 1)
                if not (isinstance(s.n, int) and s.n == 0):
                    dve.wait_ge(sem["ht_done"], s.n)
                for t in range(GROUP):
                    last = dve.tensor_scalar(h[:, t, :], shifted[s.slot][:, t, :], mean_var[:, t, 0:1],
                                             rstd[:, t:t + 1], ALU.subtract, ALU.mult)
                last.then_inc(sem["h_ready"], 1)

            def take(s):
                dve.wait_ge(sem["y_done"], s.n + 1)
                dve.wait_ge(sem["xb_ready"], s.n * 2 + 2 if final else s.n + 1)
                out = x_b[s.slot][:, :, :] if final else group_of(x_res, s.n)
                ins = dve.tensor_tensor(out, ps_y[s.slot][:, :, :], x_b[s.slot][:, :, :], ALU.add)
                if not final:
                    ins.then_inc(sem["y_taken"], 1)
                    return
                dve.drain()
                for t in range(GROUP):
                    dve.bn_stats(stats2[:, t, :], x_b[s.slot][:, t, :])
                dve.drain()
                for t in range(GROUP):
                    last = dve.bn_aggr(mean_var2[:, t, :], stats2[:, t, :])
                last.then_inc(sem["var2_ready"], 1)

            def last_normalise(s):
                dve.wait_ge(sem["rstd2_ready"], s.n + 1)
                if not (isinstance(s.n, int) and s.n < 2):
                    dve.wait_ge(stored[s.slot], s.turn * 16)
                for t in range(GROUP):
                    last = dve.tensor_scalar(result[s.slot][:, t, :], x_b[s.slot][:, t, :], mean_var2[:, t, 0:1],
                                             rstd2[:, t:t + 1], ALU.subtract, ALU.mult)
                last.then_inc(sem["result_ready"], 1)
                dve.drain().then_inc(sem["y_taken"], 1)

            def step(s, finish, front):
                for k, (c, m) in enumerate(FF_CHUNKS):
                    r = (s.slot * N + k) % 2
                    dve.wait_ge(sem["gelu_ready"], s.n * N + (k + 1))
                    dve.wait_ge(sem["value_done"], s.n * N + (k + 1))
                    dve.scalar_tensor_tensor(hidden[k][0:m, :], ps_value[r][0:m, :], b1[0:m, k:k + 1],
                                             gelu[k][0:m, :], ALU.add, ALU.mult).then_inc(sem["hidden_ready"], 1)
                    if front and k == 0:
                        statistics(s + 1)
                        normalise(s + 1)
                    if finish and k == 1:
                        take(s - 1)
                    if finish and k == 2 and final:
                        last_normalise(s - 1)

            for r in range(2):
                last = dve.memset(shifted[r][0:1, :, D // 2:D], 0.0)
            dve.drain().then_inc(sem["zeroed"], 1)
            statistics(Turn(0, 0))
            normalise(Turn(0, 0))
            run_turns(dve, n_groups, step)
            take(Turn(0, n_groups - 1))
            if final:
                last_normalise(Turn(0, n_groups - 1))



LH = 8
LD = 64
WINDOW = 64
INNER = LH * LD


def windowed_attention(nc, n_seq, layer, src, dst, consts, w):
    ident, ident_bf, neg_half, band = (consts[k] for k in ("ident", "ident_bf", "neg_half", "band"))
    FIRST, SECOND = slice(0, P), slice(P + WINDOW, 3 * P)
    with ExitStack() as stack:
        room = Room(nc, stack, f"win{layer}")
        w_qkv = room.sb("w_qkv", [D, 3, INNER])
        w_out = room.sb("w_out", [P, INNER // P, D])
        scales = room.sb("scales", [P, 2, LD])
        cos = [room.sb(f"cos{c}", [P, TILES, LD]) for c in range(2)]
        sin = [room.sb(f"sin{c}", [P, TILES, LD]) for c in range(2)]
        shifted = [room.sb(f"shifted{r}", [P, TILES, D]) for r in range(2)]
        h_t = room.sb("h_t", [D, S])
        raw = [room.sb(f"raw{c}", [P, TILES * LH, LD]) for c in range(2)]
        turned = [room.sb(f"turned{c}", [P, TILES * LH, LD]) for c in range(2)]
        swapped = [room.sb(f"swapped{c}", [P, TILES * LH, LD]) for c in range(2)]
        sq_sum = room.sb("sq_sum", [P, 2, TILES * LH])
        inv_norm = room.sb("inv_norm", [P, 2, TILES * LH])
        v = [room.sb(f"v{r}", [P, TILES, INNER]) for r in range(2)]
        qk_t = [[room.sb(f"qk_t{r}{c}", [P, LH // 2, S]) for c in range(2)] for r in range(2)]
        neg_top = room.sb("neg_top", [P, 2, TILES])
        probs = [room.sb(f"probs{r}", [P, 3 * P]) for r in range(2)]
        probs_t = [room.sb(f"probs_t{r}", [P, 3 * P]) for r in range(2)]
        total = [room.sb(f"total{r}", [P, TILES, LH]) for r in range(2)]
        inv = room.sb("inv", [P, TILES, LH])
        attn = room.sb("attn", [P, TILES, INNER])
        attn_t = room.sb("attn_t", [P, INNER // P, S])
        ps_s = [room.psum(f"ps_s{r}", [P, 512]) for r in range(2)]
        ps_p = [room.psum(f"ps_p{r}", [P, 512]) for r in range(2)]
        ps_o = [room.psum(f"ps_o{r}", [P, INNER]) for r in range(2)]
        bank = [room.psum(f"bank{r}", [P, 512]) for r in range(2)]
        names = ("w_loaded zeroed ht_done ht_copied qkv_done raw_ready v_ready sq_ready sum_ready norm_ready "
                 "turned_ready rotated qk_ready qkt_done qkt_copied s_done max_ready exp_done pt_done pt_copied "
                 "o_done attn_ready at_done at_copied y_done y_taken")
        sem = {k: room.sem(k) for k in names.split()}
        loaded = [room.sem(f"loaded{r}") for r in range(2)]
        loads = [(w_qkv[:, :, :], w["qkv"]), (w_out[:, :, :], w["out"]), (scales[:, :, :], w["scales"])]
        for c in range(2):
            loads += [(cos[c][:, :, :], w["cos"][c]), (sin[c][:, :, :], w["sin"][c])]
        block = room.block()

        @block.sync
        def _(sp):
            def load(s):
                shift_loads(sp, src, shifted[s.slot], s.n, TILES, loaded[s.slot])

            for to, of in loads:
                sp.dma_start(to, of).then_inc(sem["w_loaded"], 16)
            sp.wait_ge(sem["zeroed"], 1)
            load(Turn(0, 0))
            load(Turn(0, 1))
            with sp.Fori(0, (n_seq - 2) // 2) as i:
                for c in range(2):
                    s = Turn(i, 2 + c)
                    sp.wait_ge(sem["ht_done"], (s - 1).n)
                    load(s)

        @block.tensor
        def _(pe):
            def turn_h(s):
                pe.wait_ge(loaded[s.slot], s.turn * 48 + 48)
                for t in range(TILES):
                    last = pe.transpose(bank[0][:, t * P:(t + 1) * P], shifted[s.slot][:, t, :], ident[:, :])
                last.then_inc(sem["ht_done"], 1)

            def project(s, c):
                pe.wait_ge(sem["ht_copied"], s.n + 1)
                for t in range(TILES):
                    if c >= 1:
                        pe.wait_ge(sem["raw_ready"], s.n * 4 + ((c - 1) * 2 + t + 1))
                    pe.matmul(bank[t][:, :], h_t[:, t * P:(t + 1) * P], w_qkv[:, c, :],
                              start=True, stop=True).then_inc(sem["qkv_done"], 1)

            def turn_qk(s, c):
                pe.wait_ge(sem["qk_ready"], s.n * 2 + (c + 1))
                for t in range(TILES):
                    if c == 1:
                        pe.wait_ge(sem["qkt_copied"], s.n * 4 + (t + 1))
                    for j in range(LH // 2):
                        at = t * LH + 2 * j
                        last = pe.transpose(bank[t][:, j * P:(j + 1) * P], raw[c][:, at:at + 2, :], ident[:, :])
                    last.then_inc(sem["qkt_done"], 1)

            def scores(s, h):
                half = slice(LD * (h % 2), LD * (h % 2) + LD)
                q, k = (qk_t[s.slot][c][half, h // 2, :] for c in range(2))
                if not (isinstance(s.n, int) and s.n == 0 and h < 2):
                    pe.wait_ge(sem["exp_done"], s.n * LH + (h - 1))
                out = ps_s[h % 2]
                pe.matmul(out[:, 0:P], q[:, 0:P], k[:, 0:P], start=True, stop=False)
                pe.matmul(out[:, P:5 * WINDOW], q[:, P:S], k[:, WINDOW:S], start=False, stop=False)
                pe.matmul(out[:, 0:5 * WINDOW], ident_bf[:, :], band[:, :], start=False, stop=True)\
                  .then_inc(sem["s_done"], 1)

            def turn_probs(s, h):
                pe.wait_ge(sem["exp_done"], s.n * LH + (h + 1))
                if not (isinstance(s.n, int) and s.n == 0 and h < 2):
                    pe.wait_ge(sem["pt_copied"], s.n * LH + (h - 1))
                for b in range(3):
                    last = pe.transpose(ps_p[h % 2][:, b * P:(b + 1) * P], probs[h % 2][:, b * P:(b + 1) * P],
                                        ident[:, :])
                last.then_inc(sem["pt_done"], 1)

            def weigh(s, h):
                pe.wait_ge(sem["pt_copied"], s.n * LH + (h + 1))
                if h == 0 and not (isinstance(s.n, int) and s.n == 0):
                    pe.wait_ge(sem["attn_ready"], s.n)
                cols = slice(h * LD, (h + 1) * LD)
                p = probs_t[h % 2]
                pe.matmul(ps_o[0][:, cols], p[:, 0:P], v[s.slot][:, 0, cols], start=True, stop=True)
                pe.matmul(ps_o[1][:, cols], p[:, P:2 * P], v[s.slot][:, 0, cols], start=True, stop=False)
                pe.matmul(ps_o[1][:, cols], p[:, 2 * P:3 * P], v[s.slot][:, 1, cols],
                          start=False, stop=True).then_inc(sem["o_done"], 1)

            def turn_attn(s):
                pe.wait_ge(sem["attn_ready"], s.n + 1)
                for t in range(TILES):
                    for c in range(INNER // P):
                        last = pe.transpose(bank[t][:, c * P:(c + 1) * P], attn[:, t, c * P:(c + 1) * P], ident[:, :])
                    last.then_inc(sem["at_done"], 1)

            def project_out(s):
                pe.wait_ge(sem["at_copied"], s.n * 2 + 2)
                for t in range(TILES):
                    for c in range(INNER // P):
                        last = pe.matmul(bank[0][:, t * D:(t + 1) * D], attn_t[:, c, t * P:(t + 1) * P],
                                         w_out[:, c, :], start=c == 0, stop=c == INNER // P - 1)
                last.then_inc(sem["y_done"], 1)

            def step(s, finish, front):
                pe.wait_ge(sem["qkt_copied"], s.n * 4 + 4)
                for h in range(LH):
                    scores(s, h)
                    if h == 0:
                        if front:
                            turn_h(s + 1)
                        if finish:
                            turn_probs(s - 1, LH - 1)
                            weigh(s - 1, LH - 2)
                    else:
                        turn_probs(s, h - 1)
                        if h == 1 and finish:
                            weigh(s - 1, LH - 1)
                        if h >= 2:
                            weigh(s, h - 2)
                    if front and h in (1, 2, 3):
                        project(s + 1, h - 1)
                    if h == 4 and finish:
                        if front:
                            pe.wait_ge(sem["v_ready"], (s + 1).n + 1)
                        turn_attn(s - 1)
                    if h == 5 and finish:
                        project_out(s - 1)
                    if front and h >= 6:
                        if h == 6:
                            if finish:
                                pe.wait_ge(sem["y_taken"], s.n)
                            pe.wait_ge(sem["v_ready"], (s + 1).n + 1)
                        turn_qk(s + 1, h - 6)

            def tail(s):
                turn_probs(s, LH - 1)
                weigh(s, LH - 2)
                weigh(s, LH - 1)
                turn_attn(s)
                project_out(s)

            pe.wait_ge(sem["w_loaded"], 16 * len(loads))
            pe.wait_ge(sem["zeroed"], 2)
            s0 = Turn(0, 0)
            turn_h(s0)
            for c in range(3):
                project(s0, c)
            pe.wait_ge(sem["v_ready"], 1)
            turn_qk(s0, 0)
            turn_qk(s0, 1)
            run_turns(pe, n_seq, step)
            tail(Turn(0, n_seq - 1))

        @block.scalar
        def _(act):
            def take_h(s):
                act.wait_ge(sem["ht_done"], s.n + 1)
                act.copy(h_t[:, :], bank[0][:, 0:S]).then_inc(sem["ht_copied"], 1)

            def take(s, c):
                if c < 2 and not (isinstance(s.n, int) and s.n == 0):
                    act.wait_ge(sem["qkt_done"], s.n * 4)
                for t in range(TILES):
                    act.wait_ge(sem["qkv_done"], s.n * 6 + (c * 2 + t + 1))
                    if c < 2:
                        act.copy(raw[c][:, t * LH:(t + 1) * LH, :],
                                 bank[t][:, :].rearrange("p (h d) -> p h d", d=LD)).then_inc(sem["raw_ready"], 1)
                    else:
                        last = act.copy(v[s.slot][:, t, :], bank[t][:, :])
                if c == 2:
                    last.then_inc(sem["v_ready"], 1)

            def take_qkt(s, c):
                for t in range(TILES):
                    act.wait_ge(sem["qkt_done"], s.n * 4 + (c * 2 + t + 1))
                    act.copy(qk_t[s.slot][c][:, :, t * P:(t + 1) * P],
                             bank[t][:, :].rearrange("p (j c) -> p j c", c=P)).then_inc(sem["qkt_copied"], 1)

            def take_attn(s):
                for t in range(TILES):
                    act.wait_ge(sem["at_done"], s.n * 2 + (t + 1))
                    act.copy(attn_t[:, :, t * P:(t + 1) * P],
                             bank[t][:, :].rearrange("p (c k) -> p c k", k=P)).then_inc(sem["at_copied"], 1)

            def exponentials(s, h):
                act.wait_ge(sem["max_ready"], s.n * LH + (h + 1))
                if not (isinstance(s.n, int) and s.n == 0 and h < 2):
                    act.wait_ge(sem["pt_done"], s.n * LH + (h - 1))
                out = probs[h % 2]
                act.activation(out[:, FIRST], ps_s[h % 2][:, 0:P], ACT.Exp, bias=neg_top[:, h % 2, 0:1],
                               accum_out=total[s.slot][:, 0, h:h + 1])
                act.activation(out[:, SECOND], ps_s[h % 2][:, P:5 * WINDOW], ACT.Exp, bias=neg_top[:, h % 2, 1:2],
                               accum_out=total[s.slot][:, 1, h:h + 1]).then_inc(sem["exp_done"], 1)

            def step(s, finish, front):
                for h in range(LH):
                    exponentials(s, h)
                    if front:
                        if h == 0:
                            take_h(s + 1)
                        if h in (1, 2, 3):
                            take(s + 1, h - 1)
                    if h == 4 and finish:
                        take_attn(s - 1)
                    if front and h >= 6:
                        take_qkt(s + 1, h - 6)

            s0 = Turn(0, 0)
            take_h(s0)
            for c in range(3):
                take(s0, c)
            take_qkt(s0, 0)
            take_qkt(s0, 1)
            run_turns(act, n_seq, step)
            take_attn(Turn(0, n_seq - 1))

        @block.gpsimd
        def _(pool):
            def squares(s):
                for c in range(2):
                    pool.wait_ge(sem["raw_ready"], s.n * 4 + (c * 2 + 2))
                    if not (isinstance(s.n, int) and s.n == 0):
                        pool.wait_ge(sem["turned_ready"], s.n * 2)
                        pool.wait_ge(sem["rotated"], s.n * 2)
                    pool.tensor_tensor(swapped[c][:, :, :], raw[c][:, :, :], raw[c][:, :, :], ALU.mult)\
                        .then_inc(sem["sq_ready"], 1)

            def norms(s):
                pool.wait_ge(sem["sum_ready"], s.n + 1)
                pool.tensor_tensor(inv_norm[:, :, :].rearrange("p c h -> p (c h)"),
                                   sq_sum[:, :, :].rearrange("p c h -> p (c h)"), neg_half[:, 0:2 * TILES * LH],
                                   ALU.pow).then_inc(sem["norm_ready"], 1)

            def add_turned(s):
                for c in range(2):
                    pool.wait_ge(sem["turned_ready"], s.n * 2 + (c + 1))
                    pool.tensor_tensor(turned[c][:, :, :], turned[c][:, :, :], swapped[c][:, :, :], ALU.add)\
                        .then_inc(sem["rotated"], 1)

            def step(s, finish, front):
                if front:
                    squares(s + 1)
                    norms(s + 1)
                    add_turned(s + 1)

            squares(Turn(0, 0))
            norms(Turn(0, 0))
            add_turned(Turn(0, 0))
            run_turns(pool, n_seq, step)

        @block.vector
        def _(dve):
            def by_tile(a):
                return a.rearrange("p (t h) d -> p t h d", t=TILES)

            def sums(s):
                for c in range(2):
                    dve.wait_ge(sem["sq_ready"], s.n * 2 + (c + 1))
                    last = dve.tensor_reduce(sq_sum[:, c, :], swapped[c][:, :, :], AX_X, ALU.add)
                dve.drain()
                dve.tensor_scalar(sq_sum[:, :, :], sq_sum[:, :, :], 1e-24, None, ALU.max).then_inc(sem["sum_ready"], 1)

            def turn(s, c):
                half = [P, TILES, LH, LD // 2]
                x, a, b = (by_tile(m[c][:, :, :]) for m in (raw, turned, swapped))
                dve.tensor_tensor(a, x, cos[c][:, :, :].unsqueeze(2).broadcast_to([P, TILES, LH, LD]), ALU.mult)
                dve.tensor_tensor(b[:, :, :, 0:LD // 2], x[:, :, :, LD // 2:LD],
                                  sin[c][:, :, 0:LD // 2].unsqueeze(2).broadcast_to(half), ALU.mult)
                dve.tensor_tensor(b[:, :, :, LD // 2:LD], x[:, :, :, 0:LD // 2],
                                  sin[c][:, :, LD // 2:LD].unsqueeze(2).broadcast_to(half), ALU.mult)
                dve.drain().then_inc(sem["turned_ready"], 1)

            def scale(s, c):
                dve.wait_ge(sem["norm_ready"], s.n + 1)
                dve.wait_ge(sem["rotated"], s.n * 2 + (c + 1))
                dve.tensor_tensor(raw[c][:, :, :], turned[c][:, :, :],
                                  inv_norm[:, c, :].unsqueeze(2).broadcast_to([P, TILES * LH, LD]), ALU.mult)\
                   .then_inc(sem["qk_ready"], 1)

            def maximum(s, h):
                dve.wait_ge(sem["s_done"], s.n * LH + (h + 1))
                dve.tensor_reduce(neg_top[:, h % 2, 0:1], ps_s[h % 2][:, 0:P], AX_X, ALU.max, negate=True)
                dve.tensor_reduce(neg_top[:, h % 2, 1:2], ps_s[h % 2][:, P:5 * WINDOW], AX_X, ALU.max, negate=True)\
                   .then_inc(sem["max_ready"], 1)

            def take_probs(s, h):
                dve.wait_ge(sem["pt_done"], s.n * LH + (h + 1))
                dve.tensor_copy(probs_t[h % 2][:, :], ps_p[h % 2][:, 0:3 * P]).then_inc(sem["pt_copied"], 1)

            def normalise(s):
                dve.reciprocal(inv[:, :, :], total[s.slot][:, :, :])
                dve.drain()
                dve.wait_ge(sem["o_done"], s.n * LH + LH)
                for t in range(TILES):
                    last = dve.tensor_tensor(attn[:, t, :].rearrange("p (h d) -> p h d", d=LD),
                                             ps_o[t][:, :].rearrange("p (h d) -> p h d", d=LD),
                                             inv[:, t, :].unsqueeze(2).broadcast_to([P, LH, LD]), ALU.mult)
                last.then_inc(sem["attn_ready"], 1)

            def residual(s):
                dve.wait_ge(sem["y_done"], s.n + 1)
                dve.tensor_tensor(seq(dst, s.n), bank[0][:, 0:S].rearrange("p (t d) -> p t d", t=TILES),
                                  seq(src, s.n), ALU.add).then_inc(sem["y_taken"], 1)

            def step(s, finish, front):
                for h in range(LH):
                    maximum(s, h)
                    if h == 0:
                        if finish:
                            take_probs(s - 1, LH - 1)
                    else:
                        take_probs(s, h - 1)
                    if h == 1 and finish:
                        normalise(s - 1)
                    if front and h == 3:
                        sums(s + 1)
                        turn(s + 1, 0)
                    if front and h == 4:
                        turn(s + 1, 1)
                    if front and h == 5:
                        scale(s + 1, 0)
                        scale(s + 1, 1)
                    if finish and h == 5:
                        residual(s - 1)

            for r in range(2):
                dve.memset(shifted[r][0:1, :, D // 2:D], 0.0)
                dve.memset(probs[r][:, :], 0.0)
            dve.drain().then_inc(sem["zeroed"], 1)
            dve.wait_ge(sem["w_loaded"], 16 * len(loads))
            for c in range(2):
                q = scales[:, c, :].unsqueeze(1)
                dve.tensor_tensor(cos[c][:, :, :], cos[c][:, :, :], q.broadcast_to([P, TILES, LD]), ALU.mult)
                for a, b in ((0, LD // 2), (LD // 2, 0)):
                    dve.tensor_tensor(sin[c][:, :, a:a + LD // 2], sin[c][:, :, a:a + LD // 2],
                                      q[:, :, b:b + LD // 2].broadcast_to([P, TILES, LD // 2]), ALU.mult)
            dve.drain().then_inc(sem["zeroed"], 1)
            s0 = Turn(0, 0)
            sums(s0)
            turn(s0, 0)
            turn(s0, 1)
            scale(s0, 0)
            scale(s0, 1)
            run_turns(dve, n_seq, step)
            take_probs(Turn(0, n_seq - 1), LH - 1)
            normalise(Turn(0, n_seq - 1))
            residual(Turn(0, n_seq - 1))



def post_ln_network(nc, x, consts, w, out):
    n_seq = x.shape[0]
    n_groups = n_seq * TILES // GROUP
    every = [P, P]
    with ExitStack() as stack:
        room = Room(nc, stack, "net")
        x_res = room.sb("x_res", [P, n_seq * TILES * D])
        x1_res = room.sb("x1_res", [P, n_seq * TILES * D])
        c = {k: room.sb(k, every) for k in ("ident", "neg_half", "ln_eps", "rms_eps", "eighth")}
        c["ident_bf"] = room.sb("ident_bf", every, BF16)
        c["mask_qk"] = room.sb("mask_qk", [P, TILES, P], BF16)
        c["mask_kq"] = room.sb("mask_kq", [P, TILES, P], BF16)
        c["pick"] = room.sb("pick", [P, HEADS // 2, P], BF16)
        c["band"] = room.sb("band", [P, 5 * WINDOW], BF16)
        c["cos"] = room.sb("cos", [P, TILES, HD])
        c["sin"] = room.sb("sin", [P, TILES, HD])
        c["tril"] = room.sb("tril", [P, 3 * P])
        gqa = {"eighth": c["eighth"]}
        mha = {}
        for k, width in (("qkv", 224), ("out", D), ("gate", D), ("ln1", 1), ("neg_bg", 1)):
            gqa[k] = room.sb(f"gqa_{k}", [D, width])
        for k, width in (("b_qkv", 224), ("bo", D), ("qk_norm", 24 * HD)):
            gqa[k] = room.sb(f"gqa_{k}", [P, width])
        for k, width in (("qkv", 384), ("out", D)):
            mha[k] = room.sb(f"mha_{k}", [D, width])
        g = w["gqa"]
        gqa["loads"] = [(gqa[k][:, :], g[k]) for k in ("qkv", "out", "ln1")]
        gqa["loads"] += [(gqa[k][:, :], g[k].broadcast_to([P, g[k].shape[1]])) for k in ("b_qkv", "bo", "qk_norm")]
        mha["loads"] = [(mha[k][:, :], w["mha"][k]) for k in ("qkv", "out")]
        for each in (gqa, mha):
            each["count"] = len(each["loads"])

        with ExitStack() as first:
            early = Room(nc, first, "setup")
            wide = {k: early.sb(k, [P, consts[k].shape[1]]) for k in ("mask_qk", "mask_kq", "pick", "band")}
            loaded, zeroed, filled = (early.sem(k) for k in ("loaded", "zeroed", "filled"))
            block = early.block()

            @block.sync
            def _(sp):
                loads = [(wide[k][:, :], consts[k]) for k in wide]
                loads += [(c["ident"][:, :], consts["ident"]), (c["tril"][:, :], consts["tril"]),
                          (c["cos"][:, :, :], consts["cos"]), (c["sin"][:, :, :], consts["sin"]),
                          (gqa["neg_bg"][:, :], g["bg"])]
                for dst, src in loads:
                    sp.dma_start(dst, src).then_inc(loaded, 16)
                sp.wait_ge(zeroed, 1)
                for h in range(HEADS):
                    at = slice(h * HD, (h + 1) * HD)
                    sp.dma_start(gqa["gate"][at, at], g["gate"]).then_inc(filled, 16)
                sp.wait_ge(filled, 16 * HEADS)

            @block.vector
            def _(dve):
                dve.memset(gqa["gate"][:, :], 0.0)
                dve.drain().then_inc(zeroed, 1)
                for k, value in (("neg_half", -0.5), ("ln_eps", LN_EPS), ("rms_eps", RMS_EPS), ("eighth", 1.0 / HD)):
                    dve.memset(c[k][:, :], value)
                dve.wait_ge(loaded, 16 * (len(wide) + 5))
                dve.tensor_copy(c["ident_bf"][:, :], c["ident"][:, :])
                for t in range(TILES):
                    dve.tensor_copy(c["mask_qk"][:, t, :], wide["mask_qk"][:, :])
                    dve.tensor_copy(c["mask_kq"][:, t, :], wide["mask_kq"][:, :])
                dve.tensor_copy(c["pick"][:, :, :], wide["pick"][:, :].rearrange("p (j k) -> p j k", k=P))
                dve.tensor_copy(c["band"][:, :], wide["band"][:, :])
                dve.tensor_scalar(gqa["neg_bg"][:, :], gqa["neg_bg"][:, :], -1.0, None, ALU.mult)

        single_head_attention(nc, x_res, x, w["sha"][0], w["sha"][1], w["sha"][2],
                              c["ident"], c["neg_half"], c["ln_eps"], c["tril"])
        many_head_attention(nc, n_seq, x_res, x1_res, c, gqa, True)
        mixture_of_experts(nc, n_groups, x_res, x1_res, c, w["moe"])
        many_head_attention(nc, n_seq, x_res, x_res, c, mha, False)
        for layer in range(2):
            windowed_attention(nc, n_seq, layer, x_res if layer == 0 else x1_res, x1_res, c, w["win"][layer])
            gated_feed_forward(nc, n_groups, layer, x1_res, c, w["ffn"][layer], first=x_res,
                               out_dram=out if layer == 1 else None)


def by_token_tile(table):
    n = table.shape[1]
    return np.ascontiguousarray(table.reshape(TILES, P, n).transpose(1, 0, 2)).astype(np.float32)


def rotation(width):
    f4 = np.float32
    inv = f4(1) / f4(10000.0) ** (np.arange(0, width, 2, dtype=f4) / f4(width))
    angle = np.arange(S, dtype=f4)[:, None] * inv[None, :]
    cos, sin = np.cos(angle), np.sin(angle)
    return np.concatenate([cos, cos], 1), np.concatenate([-sin, sin], 1)


def shape_constants():
    f4 = np.float32
    one = np.tril(np.ones((P, P), f4))
    late = np.where(one > 0, f4(0), f4(MASKED))
    pick = np.zeros((P, HEADS // 2, P), f4)
    for j in range(HEADS // 2):
        for half in (0, ROWS):
            pick[half + j, j, :] = 1
            pick[half + HEADS // 2 + j, j, :] = 1
    q = np.arange(P)[:, None]
    k0, k1 = np.arange(P)[None, :], np.arange(WINDOW, S)[None, :]
    near0 = (k0 <= q) & (k0 >= q - WINDOW)
    near1 = (k1 <= q + P) & (k1 >= q + P - WINDOW)
    cos, sin = rotation(HD)
    made = {
        "ident": np.eye(P, dtype=f4), "tril": np.concatenate([one, np.ones((P, P), f4), one], 1),
        "mask_qk": late, "mask_kq": late.T, "pick": pick.reshape(P, -1),
        "band": np.where(np.concatenate([near0, near1], 1), f4(0), f4(MASKED)),
        "cos": by_token_tile(cos), "sin": by_token_tile(sin),
        "experts": np.arange(EXPERTS, dtype=f4)[None, :],
    }
    cos, sin = rotation(LD)
    half = np.arange(0, LD, 2, dtype=f4)
    base = (half + f4(0.4 * LD)) / f4(1.4 * LD)
    power = (np.arange(S, dtype=f4) - S // 2) / f4(WINDOW // 2)
    grow = base[None, :] ** power[:, None]
    grow = np.concatenate([grow, grow], 1)
    for name, table in (("cos", cos), ("sin", sin)):
        made[f"{name}_q"] = by_token_tile(table * grow * f4(8))
        made[f"{name}_k"] = by_token_tile(table / grow)
    return made


def kernel(**inputs):
    import concourse.bacc as bacc
    from concourse.bass_utils import run_bass_kernel_spmd

    a = {k: np.asarray(v) for k, v in inputs.items()}

    def rope_halves(weights):
        return weights.reshape(HEADS, HD // 2, 2, D).transpose(0, 2, 1, 3).reshape(D, D).T

    def keys_twice(weights):
        return np.repeat(weights.reshape(-1, 4, 1, HD), 2, axis=2).reshape(weights.shape[0], -1)

    row = lambda k: a[k].reshape(1, -1)
    column = lambda k: a[k].reshape(-1, 1)
    arrays = {
        "x": a["L0_attn_x"],
        "sha_q": a["L0_attn_WQ"].T, "sha_k": a["L0_attn_WK"].T, "sha_v": a["L0_attn_WV"].T,
        "gqa_qkv": np.concatenate([a["L0_ffn_Wq"], keys_twice(a["L0_ffn_Wk"]), a["L0_ffn_Wv"]], 1),
        "gqa_b_qkv": np.concatenate([row("L0_ffn_bq"), keys_twice(row("L0_ffn_bk")), row("L0_ffn_bv")], 1),
        "gqa_qk_norm": np.concatenate([np.tile(row("L0_ffn_qn_w"), (1, HEADS)), np.tile(row("L0_ffn_kn_w"), (1, 8))], 1),
        "gqa_out": a["L0_ffn_Wo"], "gqa_bo": row("L0_ffn_bo"), "gqa_ln1": column("L0_ffn_ln1_w"),
        "gqa_gate": a["L0_ffn_Wg"], "gqa_bg": np.tile(a["L0_ffn_bg"], HEADS).reshape(-1, 1),
        "moe_W1": a["L0_ffn_W1"], "moe_W2": a["L0_ffn_W2"],
        "moe_b1": a["L0_ffn_b1"].reshape(EXPERTS, 2 * CHUNKS, P).transpose(2, 0, 1),
        "moe_b2": a["L0_ffn_b2"], "moe_Wr": a["L0_ffn_Wr"], "moe_br": row("L0_ffn_br"),
        "moe_ln2": column("L0_ffn_ln2_w"),
        "mha_qkv": np.concatenate([rope_halves(a["L1_attn_Wq"]), rope_halves(a["L1_attn_Wk"]), a["L1_attn_Wv"].T], 1),
        "mha_out": a["L1_attn_Wo"].T,
    }
    for n in range(2):
        arrays.update({
            f"win{n}_qkv": a["L1_ffn_wqkv"][n].reshape(D, 3, INNER), f"win{n}_out": a["L1_ffn_wo"][n],
            f"win{n}_scales": np.stack([a["L1_ffn_q_scale"][n], a["L1_ffn_k_scale"][n]])[None],
            f"ffn{n}_w1": a["L1_ffn_w1"][n], f"ffn{n}_w2": a["L1_ffn_w2"][n],
            f"ffn{n}_b1": a["L1_ffn_b1"][n].reshape(-1, 1), f"ffn{n}_b2": a["L1_ffn_b2"][n].reshape(1, -1),
            f"ffn{n}_ln_g": a["L1_ffn_ln_g"][n].reshape(-1, 1), f"ffn{n}_ln_b": a["L1_ffn_ln_b"][n].reshape(-1, 1),
        })
    arrays.update({f"const_{k}": v for k, v in shape_constants().items()})
    arrays = {f"in_{k}": np.ascontiguousarray(v) for k, v in arrays.items()}

    nc = bacc.Bacc("TRN2", target_bir_lowering=False, num_devices=1)
    t = {k[3:]: nc.dram_tensor(k, v.shape, mybir.dt.from_np(v.dtype), kind="ExternalInput").ap()
         for k, v in arrays.items()}
    out = nc.dram_tensor("out_0", a["L0_attn_x"].shape, F32, kind="ExternalOutput").ap()
    consts = {k[6:]: v for k, v in t.items() if k.startswith("const_")}
    weights = {
        "sha": [t["sha_q"], t["sha_k"], t["sha_v"]],
        "gqa": {k[4:]: v for k, v in t.items() if k.startswith("gqa_")},
        "mha": {k[4:]: v for k, v in t.items() if k.startswith("mha_")},
        "moe": {
            "W1": t["moe_W1"].rearrange("e d f -> d e f"), "b1": t["moe_b1"], "b2": t["moe_b2"],
            "W2": t["moe_W2"].rearrange("e (c p) d -> p e c d", p=P), "Wr": t["moe_Wr"],
            "br": t["moe_br"].broadcast_to([P, EXPERTS]), "ln2": t["moe_ln2"],
            "experts": consts["experts"].broadcast_to([P, EXPERTS]),
        },
        "win": [{
            "qkv": t[f"win{n}_qkv"], "out": t[f"win{n}_out"].rearrange("(c p) d -> p c d", p=P),
            "scales": t[f"win{n}_scales"].broadcast_to([P, 2, LD]),
            "cos": [consts["cos_q"], consts["cos_k"]], "sin": [consts["sin_q"], consts["sin_k"]],
        } for n in range(2)],
        "ffn": [{
            "w1": t[f"ffn{n}_w1"], "w2": t[f"ffn{n}_w2"], "b1": t[f"ffn{n}_b1"],
            "b2": t[f"ffn{n}_b2"].broadcast_to([P, D]), "ln_g": t[f"ffn{n}_ln_g"], "ln_b": t[f"ffn{n}_ln_b"],
        } for n in range(2)],
    }
    post_ln_network(nc, t["x"], consts, weights, out)
    result = run_bass_kernel_spmd(nc, [arrays], core_ids=[0])
    return result.results[0]["out_0"]
```

```python
from contextlib import ExitStack

import numpy as np
import concourse.bass as bass
from concourse import mybir

F32 = mybir.dt.float32
BF16 = mybir.dt.bfloat16
U32 = mybir.dt.uint32
I32 = mybir.dt.int32
ALU = mybir.AluOpType
ACT = mybir.ActivationFunctionType
AX_X = mybir.AxisListType.X

P = 128
D = 128
S = 256
TILES = S // P
LN_EPS = 1e-5
RMS_EPS = 1e-6
MASKED = -1e30


class Room:

    def __init__(self, nc, stack, stage):
        self.nc, self.stack, self.stage, self.sems = nc, stack, stage, []

    def sb(self, name, shape, dt=F32):
        return self.stack.enter_context(self.nc.sbuf_tensor(f"{self.stage}_{name}", shape, dt))

    def psum(self, name, shape, dt=F32):
        return self.stack.enter_context(self.nc.psum_tensor(f"{self.stage}_{name}", shape, dt))

    def sem(self, name):
        made = self.stack.enter_context(self.nc.semaphore(f"{self.stage}_{name}"))
        self.sems.append(made)
        return made

    def block(self):
        self.stack.callback(self.clear)
        return self.stack.enter_context(self.nc.Block())

    def clear(self):
        numbers = sorted(s.num for s in self.sems)
        starts = [a for a in numbers if a - 1 not in numbers]
        ends = [a + 1 for a in numbers if a + 1 not in numbers]
        with self.nc.Block() as block:
            @block.gpsimd
            def _(pool):
                for start, end in zip(starts, ends):
                    pool.sem_clear(range(start, end))


def inverse_root(dve, part, x, minus_half_x, guess, out):
    dve.drain()
    if part == 0:
        return dve.tensor_scalar(guess.bitcast(I32), x.bitcast(I32), -0.5, float(0x5F3759DF), ALU.mult, ALU.add)
    dve.tensor_tensor(x, guess, guess, ALU.mult)
    dve.drain()
    dve.tensor_tensor(x, x, minus_half_x, ALU.mult)
    dve.drain()
    return dve.scalar_tensor_tensor(out if part == 3 else guess, x, 1.5, guess, ALU.add, ALU.mult)


def seq(x_res, n):
    return x_res[:, bass.ds(n * (TILES * D), TILES * D)].rearrange("p (t d) -> p t d", t=TILES)


def tile(x_res, n, t):
    return x_res[:, bass.ds(n * (TILES * D) + t * D, D)]


def single_head_attention(nc, x_res, x_dram, wq_t, wk_t, wv_t, ident, neg_half, ln_eps, tril):
    n_seq = x_dram.shape[0]
    x_tiles = x_dram.rearrange("b (t p) d -> b p t d", p=P)
    scale = float(D) ** -0.5
    with ExitStack() as stack:
        room = Room(nc, stack, "sha")
        w = room.sb("w", [D, 3, D])
        x_in = [room.sb(f"x_in{s}", [P, TILES, D]) for s in range(2)]
        x_t = [room.sb(f"x_t{s}", [D, S]) for s in range(2)]
        qk_t = [room.sb(f"qk_t{s}", [D, 2, S]) for s in range(2)]
        v = [room.sb(f"v{s}", [P, TILES, D]) for s in range(2)]
        scores = [room.sb(f"scores{s}", [P, 3 * P]) for s in range(2)]
        dead = [room.sb(f"dead{s}", [P, 3 * P]) for s in range(2)]
        probs = [room.sb(f"probs{s}", [P, 3 * P]) for s in range(2)]
        probs_t = [room.sb(f"probs_t{s}", [P, 3 * P]) for s in range(2)]
        top = [room.sb(f"top{s}", [P, TILES]) for s in range(2)]
        bias = [room.sb(f"bias{s}", [P, TILES]) for s in range(2)]
        total = [room.sb(f"total{s}", [P, TILES]) for s in range(2)]
        inv = [room.sb(f"inv{s}", [P, TILES]) for s in range(2)]
        y = [room.sb(f"y{s}", [P, TILES, D]) for s in range(2)]
        stats = [room.sb(f"stats{s}", [P, TILES, 6]) for s in range(2)]
        mean_var = [room.sb(f"mean_var{s}", [P, TILES, 2]) for s in range(2)]
        veps = [room.sb(f"veps{s}", [P, TILES]) for s in range(2)]
        rstd = [room.sb(f"rstd{s}", [P, TILES]) for s in range(2)]
        ps_a = [room.psum(f"ps_a{s}", [P, 512]) for s in range(2)]
        ps_qk = [room.psum(f"ps_qk{s}", [P, 2, S]) for s in range(2)]
        ps_v = [room.psum(f"ps_v{s}", [P, TILES, D]) for s in range(2)]
        ps_p = [room.psum(f"ps_p{s}", [P, 512]) for s in range(2)]
        w_loaded = room.sem("w_loaded")
        x_loaded = [room.sem(f"x_loaded{s}") for s in range(2)]
        xt_done = room.sem("xt_done")
        xt_copied = room.sem("xt_copied")
        qk_done = room.sem("qk_done")
        qk_copied = room.sem("qk_copied")
        v_done = room.sem("v_done")
        v_copied = room.sem("v_copied")
        scores_done = room.sem("scores_done")
        bias_ready = room.sem("bias_ready")
        probs_ready = room.sem("probs_ready")
        pt_done = room.sem("pt_done")
        pt_copied = room.sem("pt_copied")
        out_done = room.sem("out_done")
        var_ready = room.sem("var_ready")
        rstd_ready = room.sem("rstd_ready")
        x_free = room.sem("x_free")
        row = [slice(0, P), slice(P, 3 * P)]
        block = room.block()

        @block.sync
        def _(sp):
            for c, src in enumerate((wq_t, wk_t, wv_t)):
                sp.dma_start(w[:, c, :], src).then_inc(w_loaded, 16)
            with sp.Fori(0, n_seq // 2) as i:
                for s in range(2):
                    n = i * 2 + s
                    sp.wait_ge(x_free, n + 1)
                    src = x_tiles[bass.ds(n, 1)].rearrange("b p t d -> (b p) t d")
                    sp.dma_start(x_in[s][:, :, :], src).then_inc(x_loaded[s], 16)

        @block.tensor
        def _(pe):
            pe.wait_ge(w_loaded, 48)
            with pe.Fori(0, n_seq // 2) as i:
                for s in range(2):
                    n = i * 2 + s
                    pe.wait_ge(x_loaded[s], i * 16 + 16)
                    for t in range(TILES):
                        last = pe.transpose(ps_a[s][:, t * P:(t + 1) * P], x_in[s][:, t, :], ident[:, :])
                    last.then_inc(xt_done, 1)
                for s in range(2):
                    n = i * 2 + s
                    pe.wait_ge(xt_copied, n + 1)
                    for c in range(2):
                        last = pe.matmul(ps_qk[s][:, c, :], w[:, c, :], x_t[s][:, :], start=True, stop=True)
                    last.then_inc(qk_done, 1)
                    for t in range(TILES):
                        last = pe.matmul(ps_v[s][:, t, :], x_t[s][:, t * P:(t + 1) * P], w[:, 2, :],
                                         start=True, stop=True)
                    last.then_inc(v_done, 1)
                for s in range(2):
                    n = i * 2 + s
                    pe.wait_ge(qk_copied, n + 1)
                    pe.matmul(ps_a[s][:, row[0]], qk_t[s][:, 0, 0:P], qk_t[s][:, 1, 0:P], start=True, stop=True)
                    pe.matmul(ps_a[s][:, row[1]], qk_t[s][:, 0, P:S], qk_t[s][:, 1, :],
                              start=True, stop=True).then_inc(scores_done, 1)
                for s in range(2):
                    n = i * 2 + s
                    pe.wait_ge(probs_ready, n + 1)
                    for b in range(3):
                        last = pe.transpose(ps_p[s][:, b * P:(b + 1) * P], probs[s][:, b * P:(b + 1) * P],
                                            ident[:, :])
                    last.then_inc(pt_done, 1)
                for s in range(2):
                    n = i * 2 + s
                    pe.wait_ge(pt_copied, n + 1)
                    pe.wait_ge(v_copied, n + 1)
                    pe.matmul(ps_p[s][:, 0:D], probs_t[s][:, 0:P], v[s][:, 0, :], start=True, stop=True)
                    for t in range(TILES):
                        last = pe.matmul(ps_p[s][:, D:2 * D], probs_t[s][:, (1 + t) * P:(2 + t) * P],
                                         v[s][:, t, :], start=t == 0, stop=t == 1)
                    last.then_inc(out_done, 1)

        @block.scalar
        def _(act):
            with act.Fori(0, n_seq // 2) as i:
                for s in range(2):
                    n = i * 2 + s
                    act.wait_ge(xt_done, n + 1)
                    act.copy(x_t[s][:, :], ps_a[s][:, 0:S]).then_inc(xt_copied, 1)
                for s in range(2):
                    n = i * 2 + s
                    act.wait_ge(v_done, n + 1)
                    act.copy(v[s][:, :, :], ps_v[s][:, :, :]).then_inc(v_copied, 1)
                for s in range(2):
                    n = i * 2 + s
                    act.wait_ge(bias_ready, n + 1)
                    for t in range(TILES):
                        last = act.activation(probs[s][:, row[t]], scores[s][:, row[t]], ACT.Exp,
                                              bias=bias[s][:, t:t + 1], scale=scale,
                                              accum_out=total[s][:, t:t + 1])
                    last.then_inc(probs_ready, 1)

        @block.gpsimd
        def _(pool):
            with pool.Fori(0, n_seq // 2) as i:
                for s in range(2):
                    pool.wait_ge(var_ready, i * 2 + (s + 1))
                    pool.tensor_tensor(veps[s][:, :], mean_var[s][:, :, 1], ln_eps[:, 0:TILES], ALU.add)
                    pool.drain()
                    pool.tensor_tensor(rstd[s][:, :], veps[s][:, :], neg_half[:, 0:TILES],
                                       ALU.pow).then_inc(rstd_ready, 1)

        @block.vector
        def _(dve):
            dve.sem_inc(x_free, 2)
            with dve.Fori(0, n_seq // 2) as i:
                for s in range(2):
                    n = i * 2 + s
                    dve.wait_ge(qk_done, n + 1)
                    dve.tensor_copy(qk_t[s][:, :, :], ps_qk[s][:, :, :]).then_inc(qk_copied, 1)
                for s in range(2):
                    n = i * 2 + s
                    dve.wait_ge(scores_done, n + 1)
                    dve.tensor_tensor(scores[s][:, :], ps_a[s][:, 0:3 * P], tril[:, :], ALU.mult)
                    dve.drain()
                    dve.tensor_scalar(dead[s][:, :], scores[s][:, :], 0.0, MASKED, ALU.is_equal, ALU.mult)
                    dve.drain()
                    for t in range(TILES):
                        dve.tensor_tensor_reduce(scores[s][:, row[t]], scores[s][:, row[t]], dead[s][:, row[t]],
                                                 1.0, -3e38, ALU.add, ALU.max, top[s][:, t:t + 1])
                    dve.drain()
                    dve.tensor_scalar(bias[s][:, :], top[s][:, :], -scale, None, ALU.mult).then_inc(bias_ready, 1)
                for s in range(2):
                    n = i * 2 + s
                    dve.wait_ge(pt_done, n + 1)
                    dve.tensor_copy(probs_t[s][:, :], ps_p[s][:, 0:3 * P]).then_inc(pt_copied, 1)
                    dve.reciprocal(inv[s][:, :], total[s][:, :])
                for s in range(2):
                    n = i * 2 + s
                    dve.drain()
                    dve.wait_ge(out_done, n + 1)
                    for t in range(TILES):
                        last = dve.scalar_tensor_tensor(y[s][:, t, :], ps_p[s][:, t * D:(t + 1) * D],
                                                        inv[s][:, t:t + 1], x_in[s][:, t, :], ALU.mult, ALU.add)
                    last.then_inc(x_free, 1)
                    dve.drain()
                    for t in range(TILES):
                        dve.bn_stats(stats[s][:, t, :], y[s][:, t, :])
                    dve.drain()
                    for t in range(TILES):
                        last = dve.bn_aggr(mean_var[s][:, t, :], stats[s][:, t, :])
                    last.then_inc(var_ready, 1)
                for s in range(2):
                    n = i * 2 + s
                    dve.drain()
                    dve.wait_ge(rstd_ready, n + 1)
                    for t in range(TILES):
                        dve.tensor_scalar(tile(x_res, n, t), y[s][:, t, :], mean_var[s][:, t, 0:1],
                                          rstd[s][:, t:t + 1], ALU.subtract, ALU.mult)


HEADS = 16
HD = 8
ROWS = 64
QUADS = HEADS // 4


class Step:

    def __init__(self, third, offset):
        self.third, self.offset = third, offset
        self.n = third * 3 + offset
        self.slot = offset % 3
        self.turn = third + offset // 3

    def __add__(self, k):
        return Step(self.third, self.offset + k)

    def __sub__(self, k):
        return Step(self.third, self.offset - k)


def run_steps(eng, n_seq, step):
    step(Step(0, 0), True, False, False, True)
    step(Step(0, 1), True, True, False, True)
    assert (n_seq - 5) % 3 == 0
    with eng.Fori(0, (n_seq - 5) // 3) as i:
        for c in range(3):
            step(Step(i, 2 + c), True, True, True, True)
    step(Step(0, n_seq - 3), True, True, True, True)
    step(Step(0, n_seq - 2), True, True, True, True)
    step(Step(0, n_seq - 1), True, True, True, False)
    step(Step(0, n_seq), False, True, True, False)
    step(Step(0, n_seq + 1), False, False, True, False)


def many_head_attention(nc, n_seq, x_res, out_res, consts, w, gated):
    ident, ident_bf, neg_half, eps_ln, eps_rms = (consts[k] for k in ("ident", "ident_bf", "neg_half", "ln_eps", "rms_eps"))
    NK = 8 if gated else 16
    NV = 4 if gated else 16
    NQK = HEADS + NK
    W = NQK * HD + NV * HD
    scale = float(HD) ** -0.5
    with ExitStack() as stack:
        room = Room(nc, stack, "gqa" if gated else "mha")
        x_in = [room.sb(f"x_in{r}", [P, TILES, D]) for r in range(3)]
        x_t = [room.sb(f"x_t{r}", [D, S]) for r in range(3)]
        qk = room.sb("qk", [P, TILES * NQK, HD])
        turned = room.sb("turned", [P, TILES * NQK, HD])
        swapped = room.sb("swapped", [P, TILES * NQK, HD])
        squares = room.sb("squares", [P, TILES * NQK, HD])
        rope_cos = room.sb("rope_cos", [P, TILES * NQK, HD])
        rope_sin = room.sb("rope_sin", [P, TILES * NQK, HD])
        sq_sum = room.sb("sq_sum", [P, TILES * NQK])
        mean_eps = room.sb("mean_eps", [P, TILES * NQK])
        minus_half = room.sb("minus_half", [P, TILES * NQK])
        guess = room.sb("guess", [P, TILES * NQK])
        head_rms = room.sb("head_rms", [P, TILES * NQK])
        rest_q = room.sb("rest_q", [P, TILES * HEADS, HD])
        rest_k = room.sb("rest_k", [P, TILES * NK, HD])
        q_rows = room.sb("q_rows", [P, TILES * HEADS, ROWS], BF16)
        k_rows = room.sb("k_rows", [P, TILES * NK, ROWS], BF16)
        q_t = [room.sb(f"q_t{r}", [P, HEADS // 2, S], BF16) for r in range(3)]
        k_t = [room.sb(f"k_t{r}", [P, NK // 2, S], BF16) for r in range(3)]
        v_ext = [room.sb(f"v_ext{r}", [P, TILES, NV, 32]) for r in range(3)]
        neg_top = room.sb("neg_top", [P, TILES, HEADS])
        m_rows = room.sb("m_rows", [P, TILES, P], BF16)
        m_t = [room.sb(f"m_t{r}", [P, S], BF16) for r in range(3)]
        probs = room.sb("probs", [P, 8, 2 * S])
        o_t = room.sb("o_t", [P, QUADS, S])
        inv = room.sb("inv", [P, TILES, HEADS])
        attn = room.sb("attn", [P, TILES, D])
        attn_t = room.sb("attn_t", [D, S])
        gate_t = room.sb("gate_t", [D, S])
        x_ms = room.sb("x_ms", [P, TILES])
        x_ms_eps = room.sb("x_ms_eps", [P, TILES])
        x_rms = room.sb("x_rms", [P, TILES])
        sq = room.sb("sq", [P, D])
        y = room.sb("y", [P, TILES, D])
        stats = room.sb("stats", [P, TILES, 6])
        mean_var = room.sb("mean_var", [P, TILES, 2])
        rstd = room.sb("rstd", [P, TILES])
        ps_s = [room.psum(f"ps_s{r}", [P, 2 * S]) for r in range(2)]
        ps_st = [room.psum(f"ps_st{r}", [P, 2 * S]) for r in range(2)]
        ps_pv = room.psum("ps_pv", [P, QUADS, S])
        front = [room.psum(f"front{r}", [P, 512]) for r in range(2)]
        front_bf = [f[:, :].bitcast(BF16) for f in front]

        names = ("w_loaded xt_done xt_copied x_ms_ready x_rms_ready qkv_done qkv_taken head_rms_ready "
                 "q_high_ready k_high_ready q_rest_ready k_rest_ready q_mid_ready k_mid_ready q_low_ready k_low_ready "
                 "turned_ready qt_done qt_copied kt_done kt_copied s_done max_done "
                 "m_rows_ready mt_done mt_copied st_done exp_done pv_done ot_copied ot_done attn_ready at_done "
                 "at_copied z_done z_exp_ready gated_ready y_done y_taken var_ready rstd_ready zeroed")
        sem = {k: room.sem(k) for k in names.split()}
        x_loaded = [room.sem(f"x_loaded{r}") for r in range(3)]
        block = room.block()

        def kgroup(h):
            return (h // 2) * NK // HEADS

        def vhead(h):
            return h * NV // HEADS

        def piece(rows, place):
            return rows[:, :, place * HD:(place + 1) * HD]

        def by_tile(a):
            return a.rearrange("p (t h) d -> p t h d", t=TILES)

        def turned_heads(rows):
            whole = by_tile(turned[:, :, :])
            return whole[:, :, 0:HEADS, :] if rows is q_rows else whole[:, :, HEADS:NQK, :]

        def copy_high(eng_copy, rows, place):
            return eng_copy(by_tile(piece(rows, place)), turned_heads(rows))

        @block.sync
        def _(sp):
            def load(s):
                sp.dma_start(x_in[s.slot][:, :, :], seq(x_res, s.n)).then_inc(x_loaded[s.slot], 16)

            for to, of in w["loads"]:
                sp.dma_start(to, of).then_inc(sem["w_loaded"], 16)
            for n in range(3):
                load(Step(0, n))
            with sp.Fori(0, (n_seq - 5) // 3) as i:
                for c in range(3):
                    s = Step(i, 3 + c)
                    sp.wait_ge(sem["xt_done"], (s - 2).n)
                    if gated:
                        sp.wait_ge(sem["x_ms_ready"], (s - 2).n)
                    load(s)
            for n in range(n_seq - 2, n_seq):
                sp.wait_ge(sem["xt_done"], n - 2)
                if gated:
                    sp.wait_ge(sem["x_ms_ready"], n - 2)
                load(Step(0, n))

        @block.tensor
        def _(pe):
            def turn_x(s):
                pe.wait_ge(x_loaded[s.slot], s.turn * 16 + 16)
                for t in range(TILES):
                    last = pe.transpose(front[1][:, t * P:(t + 1) * P], x_in[s.slot][:, t, :], ident[:, :])
                last.then_inc(sem["xt_done"], 1)

            def project_qkv(s):
                pe.wait_ge(sem["xt_copied"], s.n + 1)
                for t in range(TILES):
                    pe.matmul(front[t][:, 0:W], x_t[s.slot][:, t * P:(t + 1) * P], w["qkv"][:, 0:W],
                              start=True, stop=True).then_inc(sem["qkv_done"], 1)

            def turn_rows(s, t, rows):
                is_q = rows is q_rows
                heads, kind = (HEADS, "q") if is_q else (NK, "k")
                if t == 0:
                    for made in ("high", "mid", "low"):
                        pe.wait_ge(sem[f"{kind}_{made}_ready"], s.n + 1)
                if not is_q:
                    pe.wait_ge(sem["qt_copied"], s.n * 2 + (t + 1))
                for j in range(heads // 2):
                    last = pe.transpose(front_bf[t][:, j * P:(j + 1) * P],
                                        rows[:, t * heads + 2 * j:t * heads + 2 * j + 2, :], ident_bf[:, :])
                last.then_inc(sem[f"{kind}t_done"], 1)

            def turn_m(s):
                pe.wait_ge(sem["m_rows_ready"], s.n + 1)
                for t in range(TILES):
                    last = pe.transpose(front_bf[0][:, t * P:(t + 1) * P], m_rows[:, t, :], ident_bf[:, :])
                last.then_inc(sem["mt_done"], 1)

            def scores(s, h):
                half = slice(ROWS * (h % 2), ROWS * (h % 2) + ROWS)
                q, k, out = q_t[s.slot][half, h // 2, :], k_t[s.slot][half, kgroup(h), :], ps_s[h % 2]
                if gated:
                    pe.matmul(out[:, 0:P], q[:, 0:P], k[:, 0:P], start=True, stop=False)
                    pe.matmul(out[:, P:3 * P], q[:, P:S], k[:, :], start=False, stop=False)
                    diagonal = out[:, :].rearrange("p (b c) -> p b c", c=S)[:, :, 0:P]
                    last = pe.matmul(diagonal, ident_bf[:, :], consts["mask_qk"][:, :, :], start=False, stop=True)
                else:
                    pe.matmul(out[:, 0:S], q[:, 0:P], k[:, :], start=True, stop=True)
                    last = pe.matmul(out[:, S:2 * S], q[:, P:S], k[:, :], start=True, stop=True)
                last.then_inc(sem["s_done"], 1)

            def scores_t(s, h):
                half = slice(ROWS * (h % 2), ROWS * (h % 2) + ROWS)
                q, k, out = q_t[s.slot][half, h // 2, :], k_t[s.slot][half, kgroup(h), :], ps_st[h % 2]
                pick, m = consts["pick"][half, h // 2, :], m_t[s.slot][half, :]
                pe.matmul(out[:, 0:S], pick, m, start=True, stop=False)
                if gated:
                    pe.matmul(out[:, S:3 * P], pick, m[:, P:S], start=False, stop=False)
                    pe.matmul(out[:, 0:S], k[:, 0:P], q, start=False, stop=False)
                    pe.matmul(out[:, S:3 * P], k[:, P:S], q[:, P:S], start=False, stop=False)
                    diagonal = out[:, :].rearrange("p (b c) -> p b c", c=S)[:, :, 0:P]
                    last = pe.matmul(diagonal, ident_bf[:, :], consts["mask_kq"][:, :, :], start=False, stop=True)
                else:
                    pe.matmul(out[:, S:2 * S], pick, m, start=False, stop=False)
                    pe.matmul(out[:, 0:S], k[:, 0:P], q, start=False, stop=False)
                    last = pe.matmul(out[:, S:2 * S], k[:, P:S], q, start=False, stop=True)
                last.then_inc(sem["st_done"], 1)

            def weigh_values(s, g):
                pe.wait_ge(sem["exp_done"], s.n * HEADS + 4 * (g + 1))
                for t in range(TILES):
                    for c in range(4):
                        h = 4 * g + c
                        slot = probs[:, h % 8, :]
                        if t == 0:
                            out, p = ps_pv[32 * c:32 * c + 32, g, :], slot[:, 0:S]
                        elif gated:
                            out, p = ps_pv[32 * c:32 * c + 32, g, P:S], slot[:, S:3 * P]
                        else:
                            out, p = ps_pv[32 * c:32 * c + 32, g, :], slot[:, S:2 * S]
                        last = pe.matmul(out, v_ext[s.slot][:, t, vhead(h), :], p, start=t == 0, stop=t == 1)
                last.then_inc(sem["pv_done"], 1)

            def turn_outputs(s, has_front):
                pe.wait_ge(sem["ot_copied"], s.n + 1)
                if has_front:
                    pe.wait_ge(sem["qkv_taken"], s.n + 4)
                else:
                    pe.wait_ge(sem["y_taken"], s.n)
                for t in range(TILES):
                    for g in range(QUADS):
                        last = pe.transpose(front[t][:, g * P:(g + 1) * P], o_t[:, g, t * P:(t + 1) * P], ident[:, :])
                last.then_inc(sem["ot_done"], 1)

            def turn_attn(s):
                pe.wait_ge(sem["attn_ready"], s.n + 1)
                for t in range(TILES):
                    last = pe.transpose(front[0][:, t * P:(t + 1) * P], attn[:, t, :], ident[:, :])
                last.then_inc(sem["at_done"], 1)

            def gate_logits(s):
                pe.wait_ge(sem["at_copied"], s.n + 1)
                pe.matmul(front[1][:, 0:S], w["gate"][:, :], attn_t[:, :], start=True, stop=True)\
                  .then_inc(sem["z_done"], 1)

            def project_out(s):
                pe.wait_ge(sem["gated_ready" if gated else "at_copied"], s.n + 1)
                for t in range(TILES):
                    last = pe.matmul(front[0][:, t * D:(t + 1) * D], attn_t[:, t * P:(t + 1) * P], w["out"][:, :],
                                     start=True, stop=True)
                last.then_inc(sem["y_done"], 1)

            def begin(s, slot, after_attend, after_finish):
                if slot == 0:
                    turn_x(s)
                if slot == 1:
                    if after_attend:
                        pe.wait_ge(sem["mt_copied"], (s - 1).n)
                    project_qkv(s)
                if slot == 11:
                    if after_finish:
                        pe.wait_ge(sem["y_taken"], (s - 2).n)
                        if gated:
                            pe.wait_ge(sem["z_exp_ready"], (s - 2).n)
                    turn_rows(s, 0, q_rows)
                    turn_rows(s, 1, q_rows)
                if slot == 12:
                    turn_rows(s, 0, k_rows)
                if slot == 13:
                    turn_rows(s, 1, k_rows)

            def step(s, do_scores, attend, finish, do_front):
                for h in range(HEADS):
                    if do_scores:
                        if h == 0:
                            pe.wait_ge(sem["kt_copied"], s.n * 2 + 2)
                        if not (isinstance(s.n, int) and s.n == 0 and h < 2):
                            pe.wait_ge(sem["max_done"], s.n * HEADS + (h - 1))
                        scores(s, h)
                    if h == 0:
                        if do_front:
                            begin(s + 1, 0, attend, finish)
                        if attend:
                            if not do_scores:
                                pe.wait_ge(sem["y_taken"], (s - 2).n)
                            turn_m(s - 1)
                        if finish:
                            weigh_values(s - 2, 3)
                        if attend:
                            pe.wait_ge(sem["mt_copied"], s.n)
                    if attend:
                        if not (isinstance(s.n, int) and s.n == 1 and h < 2):
                            pe.wait_ge(sem["exp_done"], (s - 1).n * HEADS + (h - 1))
                        scores_t(s - 1, h)
                    if attend and h in (5, 9, 13):
                        if h == 5 and finish:
                            pe.wait_ge(sem["ot_copied"], (s - 1).n)
                        weigh_values(s - 1, (h - 5) // 4)
                    if finish:
                        if h == 3:
                            turn_outputs(s - 2, do_front)
                        if h == 5:
                            turn_attn(s - 2)
                        if h == 6 and gated:
                            gate_logits(s - 2)
                        if h == 9:
                            project_out(s - 2)
                    if do_front and h > 0:
                        begin(s + 1, h, attend, finish)

            pe.wait_ge(sem["zeroed"], 1)
            pe.wait_ge(sem["w_loaded"], 16 * w["count"])
            for slot in range(HEADS):
                begin(Step(0, 0), slot, False, False)
            run_steps(pe, n_seq, step)

        @block.scalar
        def _(act):
            def take_x(s):
                act.wait_ge(sem["xt_done"], s.n + 1)
                if gated:
                    ins = act.activation(x_t[s.slot][:, :], front[1][:, 0:S], ACT.Copy, scale=w["ln1"][:, 0:1])
                else:
                    ins = act.copy(x_t[s.slot][:, :], front[1][:, 0:S])
                ins.then_inc(sem["xt_copied"], 1)

            def take_queries(s, t):
                act.wait_ge(sem["qt_done"], s.n * 2 + (t + 1))
                act.copy(q_t[s.slot][:, :, t * P:(t + 1) * P],
                         front_bf[t][:, 0:HEADS // 2 * P].rearrange("p (j c) -> p j c", c=P))\
                   .then_inc(sem["qt_copied"], 1)

            def take_m(s):
                act.wait_ge(sem["mt_done"], s.n + 1)
                act.copy(m_t[s.slot][:, :], front_bf[0][:, 0:S]).then_inc(sem["mt_copied"], 1)

            def copy_highs(s, rows, places, done):
                act.wait_ge(sem["turned_ready"], s.n + 1)
                for place in places:
                    last = copy_high(act.copy, rows, place)
                last.then_inc(sem[done], 1)

            def begin(s, slot):
                if slot == 0:
                    take_x(s)
                if slot == 8:
                    copy_highs(s, q_rows, (1, 2), "q_high_ready")
                if slot == 9:
                    copy_highs(s, k_rows, (3, 4), "k_high_ready")
                if slot == 11:
                    take_queries(s, 0)
                if slot == 12:
                    take_queries(s, 1)

            def take_outputs(s):
                act.wait_ge(sem["pv_done"], s.n * QUADS + QUADS)
                for g in range(0, QUADS, 2):
                    last = act.copy(o_t[:, g:g + 2, :], ps_pv[:, g:g + 2, :])
                last.then_inc(sem["ot_copied"], 1)

            def take_attn(s):
                act.wait_ge(sem["at_done"], s.n + 1)
                act.copy(attn_t[:, :], front[0][:, 0:S]).then_inc(sem["at_copied"], 1)

            def gate_exp(s):
                act.wait_ge(sem["z_done"], s.n + 1)
                act.activation(gate_t[:, :], front[1][:, 0:S], ACT.Exp, bias=w["neg_bg"][:, 0:1], scale=-1.0)\
                   .then_inc(sem["z_exp_ready"], 1)

            def step(s, do_scores, attend, finish, do_front):
                if do_front:
                    begin(s + 1, 0)
                if attend:
                    take_m(s - 1)
                for h in range(HEADS):
                    if attend:
                        a = s - 1
                        act.wait_ge(sem["st_done"], a.n * HEADS + (h + 1))
                        if not (isinstance(s.n, int) and s.n == 1 and h < 8):
                            act.wait_ge(sem["pv_done"], a.n * QUADS + (h // 4 - 1))
                        n_cols = 3 * P if gated else 4 * P
                        act.activation(probs[:, h % 8, 0:n_cols], ps_st[h % 2][:, 0:n_cols], ACT.Exp, scale=scale)\
                           .then_inc(sem["exp_done"], 1)
                    if finish:
                        if h == 1:
                            take_outputs(s - 2)
                        if h == 5:
                            take_attn(s - 2)
                        if h == 6 and gated:
                            gate_exp(s - 2)
                    if do_front and h > 0:
                        begin(s + 1, h)

            for slot in range(HEADS):
                begin(Step(0, 0), slot)
            run_steps(act, n_seq, step)

        @block.gpsimd
        def _(pool):
            def x_norm(s):
                pool.wait_ge(sem["x_ms_ready"], s.n + 1)
                pool.tensor_tensor(x_ms_eps[:, :], x_ms[:, :], eps_rms[:, 0:TILES], ALU.add)
                pool.drain()
                pool.tensor_tensor(x_rms[:, :], x_ms_eps[:, :], neg_half[:, 0:TILES], ALU.pow)\
                    .then_inc(sem["x_rms_ready"], 1)

            def rotate(s):
                x, b = qk[:, :, :], swapped[:, :, :]
                pool.tensor_tensor(turned[:, :, :], x, rope_cos[:, :, :], ALU.mult)
                pool.tensor_tensor(b[:, :, 0:4], x[:, :, 4:8], rope_sin[:, :, 0:4], ALU.mult)
                pool.tensor_tensor(b[:, :, 4:8], x[:, :, 0:4], rope_sin[:, :, 4:8], ALU.mult)
                pool.drain()
                last = pool.tensor_tensor(turned[:, :, :], turned[:, :, :], b, ALU.add)
                if gated:
                    pool.drain()
                    pool.wait_ge(sem["head_rms_ready"], s.n + 1)
                    last = pool.tensor_tensor(turned[:, :, :], turned[:, :, :],
                                              head_rms[:, :].unsqueeze(2).broadcast_to([P, TILES * NQK, HD]), ALU.mult)
                last.then_inc(sem["turned_ready"], 1)
                pool.drain()

            def split(s, rows, rest, mid_place, low_place, kind):
                copy_high(pool.tensor_copy, rows, 0)
                pool.drain()
                pool.tensor_tensor(by_tile(rest[:, :, :]), turned_heads(rows), by_tile(piece(rows, 0)), ALU.subtract)\
                    .then_inc(sem[f"{kind}_rest_ready"], 1)
                pool.drain()
                pool.tensor_copy(piece(rows, mid_place), rest[:, :, :])
                pool.drain()
                pool.tensor_tensor(piece(rows, low_place), rest[:, :, :], piece(rows, mid_place), ALU.subtract)\
                    .then_inc(sem[f"{kind}_low_ready"], 1)

            def begin(s):
                if gated:
                    x_norm(s)
                pool.wait_ge(sem["qkv_taken"], s.n + 1)
                rotate(s)
                split(s, q_rows, rest_q, 3, 4, "q")
                split(s, k_rows, rest_k, 1, 2, "k")

            def layer_norm(s):
                pool.wait_ge(sem["var_ready"], s.n + 1)
                pool.tensor_tensor(x_ms_eps[:, :], mean_var[:, :, 1], eps_ln[:, 0:TILES], ALU.add)
                pool.drain()
                pool.tensor_tensor(rstd[:, :], x_ms_eps[:, :], neg_half[:, 0:TILES], ALU.pow)\
                    .then_inc(sem["rstd_ready"], 1)

            def step(s, do_scores, attend, finish, do_front):
                if do_front:
                    begin(s + 1)
                if finish and not gated:
                    layer_norm(s - 2)

            begin(Step(0, 0))
            run_steps(pool, n_seq, step)

        @block.vector
        def _(dve):
            cos, sin = consts["cos"], consts["sin"]

            def x_squares(s):
                dve.wait_ge(x_loaded[s.slot], s.turn * 16 + 16)
                for t in range(TILES):
                    x = x_in[s.slot][:, t, :]
                    last = dve.tensor_tensor_reduce(sq[:, :], x, x, 1.0 / D, 0.0, ALU.mult, ALU.add, x_ms[:, t:t + 1])
                    dve.drain()
                last.then_inc(sem["x_ms_ready"], 1)

            def take_qkv(s):
                if gated:
                    dve.wait_ge(sem["x_rms_ready"], s.n + 1)
                for t in range(TILES):
                    dve.wait_ge(sem["qkv_done"], s.n * 2 + (t + 1))
                    made = qk[:, t * NQK:(t + 1) * NQK, :].rearrange("p h d -> p (h d)")
                    v_made = v_ext[s.slot][:, t, :, 0:HD]
                    v_from = front[t][:, NQK * HD:W].rearrange("p (h d) -> p h d", d=HD)
                    if gated:
                        dve.scalar_tensor_tensor(made, front[t][:, 0:NQK * HD], x_rms[:, t:t + 1],
                                                 w["b_qkv"][:, 0:NQK * HD], ALU.mult, ALU.add)
                        last = dve.scalar_tensor_tensor(
                            v_made, v_from, x_rms[:, t:t + 1],
                            w["b_qkv"][:, NQK * HD:W].rearrange("p (h d) -> p h d", d=HD), ALU.mult, ALU.add)
                    else:
                        dve.tensor_copy(made, front[t][:, 0:NQK * HD])
                        last = dve.tensor_copy(v_made, v_from)
                last.then_inc(sem["qkv_taken"], 1)

            def norm_heads(s, part):
                if part == 0:
                    dve.drain()
                    dve.tensor_tensor(squares[:, :, :], qk[:, :, :], qk[:, :, :], ALU.mult)
                if part == 1:
                    dve.drain()
                    dve.tensor_reduce(sq_sum[:, :], squares[:, :, :], AX_X, ALU.add)
                if part == 2:
                    dve.drain()
                    dve.tensor_scalar(mean_eps[:, :], sq_sum[:, :], 1.0 / HD, RMS_EPS, ALU.mult, ALU.add)
                    dve.tensor_scalar(minus_half[:, :], sq_sum[:, :], -0.5 / HD, -0.5 * RMS_EPS, ALU.mult, ALU.add)
                if part >= 2:
                    last = inverse_root(dve, part - 2, mean_eps[:, :], minus_half[:, :], guess[:, :], head_rms[:, :])
                if part == 5:
                    last.then_inc(sem["head_rms_ready"], 1)

            def copy_mid(s, rows, rest, kind):
                dve.wait_ge(sem[f"{kind}_rest_ready"], s.n + 1)
                dve.tensor_copy(piece(rows, 5), rest[:, :, :]).then_inc(sem[f"{kind}_mid_ready"], 1)

            def take_keys(s, t):
                dve.wait_ge(sem["kt_done"], s.n * 2 + (t + 1))
                dve.tensor_copy(k_t[s.slot][:, :, t * P:(t + 1) * P],
                                front_bf[t][:, 0:NK // 2 * P].rearrange("p (j c) -> p j c", c=P))\
                   .then_inc(sem["kt_copied"], 1)

            def begin(s, slot):
                if slot == 0 and gated:
                    x_squares(s)
                if slot == 2:
                    take_qkv(s)
                if slot in (2, 3, 4, 5, 6, 7) and gated:
                    norm_heads(s, slot - 2)
                if slot == 10:
                    copy_mid(s, q_rows, rest_q, "q")
                if slot == 11:
                    copy_mid(s, k_rows, rest_k, "k")
                if slot == 13:
                    take_keys(s, 0)
                if slot == 14:
                    take_keys(s, 1)

            def split_max(s):
                top = neg_top[:, :, :].rearrange("p t (j c) -> p t c j", c=2)
                m = m_rows[:, :, :].rearrange("p t (c r) -> p t c r", c=2)
                high, low = m[:, :, :, 0:HEADS // 2], m[:, :, :, HEADS // 2:HEADS]
                dve.tensor_copy(high, top)
                dve.drain()
                dve.tensor_tensor(low, top, high, ALU.subtract).then_inc(sem["m_rows_ready"], 1)

            def maximum(s, h):
                dve.wait_ge(sem["s_done"], s.n * HEADS + (h + 1))
                if gated:
                    dve.tensor_reduce(neg_top[:, 0, h:h + 1], ps_s[h % 2][:, 0:P], AX_X, ALU.max, negate=True)
                    last = dve.tensor_reduce(neg_top[:, 1, h:h + 1], ps_s[h % 2][:, P:3 * P], AX_X, ALU.max, negate=True)
                else:
                    last = dve.tensor_reduce(neg_top[:, :, h:h + 1],
                                             ps_s[h % 2][:, :].rearrange("p (t c) -> p t c", t=TILES),
                                             AX_X, ALU.max, negate=True)
                last.then_inc(sem["max_done"], 1)

            def normalise(s):
                dve.wait_ge(sem["ot_done"], s.n + 1)
                for t in range(TILES):
                    o = front[t][:, :].rearrange("p (h c) -> p h c", c=32)
                    dve.reciprocal(inv[:, t, :], o[:, :, HD])
                dve.drain()
                for t in range(TILES):
                    o = front[t][:, :].rearrange("p (h c) -> p h c", c=32)
                    last = dve.tensor_tensor(attn[:, t, :].rearrange("p (h d) -> p h d", d=HD), o[:, :, 0:HD],
                                             inv[:, t, :].unsqueeze(2).broadcast_to([P, HEADS, HD]), ALU.mult)
                last.then_inc(sem["attn_ready"], 1)

            def gate(s):
                dve.wait_ge(sem["z_exp_ready"], s.n + 1)
                dve.tensor_scalar(gate_t[:, :], gate_t[:, :], 1.0, None, ALU.add)
                dve.drain()
                dve.reciprocal(gate_t[:, :], gate_t[:, :])
                dve.drain()
                dve.tensor_tensor(attn_t[:, :], attn_t[:, :], gate_t[:, :], ALU.mult).then_inc(sem["gated_ready"], 1)

            def residual(s):
                dve.wait_ge(sem["y_done"], s.n + 1)
                dve.tensor_tensor(y[:, :, :], front[0][:, 0:S].rearrange("p (t d) -> p t d", t=TILES),
                                  seq(x_res, s.n), ALU.add).then_inc(sem["y_taken"], 1)
                dve.drain()
                if gated:
                    dve.tensor_tensor(seq(out_res, s.n), y[:, :, :],
                                      w["bo"][:, :].unsqueeze(1).broadcast_to([P, TILES, D]), ALU.add)
                else:
                    for t in range(TILES):
                        dve.bn_stats(stats[:, t, :], y[:, t, :])
                    dve.drain()
                    for t in range(TILES):
                        last = dve.bn_aggr(mean_var[:, t, :], stats[:, t, :])
                    last.then_inc(sem["var_ready"], 1)

            def layer_norm(s):
                dve.wait_ge(sem["rstd_ready"], s.n + 1)
                for t in range(TILES):
                    dve.tensor_scalar(tile(out_res, s.n, t), y[:, t, :], mean_var[:, t, 0:1],
                                      rstd[:, t:t + 1], ALU.subtract, ALU.mult)

            def step(s, do_scores, attend, finish, do_front):
                for h in range(HEADS):
                    if do_scores:
                        maximum(s, h)
                    if h == 15 and do_scores:
                        dve.drain()
                        split_max(s)
                        dve.drain()
                    if finish:
                        if h == 4:
                            normalise(s - 2)
                        if h == 7 and gated:
                            gate(s - 2)
                        if h == 9:
                            residual(s - 2)
                        if h == 15 and not gated:
                            layer_norm(s - 2)
                    if do_front:
                        begin(s + 1, h)

            dve.wait_ge(sem["w_loaded"], 16 * w["count"])
            for table, angle in ((rope_cos, cos), (rope_sin, sin)):
                if gated:
                    for t in range(TILES):
                        dve.tensor_tensor(table[:, t * NQK:(t + 1) * NQK, :],
                                          angle[:, t:t + 1, :].broadcast_to([P, NQK, HD]),
                                          w["qk_norm"][:, :].rearrange("p (h d) -> p h d", d=HD), ALU.mult)
                else:
                    dve.tensor_copy(by_tile(table[:, :, :]),
                                    angle[:, :, :].unsqueeze(2).broadcast_to([P, TILES, NQK, HD]))
            dve.memset(q_rows[:, :, :].bitcast(U32), 0)
            dve.memset(k_rows[:, :, :].bitcast(U32), 0)
            dve.memset(m_rows[:, :, :].bitcast(U32), 0)
            for r in range(3):
                dve.memset(v_ext[r][:, :, :, :], 0.0)
            dve.drain()
            for r in range(3):
                last = dve.memset(v_ext[r][:, :, :, HD:HD + 1], 1.0)
            dve.drain()
            last.then_inc(sem["zeroed"], 1)
            for slot in range(HEADS):
                begin(Step(0, 0), slot)
            run_steps(dve, n_seq, step)



class Turn:

    def __init__(self, half, offset):
        self.half, self.offset = half, offset
        self.n = half * 2 + offset
        self.slot = offset % 2
        self.turn = half + offset // 2

    def __add__(self, k):
        return Turn(self.half, self.offset + k)

    def __sub__(self, k):
        return Turn(self.half, self.offset - k)


def run_turns(eng, count, step):
    step(Turn(0, 0), False, True)
    assert count % 2 == 0
    with eng.Fori(0, (count - 2) // 2) as i:
        for c in range(2):
            step(Turn(i, 1 + c), True, True)
    step(Turn(0, count - 1), True, False)


GROUP = 4
COLS = GROUP * P
EXPERTS = 8
HID = 256
CHUNKS = HID // P


def group_of(x_res, n):
    return x_res[:, bass.ds(n * COLS, COLS)].rearrange("p (t d) -> p t d", t=GROUP)


def group_tile(x_res, n, t):
    return x_res[:, bass.ds(n * COLS + t * D, D)]


def mixture_of_experts(nc, n_groups, x_res, x1_res, consts, w):
    ident, neg_half, eps_ln, eps_rms = (consts[k] for k in ("ident", "neg_half", "ln_eps", "rms_eps"))
    UNITS = EXPERTS * CHUNKS
    with ExitStack() as stack:
        room = Room(nc, stack, "moe")
        w1 = room.sb("w1", [D, EXPERTS, 2 * HID])
        w2 = room.sb("w2", [P, EXPERTS, CHUNKS, D])
        b1 = room.sb("b1", [P, EXPERTS, 2 * CHUNKS])
        b2 = room.sb("b2", [EXPERTS, D])
        wr = room.sb("wr", [D, EXPERTS])
        br = room.sb("br", [P, EXPERTS])
        ln2 = room.sb("ln2", [D, 1])
        experts = room.sb("experts", [P, EXPERTS])
        x_in = [room.sb(f"x_in{r}", [P, GROUP, D]) for r in range(2)]
        h_t = [room.sb(f"h_t{r}", [D, COLS]) for r in range(2)]
        mask = [room.sb(f"mask{r}", [P, GROUP, EXPERTS]) for r in range(2)]
        mask_t = [room.sb(f"mask_t{r}", [EXPERTS, COLS]) for r in range(2)]
        acc = [room.sb(f"acc{r}", [P, GROUP, D]) for r in range(2)]
        h = room.sb("h", [P, GROUP, D])
        sq = room.sb("sq", [P, D])
        ms = room.sb("ms", [P, GROUP])
        ms_eps = room.sb("ms_eps", [P, GROUP])
        rms = room.sb("rms", [P, GROUP])
        logits = room.sb("logits", [P, GROUP, EXPERTS])
        best = room.sb("best", [P, GROUP, 8])
        index = room.sb("index", [P, GROUP, 8], U32)
        chosen = room.sb("chosen", [P, GROUP])
        sig = [room.sb(f"sig{r}", [P, COLS]) for r in range(2)]
        hidden = [room.sb(f"hidden{r}", [P, COLS]) for r in range(2)]
        stats = room.sb("stats", [P, GROUP, 6])
        mean_var = room.sb("mean_var", [P, GROUP, 2])
        var_eps = room.sb("var_eps", [P, GROUP])
        rstd = room.sb("rstd", [P, GROUP])
        ps_value = [room.psum(f"ps_value{r}", [P, COLS]) for r in range(2)]
        ps_gate = [room.psum(f"ps_gate{r}", [P, COLS]) for r in range(2)]
        ps_y = [room.psum(f"ps_y{r}", [P, GROUP, D]) for r in range(2)]
        ps_h = room.psum("ps_h", [P, COLS])
        ps_r = room.psum("ps_r", [P, COLS])
        names = ("w_loaded ms_ready rms_ready h_ready ht_done ht_copied logits_done logits_taken mask_ready "
                 "mask_turned mask_copied acc_ready value_done gate_done sig_ready hidden_ready y_done y_taken "
                 "var_ready rstd_ready finished")
        sem = {k: room.sem(k) for k in names.split()}
        x_loaded = [room.sem(f"x_loaded{r}") for r in range(2)]
        loads = [(w1[:, :, :], w["W1"]), (w2[:, :, :, :], w["W2"]), (b1[:, :, :], w["b1"]),
                 (b2[:, :], w["b2"]), (wr[:, :], w["Wr"]), (br[:, :], w["br"]), (ln2[:, :], w["ln2"]),
                 (experts[:, :], w["experts"])]
        block = room.block()
        YS = EXPERTS + 1

        @block.sync
        def _(sp):
            def load(s):
                sp.dma_start(x_in[s.slot][:, :, :], group_of(x1_res, s.n)).then_inc(x_loaded[s.slot], 16)

            for dst, src in loads:
                sp.dma_start(dst, src).then_inc(sem["w_loaded"], 16)
            load(Turn(0, 0))
            load(Turn(0, 1))
            with sp.Fori(0, (n_groups - 2) // 2) as i:
                for c in range(2):
                    s = Turn(i, 2 + c)
                    sp.wait_ge(sem["h_ready"], (s - 1).n)
                    sp.wait_ge(sem["acc_ready"], (s - 1).n)
                    load(s)

        @block.tensor
        def _(pe):
            def turn_h(s):
                pe.wait_ge(sem["h_ready"], s.n + 1)
                for t in range(GROUP):
                    last = pe.transpose(ps_h[:, t * P:(t + 1) * P], h[:, t, :], ident[:, :])
                last.then_inc(sem["ht_done"], 1)

            def route(s):
                pe.wait_ge(sem["ht_copied"], s.n + 1)
                for t in range(GROUP):
                    last = pe.matmul(ps_r[:, t * EXPERTS:(t + 1) * EXPERTS], h_t[s.slot][:, t * P:(t + 1) * P],
                                     wr[:, :], start=True, stop=True)
                last.then_inc(sem["logits_done"], 1)

            def turn_mask(s):
                pe.wait_ge(sem["mask_ready"], s.n + 1)
                for t in range(GROUP):
                    last = pe.transpose(ps_r[0:EXPERTS, t * P:(t + 1) * P], mask[s.slot][:, t, :], ident[:, :])
                last.then_inc(sem["mask_turned"], 1)

            def biases(s):
                pe.wait_ge(sem["mask_copied"], s.n + 1)
                bank(s, 0)
                for t in range(GROUP):
                    last = pe.matmul(y_bank(s, 0)[:, t, :], mask_t[s.slot][:, t * P:(t + 1) * P], b2[:, :],
                                     start=True, stop=True)
                last.then_inc(sem["y_done"], 1)

            def y_bank(s, k):
                return ps_y[(s.slot * YS + k) % 2]

            def bank(s, k):
                if not (isinstance(s.n, int) and s.n * YS + k < 2):
                    pe.wait_ge(sem["y_taken"], s.n * YS + (k - 1))

            def up(s, k):
                e, c = k // CHUNKS, k % CHUNKS
                if not (isinstance(s.n, int) and s.n * UNITS + k < 2):
                    pe.wait_ge(sem["hidden_ready"], s.n * UNITS + (k - 1))
                pe.matmul(ps_gate[k % 2][:, :], w1[:, e, HID + c * P:HID + (c + 1) * P], h_t[s.slot][:, :],
                          start=True, stop=True).then_inc(sem["gate_done"], 1)
                pe.matmul(ps_value[k % 2][:, :], w1[:, e, c * P:(c + 1) * P], h_t[s.slot][:, :],
                          start=True, stop=True).then_inc(sem["value_done"], 1)

            def down(s, k):
                e, c = k // CHUNKS, k % CHUNKS
                pe.wait_ge(sem["hidden_ready"], s.n * UNITS + (k + 1))
                if c == 0:
                    bank(s, 1 + e)
                for t in range(GROUP):
                    last = pe.matmul(y_bank(s, 1 + e)[:, t, :], hidden[k % 2][:, t * P:(t + 1) * P],
                                     w2[:, e, c, :], start=c == 0 and t == 0, stop=c == CHUNKS - 1 and t == GROUP - 1)
                if c == CHUNKS - 1:
                    last.then_inc(sem["y_done"], 1)

            def step(s, finish, front):
                biases(s)
                for k in range(UNITS + 1):
                    if k < UNITS:
                        up(s, k)
                    if k >= 1:
                        down(s, k - 1)
                    if front:
                        if k == 5:
                            turn_h(s + 1)
                        if k == 7:
                            route(s + 1)
                        if k == 10:
                            turn_mask(s + 1)

            pe.wait_ge(sem["w_loaded"], 16 * len(loads))
            turn_h(Turn(0, 0))
            route(Turn(0, 0))
            turn_mask(Turn(0, 0))
            run_turns(pe, n_groups, step)

        @block.scalar
        def _(act):
            def take_h(s):
                act.wait_ge(sem["ht_done"], s.n + 1)
                act.activation(h_t[s.slot][:, :], ps_h[:, :], ACT.Copy, scale=ln2[:, 0:1])\
                   .then_inc(sem["ht_copied"], 1)

            def take_mask(s):
                act.wait_ge(sem["mask_turned"], s.n + 1)
                act.copy(mask_t[s.slot][:, :], ps_r[0:EXPERTS, :]).then_inc(sem["mask_copied"], 1)

            def step(s, finish, front):
                for k in range(UNITS):
                    e, c = k // CHUNKS, k % CHUNKS
                    act.wait_ge(sem["gate_done"], s.n * UNITS + (k + 1))
                    if not (isinstance(s.n, int) and s.n * UNITS + k < 2):
                        act.wait_ge(sem["hidden_ready"], s.n * UNITS + (k - 1))
                    act.activation(sig[k % 2][:, :], ps_gate[k % 2][:, :], ACT.Sigmoid,
                                   bias=b1[:, e, CHUNKS + c:CHUNKS + c + 1]).then_inc(sem["sig_ready"], 1)
                    if front:
                        if k == 6:
                            take_h(s + 1)
                        if k == 11:
                            take_mask(s + 1)

            take_h(Turn(0, 0))
            take_mask(Turn(0, 0))
            run_turns(act, n_groups, step)

        @block.gpsimd
        def _(pool):
            def x_norm(s):
                pool.wait_ge(sem["ms_ready"], s.n + 1)
                pool.tensor_tensor(ms_eps[:, :], ms[:, :], eps_rms[:, 0:GROUP], ALU.add)
                pool.drain()
                pool.tensor_tensor(rms[:, :], ms_eps[:, :], neg_half[:, 0:GROUP], ALU.pow)\
                    .then_inc(sem["rms_ready"], 1)

            def start_sum(s):
                pool.wait_ge(x_loaded[s.slot], s.turn * 16 + 16)
                if not (isinstance(s.n, int) and s.n < 2):
                    pool.wait_ge(sem["finished"], (s - 1).n)
                pool.tensor_tensor(acc[s.slot][:, :, :], x_in[s.slot][:, :, :], group_of(x_res, s.n), ALU.add)\
                    .then_inc(sem["acc_ready"], 1)

            def layer_norm(s):
                pool.wait_ge(sem["var_ready"], s.n + 1)
                pool.tensor_tensor(var_eps[:, :], mean_var[:, :, 1], eps_ln[:, 0:GROUP], ALU.add)
                pool.drain()
                pool.tensor_tensor(rstd[:, :], var_eps[:, :], neg_half[:, 0:GROUP], ALU.pow)\
                    .then_inc(sem["rstd_ready"], 1)

            def step(s, finish, front):
                if finish:
                    layer_norm(s - 1)
                if front:
                    x_norm(s + 1)
                    start_sum(s + 1)

            x_norm(Turn(0, 0))
            start_sum(Turn(0, 0))
            run_turns(pool, n_groups, step)
            layer_norm(Turn(0, n_groups - 1))

        @block.vector
        def _(dve):
            def squares(s):
                dve.wait_ge(x_loaded[s.slot], s.turn * 16 + 16)
                for t in range(GROUP):
                    x = x_in[s.slot][:, t, :]
                    last = dve.tensor_tensor_reduce(sq[:, :], x, x, 1.0 / D, 0.0, ALU.mult, ALU.add, ms[:, t:t + 1])
                    dve.drain()
                last.then_inc(sem["ms_ready"], 1)

            def scale_h(s):
                dve.wait_ge(sem["rms_ready"], s.n + 1)
                for t in range(GROUP):
                    last = dve.tensor_scalar(h[:, t, :], x_in[s.slot][:, t, :], rms[:, t:t + 1], None, ALU.mult)
                last.then_inc(sem["h_ready"], 1)

            def choose(s):
                dve.wait_ge(sem["logits_done"], s.n + 1)
                dve.tensor_tensor(logits[:, :, :], ps_r[:, 0:GROUP * EXPERTS].rearrange("p (t e) -> p t e", t=GROUP),
                                  br[:, :].unsqueeze(1).broadcast_to([P, GROUP, EXPERTS]), ALU.add)
                dve.drain()
                for t in range(GROUP):
                    dve.max(best[:, t, :], logits[:, t, :])
                dve.drain()
                for t in range(GROUP):
                    dve.max_index(index[:, t, :], best[:, t, :], logits[:, t, :])
                dve.drain()
                dve.tensor_copy(chosen[:, :], index[:, :, 0])
                dve.drain()
                for t in range(GROUP):
                    last = dve.tensor_scalar(mask[s.slot][:, t, :], experts[:, :], chosen[:, t:t + 1], None, ALU.is_equal)
                last.then_inc(sem["mask_ready"], 1)

            def take_biases(s):
                dve.wait_ge(sem["y_done"], s.n * YS + 1)
                dve.wait_ge(sem["acc_ready"], s.n + 1)
                a, y = acc[s.slot], ps_y[(s.slot * YS) % 2]
                dve.tensor_tensor(a[:, :, :], y[:, :, :], a[:, :, :], ALU.add).then_inc(sem["y_taken"], 1)

            def take(s, e):
                dve.drain()
                dve.wait_ge(sem["y_done"], s.n * YS + (e + 2))
                a, y = acc[s.slot], ps_y[(s.slot * YS + 1 + e) % 2]
                for t in range(GROUP):
                    last = dve.scalar_tensor_tensor(a[:, t, :], y[:, t, :], mask[s.slot][:, t, e:e + 1], a[:, t, :],
                                                    ALU.mult, ALU.add)
                last.then_inc(sem["y_taken"], 1)

            def statistics(s):
                dve.drain()
                for t in range(GROUP):
                    dve.bn_stats(stats[:, t, :], acc[s.slot][:, t, :])
                dve.drain()
                for t in range(GROUP):
                    last = dve.bn_aggr(mean_var[:, t, :], stats[:, t, :])
                last.then_inc(sem["var_ready"], 1)

            def normalise(s):
                dve.wait_ge(sem["rstd_ready"], s.n + 1)
                for t in range(GROUP):
                    last = dve.tensor_scalar(group_tile(x_res, s.n, t), acc[s.slot][:, t, :], mean_var[:, t, 0:1],
                                             rstd[:, t:t + 1], ALU.subtract, ALU.mult)
                last.then_inc(sem["finished"], 1)

            def step(s, finish, front):
                take_biases(s)
                for k in range(UNITS):
                    e, c = k // CHUNKS, k % CHUNKS
                    dve.wait_ge(sem["sig_ready"], s.n * UNITS + (k + 1))
                    dve.wait_ge(sem["value_done"], s.n * UNITS + (k + 1))
                    dve.scalar_tensor_tensor(hidden[k % 2][:, :], ps_value[k % 2][:, :], b1[:, e, c:c + 1],
                                             sig[k % 2][:, :], ALU.add, ALU.mult).then_inc(sem["hidden_ready"], 1)
                    if k >= 2 and k % 2 == 0:
                        take(s, k // 2 - 1)
                    if finish and k == 1:
                        normalise(s - 1)
                    if front:
                        if k == 3:
                            squares(s + 1)
                        if k == 5:
                            scale_h(s + 1)
                        if k == 9:
                            choose(s + 1)
                take(s, EXPERTS - 1)
                statistics(s)

            dve.wait_ge(sem["w_loaded"], 16 * len(loads))
            squares(Turn(0, 0))
            scale_h(Turn(0, 0))
            choose(Turn(0, 0))
            run_turns(dve, n_groups, step)
            normalise(Turn(0, n_groups - 1))


def shift_loads(eng, src, dst, n, count, done):
    half = D // 2
    v = src[:, bass.ds(n * count * D, count * D)].rearrange("p (t d) -> p t d", t=count)
    eng.dma_start(dst[:, :, 0:half], v[:, :, 0:half]).then_inc(done, 16)
    eng.dma_start(dst[1:P, :, half:D], v[0:P - 1, :, half:D]).then_inc(done, 16)
    eng.dma_start(dst[0:1, 1:count:2, half:D], v[P - 1:P, 0:count:2, half:D]).then_inc(done, 16)


FF = 341
FF_CHUNKS = [(c, min(P, FF - c)) for c in range(0, FF, P)]


def gated_feed_forward(nc, n_groups, layer, x_res, consts, w, first=None, out_dram=None):
    ident, neg_half, eps_ln = (consts[k] for k in ("ident", "neg_half", "ln_eps"))
    N = len(FF_CHUNKS)
    final = out_dram is not None
    with ExitStack() as stack:
        room = Room(nc, stack, f"ffn{layer}")
        w1 = room.sb("w1", [D, 2 * FF])
        w2 = room.sb("w2", [P, N, D])
        b1 = room.sb("b1", [P, 2 * N])
        b2 = room.sb("b2", [P, D])
        ln_g = room.sb("ln_g", [D, 1])
        ln_b = room.sb("ln_b", [D, 1])
        shifted = [room.sb(f"shifted{r}", [P, GROUP, D]) for r in range(2)]
        h_t = [room.sb(f"h_t{r}", [D, COLS]) for r in range(2)]
        h = room.sb("h", [P, GROUP, D])
        x_b = [room.sb(f"x_b{r}", [P, GROUP, D]) for r in range(2)]
        result = [room.sb(f"result{r}", [P, GROUP, D]) for r in range(2)]
        gelu = [room.sb(f"gelu{r}", [P, COLS]) for r in range(3)]
        hidden = [room.sb(f"hidden{r}", [P, COLS]) for r in range(3)]
        stats = room.sb("stats", [P, GROUP, 6])
        mean_var = room.sb("mean_var", [P, GROUP, 2])
        var_eps = room.sb("var_eps", [P, GROUP])
        rstd = room.sb("rstd", [P, GROUP])
        stats2 = room.sb("stats2", [P, GROUP, 6])
        mean_var2 = room.sb("mean_var2", [P, GROUP, 2])
        rstd2 = room.sb("rstd2", [P, GROUP])
        ps_value = [room.psum(f"ps_value{r}", [P, COLS]) for r in range(2)]
        ps_gate = [room.psum(f"ps_gate{r}", [P, COLS]) for r in range(2)]
        ps_y = [room.psum(f"ps_y{r}", [P, GROUP, D]) for r in range(2)]
        ps_h = room.psum("ps_h", [P, COLS])
        names = ("w_loaded zeroed var_ready rstd_ready h_ready ht_done ht_copied xb_ready value_done gate_done "
                 "gelu_ready hidden_ready y_done y_taken var2_ready rstd2_ready result_ready")
        sem = {k: room.sem(k) for k in names.split()}
        loaded = [room.sem(f"loaded{r}") for r in range(2)]
        stored = [room.sem(f"stored{r}") for r in range(2)]
        loads = [(w1[:, :], w["w1"]), (b2[:, :], w["b2"]),
                 (ln_g[:, :], w["ln_g"]), (ln_b[:, :], w["ln_b"])]
        for k, (c, m) in enumerate(FF_CHUNKS):
            loads += [(w2[0:m, k, :], w["w2"][c:c + m, :]), (b1[0:m, k:k + 1], w["b1"][c:c + m, :]),
                      (b1[0:m, N + k:N + k + 1], w["b1"][FF + c:FF + c + m, :])]
        block = room.block()

        @block.sync
        def _(sp):
            def load(s):
                shift_loads(sp, x_res, shifted[s.slot], s.n, GROUP, loaded[s.slot])

            def store(s):
                sp.wait_ge(sem["result_ready"], s.n + 1)
                sp.dma_start(out_dram[bass.ds(s.n * 2, 2)].rearrange("b (t p) d -> p (b t) d", p=P),
                             result[s.slot][:, :, :]).then_inc(stored[s.slot], 16)

            for dst, src in loads:
                sp.dma_start(dst, src).then_inc(sem["w_loaded"], 16)
            sp.wait_ge(sem["zeroed"], 1)
            load(Turn(0, 0))
            load(Turn(0, 1))
            with sp.Fori(0, (n_groups - 2) // 2) as i:
                for c in range(2):
                    s = Turn(i, 2 + c)
                    sp.wait_ge(sem["h_ready"], (s - 1).n)
                    load(s)
                    if final:
                        store(s - 2)
            if final:
                store(Turn(0, n_groups - 2))
                store(Turn(0, n_groups - 1))
                for r in range(2):
                    sp.wait_ge(stored[r], 16 * (n_groups // 2))

        @block.tensor
        def _(pe):
            def turn_h(s):
                pe.wait_ge(sem["h_ready"], s.n + 1)
                for t in range(GROUP):
                    last = pe.transpose(ps_h[:, t * P:(t + 1) * P], h[:, t, :], ident[:, :])
                last.then_inc(sem["ht_done"], 1)

            def up(s, k):
                c, m = FF_CHUNKS[k]
                r = (s.slot * N + k) % 2
                if k == 0:
                    pe.wait_ge(sem["ht_copied"], s.n + 1)
                if not (isinstance(s.n, int) and s.n * N + k < 2):
                    pe.wait_ge(sem["hidden_ready"], s.n * N + (k - 1))
                pe.matmul(ps_gate[r][0:m, :], w1[:, FF + c:FF + c + m], h_t[s.slot][:, :],
                          start=True, stop=True).then_inc(sem["gate_done"], 1)
                pe.matmul(ps_value[r][0:m, :], w1[:, c:c + m], h_t[s.slot][:, :],
                          start=True, stop=True).then_inc(sem["value_done"], 1)

            def down(s, k):
                c, m = FF_CHUNKS[k]
                pe.wait_ge(sem["hidden_ready"], s.n * N + (k + 1))
                if k == 0 and not (isinstance(s.n, int) and s.n < 2):
                    pe.wait_ge(sem["y_taken"], (s - 1).n)
                for t in range(GROUP):
                    last = pe.matmul(ps_y[s.slot][:, t, :], hidden[k][0:m, t * P:(t + 1) * P], w2[0:m, k, :],
                                     start=k == 0 and t == 0, stop=k == N - 1 and t == GROUP - 1)
                if k == N - 1:
                    last.then_inc(sem["y_done"], 1)

            def step(s, finish, front):
                for k in range(N):
                    up(s, k)
                    if k == 0 and finish:
                        down(s - 1, N - 1)
                    if k >= 1:
                        down(s, k - 1)
                    if front and k == 1:
                        turn_h(s + 1)

            pe.wait_ge(sem["w_loaded"], 16 * len(loads))
            turn_h(Turn(0, 0))
            run_turns(pe, n_groups, step)
            down(Turn(0, n_groups - 1), N - 1)

        @block.scalar
        def _(act):
            def take_h(s):
                act.wait_ge(sem["ht_done"], s.n + 1)
                act.activation(h_t[s.slot][:, :], ps_h[:, :], ACT.Identity, bias=ln_b[:, 0:1], scale=ln_g[:, 0:1])\
                   .then_inc(sem["ht_copied"], 1)

            def step(s, finish, front):
                for k, (c, m) in enumerate(FF_CHUNKS):
                    r = (s.slot * N + k) % 2
                    act.wait_ge(sem["gate_done"], s.n * N + (k + 1))
                    if not (isinstance(s.n, int) and s.n == 0):
                        act.wait_ge(sem["hidden_ready"], s.n * N + (k + 1 - N))
                    act.activation(gelu[k][0:m, :], ps_gate[r][0:m, :], ACT.Gelu,
                                   bias=b1[0:m, N + k:N + k + 1]).then_inc(sem["gelu_ready"], 1)
                    if front and k == 1:
                        take_h(s + 1)

            take_h(Turn(0, 0))
            run_turns(act, n_groups, step)

        @block.gpsimd
        def _(pool):
            def layer_norm(s):
                pool.wait_ge(sem["var_ready"], s.n + 1)
                pool.tensor_tensor(var_eps[:, :], mean_var[:, :, 1], eps_ln[:, 0:GROUP], ALU.add)
                pool.drain()
                pool.tensor_tensor(rstd[:, :], var_eps[:, :], neg_half[:, 0:GROUP], ALU.pow)\
                    .then_inc(sem["rstd_ready"], 1)

            def last_norm(s):
                pool.wait_ge(sem["var2_ready"], s.n + 1)
                pool.tensor_tensor(var_eps[:, :], mean_var2[:, :, 1], eps_ln[:, 0:GROUP], ALU.add)
                pool.drain()
                pool.tensor_tensor(rstd2[:, :], var_eps[:, :], neg_half[:, 0:GROUP], ALU.pow)\
                    .then_inc(sem["rstd2_ready"], 1)

            def add_bias(s):
                if not (isinstance(s.n, int) and s.n < 2):
                    pool.wait_ge(sem["y_taken"], (s - 1).n)
                pool.tensor_tensor(x_b[s.slot][:, :, :], group_of(x_res, s.n),
                                   b2[:, :].unsqueeze(1).broadcast_to([P, GROUP, D]), ALU.add)\
                    .then_inc(sem["xb_ready"], 1)
                if final:
                    pool.wait_ge(sem["xb_ready"], s.n * 2 + 1)
                    pool.tensor_tensor(x_b[s.slot][:, :, :], x_b[s.slot][:, :, :], group_of(first, s.n), ALU.add)\
                        .then_inc(sem["xb_ready"], 1)

            def step(s, finish, front):
                add_bias(s)
                if front:
                    layer_norm(s + 1)
                if finish and final:
                    last_norm(s - 1)

            pool.wait_ge(sem["w_loaded"], 16 * len(loads))
            layer_norm(Turn(0, 0))
            run_turns(pool, n_groups, step)
            if final:
                last_norm(Turn(0, n_groups - 1))

        @block.vector
        def _(dve):
            def statistics(s):
                dve.wait_ge(loaded[s.slot], s.turn * 48 + 48)
                for t in range(GROUP):
                    dve.bn_stats(stats[:, t, :], shifted[s.slot][:, t, :])
                dve.drain()
                for t in range(GROUP):
                    last = dve.bn_aggr(mean_var[:, t, :], stats[:, t, :])
                last.then_inc(sem["var_ready"], 1)

            def normalise(s):
                dve.wait_ge(sem["rstd_ready"], s.n + 1)
                if not (isinstance(s.n, int) and s.n == 0):
                    dve.wait_ge(sem["ht_done"], s.n)
                for t in range(GROUP):
                    last = dve.tensor_scalar(h[:, t, :], shifted[s.slot][:, t, :], mean_var[:, t, 0:1],
                                             rstd[:, t:t + 1], ALU.subtract, ALU.mult)
                last.then_inc(sem["h_ready"], 1)

            def take(s):
                dve.wait_ge(sem["y_done"], s.n + 1)
                dve.wait_ge(sem["xb_ready"], s.n * 2 + 2 if final else s.n + 1)
                out = x_b[s.slot][:, :, :] if final else group_of(x_res, s.n)
                ins = dve.tensor_tensor(out, ps_y[s.slot][:, :, :], x_b[s.slot][:, :, :], ALU.add)
                if not final:
                    ins.then_inc(sem["y_taken"], 1)
                    return
                dve.drain()
                for t in range(GROUP):
                    dve.bn_stats(stats2[:, t, :], x_b[s.slot][:, t, :])
                dve.drain()
                for t in range(GROUP):
                    last = dve.bn_aggr(mean_var2[:, t, :], stats2[:, t, :])
                last.then_inc(sem["var2_ready"], 1)

            def last_normalise(s):
                dve.wait_ge(sem["rstd2_ready"], s.n + 1)
                if not (isinstance(s.n, int) and s.n < 2):
                    dve.wait_ge(stored[s.slot], s.turn * 16)
                for t in range(GROUP):
                    last = dve.tensor_scalar(result[s.slot][:, t, :], x_b[s.slot][:, t, :], mean_var2[:, t, 0:1],
                                             rstd2[:, t:t + 1], ALU.subtract, ALU.mult)
                last.then_inc(sem["result_ready"], 1)
                dve.drain().then_inc(sem["y_taken"], 1)

            def step(s, finish, front):
                for k, (c, m) in enumerate(FF_CHUNKS):
                    r = (s.slot * N + k) % 2
                    dve.wait_ge(sem["gelu_ready"], s.n * N + (k + 1))
                    dve.wait_ge(sem["value_done"], s.n * N + (k + 1))
                    dve.scalar_tensor_tensor(hidden[k][0:m, :], ps_value[r][0:m, :], b1[0:m, k:k + 1],
                                             gelu[k][0:m, :], ALU.add, ALU.mult).then_inc(sem["hidden_ready"], 1)
                    if front and k == 0:
                        statistics(s + 1)
                        normalise(s + 1)
                    if finish and k == 1:
                        take(s - 1)
                    if finish and k == 2 and final:
                        last_normalise(s - 1)

            for r in range(2):
                last = dve.memset(shifted[r][0:1, :, D // 2:D], 0.0)
            dve.drain().then_inc(sem["zeroed"], 1)
            statistics(Turn(0, 0))
            normalise(Turn(0, 0))
            run_turns(dve, n_groups, step)
            take(Turn(0, n_groups - 1))
            if final:
                last_normalise(Turn(0, n_groups - 1))



LH = 8
LD = 64
WINDOW = 64
INNER = LH * LD


def windowed_attention(nc, n_seq, layer, src, dst, consts, w):
    ident, ident_bf, neg_half, band = (consts[k] for k in ("ident", "ident_bf", "neg_half", "band"))
    FIRST, SECOND = slice(0, P), slice(P + WINDOW, 3 * P)
    with ExitStack() as stack:
        room = Room(nc, stack, f"win{layer}")
        w_qkv = room.sb("w_qkv", [D, 3, INNER])
        w_out = room.sb("w_out", [P, INNER // P, D])
        scales = room.sb("scales", [P, 2, LD])
        cos = [room.sb(f"cos{c}", [P, TILES, LD]) for c in range(2)]
        sin = [room.sb(f"sin{c}", [P, TILES, LD]) for c in range(2)]
        shifted = [room.sb(f"shifted{r}", [P, TILES, D]) for r in range(2)]
        h_t = room.sb("h_t", [D, S])
        raw = [room.sb(f"raw{c}", [P, TILES * LH, LD]) for c in range(2)]
        turned = [room.sb(f"turned{c}", [P, TILES * LH, LD]) for c in range(2)]
        swapped = [room.sb(f"swapped{c}", [P, TILES * LH, LD]) for c in range(2)]
        squares = [room.sb(f"squares{c}", [P, TILES * LH, LD]) for c in range(2)]
        sq_sum = room.sb("sq_sum", [P, 2, TILES * LH])
        minus_half = room.sb("minus_half", [P, 2, TILES * LH])
        guess = room.sb("guess", [P, 2, TILES * LH])
        inv_norm = room.sb("inv_norm", [P, 2, TILES * LH])
        v = [room.sb(f"v{r}", [P, TILES, INNER]) for r in range(2)]
        qk_t = [[room.sb(f"qk_t{r}{c}", [P, LH // 2, S]) for c in range(2)] for r in range(2)]
        neg_top = room.sb("neg_top", [P, 2, TILES])
        probs = [room.sb(f"probs{r}", [P, 3 * P]) for r in range(2)]
        probs_t = [room.sb(f"probs_t{r}", [P, 3 * P]) for r in range(2)]
        total = [room.sb(f"total{r}", [P, TILES, LH]) for r in range(2)]
        inv = room.sb("inv", [P, TILES, LH])
        attn = room.sb("attn", [P, TILES, INNER])
        attn_t = room.sb("attn_t", [P, INNER // P, S])
        ps_s = [room.psum(f"ps_s{r}", [P, 512]) for r in range(2)]
        ps_p = [room.psum(f"ps_p{r}", [P, 512]) for r in range(2)]
        ps_o = [room.psum(f"ps_o{r}", [P, INNER]) for r in range(2)]
        bank = [room.psum(f"bank{r}", [P, 512]) for r in range(2)]
        names = ("w_loaded zeroed ht_done ht_copied qkv_done raw_ready v_ready sq_ready "
                 "k_cos_ready rotated qk_ready qkt_done qkt_copied s_done max_ready exp_done pt_done pt_copied "
                 "o_done attn_ready at_done at_copied y_done y_taken")
        sem = {k: room.sem(k) for k in names.split()}
        loaded = [room.sem(f"loaded{r}") for r in range(2)]
        loads = [(w_qkv[:, :, :], w["qkv"]), (w_out[:, :, :], w["out"]), (scales[:, :, :], w["scales"])]
        for c in range(2):
            loads += [(cos[c][:, :, :], w["cos"][c]), (sin[c][:, :, :], w["sin"][c])]
        block = room.block()

        @block.sync
        def _(sp):
            def load(s):
                shift_loads(sp, src, shifted[s.slot], s.n, TILES, loaded[s.slot])

            for to, of in loads:
                sp.dma_start(to, of).then_inc(sem["w_loaded"], 16)
            sp.wait_ge(sem["zeroed"], 1)
            load(Turn(0, 0))
            load(Turn(0, 1))
            with sp.Fori(0, (n_seq - 2) // 2) as i:
                for c in range(2):
                    s = Turn(i, 2 + c)
                    sp.wait_ge(sem["ht_done"], (s - 1).n)
                    load(s)

        @block.tensor
        def _(pe):
            def turn_h(s):
                pe.wait_ge(loaded[s.slot], s.turn * 48 + 48)
                for t in range(TILES):
                    last = pe.transpose(bank[0][:, t * P:(t + 1) * P], shifted[s.slot][:, t, :], ident[:, :])
                last.then_inc(sem["ht_done"], 1)

            def project(s, c):
                pe.wait_ge(sem["ht_copied"], s.n + 1)
                for t in range(TILES):
                    if c >= 1:
                        pe.wait_ge(sem["raw_ready"], s.n * 4 + ((c - 1) * 2 + t + 1))
                    pe.matmul(bank[t][:, :], h_t[:, t * P:(t + 1) * P], w_qkv[:, c, :],
                              start=True, stop=True).then_inc(sem["qkv_done"], 1)

            def turn_qk(s, c):
                pe.wait_ge(sem["qk_ready"], s.n * 2 + (c + 1))
                for t in range(TILES):
                    if c == 1:
                        pe.wait_ge(sem["qkt_copied"], s.n * 4 + (t + 1))
                    for j in range(LH // 2):
                        at = t * LH + 2 * j
                        last = pe.transpose(bank[t][:, j * P:(j + 1) * P], raw[c][:, at:at + 2, :], ident[:, :])
                    last.then_inc(sem["qkt_done"], 1)

            def scores(s, h):
                half = slice(LD * (h % 2), LD * (h % 2) + LD)
                q, k = (qk_t[s.slot][c][half, h // 2, :] for c in range(2))
                if not (isinstance(s.n, int) and s.n == 0 and h < 2):
                    pe.wait_ge(sem["exp_done"], s.n * LH + (h - 1))
                out = ps_s[h % 2]
                pe.matmul(out[:, 0:P], q[:, 0:P], k[:, 0:P], start=True, stop=False)
                pe.matmul(out[:, P:5 * WINDOW], q[:, P:S], k[:, WINDOW:S], start=False, stop=False)
                pe.matmul(out[:, 0:5 * WINDOW], ident_bf[:, :], band[:, :], start=False, stop=True)\
                  .then_inc(sem["s_done"], 1)

            def turn_probs(s, h):
                pe.wait_ge(sem["exp_done"], s.n * LH + (h + 1))
                if not (isinstance(s.n, int) and s.n == 0 and h < 2):
                    pe.wait_ge(sem["pt_copied"], s.n * LH + (h - 1))
                for b in range(3):
                    last = pe.transpose(ps_p[h % 2][:, b * P:(b + 1) * P], probs[h % 2][:, b * P:(b + 1) * P],
                                        ident[:, :])
                last.then_inc(sem["pt_done"], 1)

            def weigh(s, h):
                pe.wait_ge(sem["pt_copied"], s.n * LH + (h + 1))
                if h == 0 and not (isinstance(s.n, int) and s.n == 0):
                    pe.wait_ge(sem["attn_ready"], s.n)
                cols = slice(h * LD, (h + 1) * LD)
                p = probs_t[h % 2]
                pe.matmul(ps_o[0][:, cols], p[:, 0:P], v[s.slot][:, 0, cols], start=True, stop=True)
                pe.matmul(ps_o[1][:, cols], p[:, P:2 * P], v[s.slot][:, 0, cols], start=True, stop=False)
                pe.matmul(ps_o[1][:, cols], p[:, 2 * P:3 * P], v[s.slot][:, 1, cols],
                          start=False, stop=True).then_inc(sem["o_done"], 1)

            def turn_attn(s):
                pe.wait_ge(sem["attn_ready"], s.n + 1)
                for t in range(TILES):
                    for c in range(INNER // P):
                        last = pe.transpose(bank[t][:, c * P:(c + 1) * P], attn[:, t, c * P:(c + 1) * P], ident[:, :])
                    last.then_inc(sem["at_done"], 1)

            def project_out(s):
                pe.wait_ge(sem["at_copied"], s.n * 2 + 2)
                for t in range(TILES):
                    for c in range(INNER // P):
                        last = pe.matmul(bank[0][:, t * D:(t + 1) * D], attn_t[:, c, t * P:(t + 1) * P],
                                         w_out[:, c, :], start=c == 0, stop=c == INNER // P - 1)
                last.then_inc(sem["y_done"], 1)

            def step(s, finish, front):
                pe.wait_ge(sem["qkt_copied"], s.n * 4 + 4)
                if front:
                    turn_h(s + 1)
                for h in range(LH):
                    scores(s, h)
                    if h == 0:
                        if finish:
                            turn_probs(s - 1, LH - 1)
                            weigh(s - 1, LH - 2)
                    else:
                        turn_probs(s, h - 1)
                        if h == 1 and finish:
                            weigh(s - 1, LH - 1)
                        if h >= 2:
                            weigh(s, h - 2)
                    if front and h < 3:
                        project(s + 1, h)
                    if h == 3 and finish:
                        if front:
                            pe.wait_ge(sem["v_ready"], (s + 1).n + 1)
                        turn_attn(s - 1)
                    if h == 5 and finish:
                        project_out(s - 1)
                    if front and h >= 6:
                        if h == 6:
                            if finish:
                                pe.wait_ge(sem["y_taken"], s.n)
                            pe.wait_ge(sem["v_ready"], (s + 1).n + 1)
                        turn_qk(s + 1, h - 6)

            def tail(s):
                turn_probs(s, LH - 1)
                weigh(s, LH - 2)
                weigh(s, LH - 1)
                turn_attn(s)
                project_out(s)

            pe.wait_ge(sem["w_loaded"], 16 * len(loads))
            pe.wait_ge(sem["zeroed"], 2)
            s0 = Turn(0, 0)
            turn_h(s0)
            for c in range(3):
                project(s0, c)
            pe.wait_ge(sem["v_ready"], 1)
            turn_qk(s0, 0)
            turn_qk(s0, 1)
            run_turns(pe, n_seq, step)
            tail(Turn(0, n_seq - 1))

        @block.scalar
        def _(act):
            def take_h(s):
                act.wait_ge(sem["ht_done"], s.n + 1)
                act.copy(h_t[:, :], bank[0][:, 0:S]).then_inc(sem["ht_copied"], 1)

            def take(s, c):
                if c < 2 and not (isinstance(s.n, int) and s.n == 0):
                    act.wait_ge(sem["qkt_done"], s.n * 4)
                for t in range(TILES):
                    act.wait_ge(sem["qkv_done"], s.n * 6 + (c * 2 + t + 1))
                    if c < 2:
                        act.copy(raw[c][:, t * LH:(t + 1) * LH, :],
                                 bank[t][:, :].rearrange("p (h d) -> p h d", d=LD)).then_inc(sem["raw_ready"], 1)
                    else:
                        last = act.copy(v[s.slot][:, t, :], bank[t][:, :])
                if c == 2:
                    last.then_inc(sem["v_ready"], 1)

            def square(s, c):
                act.drain()
                act.square(squares[c][:, :, :], raw[c][:, :, :]).then_inc(sem["sq_ready"], 1)

            def take_qkt(s, c):
                for t in range(TILES):
                    act.wait_ge(sem["qkt_done"], s.n * 4 + (c * 2 + t + 1))
                    act.copy(qk_t[s.slot][c][:, :, t * P:(t + 1) * P],
                             bank[t][:, :].rearrange("p (j c) -> p j c", c=P)).then_inc(sem["qkt_copied"], 1)

            def take_attn(s, t):
                act.wait_ge(sem["at_done"], s.n * 2 + (t + 1))
                act.copy(attn_t[:, :, t * P:(t + 1) * P],
                         bank[t][:, :].rearrange("p (c k) -> p c k", k=P)).then_inc(sem["at_copied"], 1)

            def exponentials(s, h):
                act.wait_ge(sem["max_ready"], s.n * LH + (h + 1))
                if not (isinstance(s.n, int) and s.n == 0 and h < 2):
                    act.wait_ge(sem["pt_done"], s.n * LH + (h - 1))
                out = probs[h % 2]
                act.activation(out[:, FIRST], ps_s[h % 2][:, 0:P], ACT.Exp, bias=neg_top[:, h % 2, 0:1],
                               accum_out=total[s.slot][:, 0, h:h + 1])
                act.activation(out[:, SECOND], ps_s[h % 2][:, P:5 * WINDOW], ACT.Exp, bias=neg_top[:, h % 2, 1:2],
                               accum_out=total[s.slot][:, 1, h:h + 1]).then_inc(sem["exp_done"], 1)

            def step(s, finish, front):
                if front:
                    take_h(s + 1)
                for h in range(LH):
                    exponentials(s, h)
                    if front and h < 3:
                        take(s + 1, h)
                        if h < 2:
                            square(s + 1, h)
                    if finish and h in (3, 4):
                        take_attn(s - 1, h - 3)
                    if front and h >= 6:
                        take_qkt(s + 1, h - 6)

            s0 = Turn(0, 0)
            take_h(s0)
            for c in range(3):
                take(s0, c)
                if c < 2:
                    square(s0, c)
            take_qkt(s0, 0)
            take_qkt(s0, 1)
            run_turns(act, n_seq, step)
            for t in range(TILES):
                take_attn(Turn(0, n_seq - 1), t)

        def by_tile(a):
            return a[:, :, :].rearrange("p (t h) d -> p t h d", t=TILES)

        def times_cos(eng, c):
            return eng.tensor_tensor(by_tile(turned[c]), by_tile(raw[c]),
                                     cos[c][:, :, :].unsqueeze(2).broadcast_to([P, TILES, LH, LD]), ALU.mult)

        @block.gpsimd
        def _(pool):
            def times_sin(c):
                half = [P, TILES, LH, LD // 2]
                x, b = by_tile(raw[c]), by_tile(swapped[c])
                for a, other in ((0, LD // 2), (LD // 2, 0)):
                    pool.tensor_tensor(b[:, :, :, a:a + LD // 2], x[:, :, :, other:other + LD // 2],
                                       sin[c][:, :, a:a + LD // 2].unsqueeze(2).broadcast_to(half), ALU.mult)

            def rotate(s, c):
                pool.wait_ge(sem["raw_ready"], s.n * 4 + (c * 2 + 2))
                times_sin(c)
                if c == 0:
                    times_cos(pool, 0)
                pool.drain()
                if c == 1:
                    pool.wait_ge(sem["k_cos_ready"], s.n + 1)
                pool.tensor_tensor(turned[c][:, :, :], turned[c][:, :, :], swapped[c][:, :, :], ALU.add)\
                    .then_inc(sem["rotated"], 1)

            def step(s, finish, front):
                if front:
                    rotate(s + 1, 0)
                    rotate(s + 1, 1)

            pool.wait_ge(sem["zeroed"], 2)
            rotate(Turn(0, 0), 0)
            rotate(Turn(0, 0), 1)
            run_turns(pool, n_seq, step)

        @block.vector
        def _(dve):
            def sums(s, c):
                dve.wait_ge(sem["sq_ready"], s.n * 2 + (c + 1))
                dve.tensor_reduce(sq_sum[:, c, :], squares[c][:, :, :], AX_X, ALU.add)

            def norms(s, part):
                if part == 0:
                    dve.drain()
                    dve.tensor_scalar(minus_half[:, :, :], sq_sum[:, :, :], 1e-24, -0.5, ALU.max, ALU.mult)
                    dve.tensor_scalar(sq_sum[:, :, :], sq_sum[:, :, :], 1e-24, None, ALU.max)
                inverse_root(dve, part, sq_sum[:, :, :], minus_half[:, :, :], guess[:, :, :], inv_norm[:, :, :])

            def turn_k(s):
                dve.wait_ge(sem["raw_ready"], s.n * 4 + 4)
                times_cos(dve, 1).then_inc(sem["k_cos_ready"], 1)

            def scale(s, c):
                dve.drain()
                dve.wait_ge(sem["rotated"], s.n * 2 + (c + 1))
                dve.tensor_tensor(raw[c][:, :, :], turned[c][:, :, :],
                                  inv_norm[:, c, :].unsqueeze(2).broadcast_to([P, TILES * LH, LD]), ALU.mult)\
                   .then_inc(sem["qk_ready"], 1)

            def maximum(s, h):
                dve.wait_ge(sem["s_done"], s.n * LH + (h + 1))
                dve.tensor_reduce(neg_top[:, h % 2, 0:1], ps_s[h % 2][:, 0:P], AX_X, ALU.max, negate=True)
                dve.tensor_reduce(neg_top[:, h % 2, 1:2], ps_s[h % 2][:, P:5 * WINDOW], AX_X, ALU.max, negate=True)\
                   .then_inc(sem["max_ready"], 1)

            def take_probs(s, h):
                dve.wait_ge(sem["pt_done"], s.n * LH + (h + 1))
                dve.tensor_copy(probs_t[h % 2][:, :], ps_p[h % 2][:, 0:3 * P]).then_inc(sem["pt_copied"], 1)

            def normalise(s):
                dve.reciprocal(inv[:, :, :], total[s.slot][:, :, :])
                dve.drain()
                dve.wait_ge(sem["o_done"], s.n * LH + LH)
                for t in range(TILES):
                    last = dve.tensor_tensor(attn[:, t, :].rearrange("p (h d) -> p h d", d=LD),
                                             ps_o[t][:, :].rearrange("p (h d) -> p h d", d=LD),
                                             inv[:, t, :].unsqueeze(2).broadcast_to([P, LH, LD]), ALU.mult)
                last.then_inc(sem["attn_ready"], 1)

            def residual(s):
                dve.wait_ge(sem["y_done"], s.n + 1)
                dve.tensor_tensor(seq(dst, s.n), bank[0][:, 0:S].rearrange("p (t d) -> p t d", t=TILES),
                                  seq(src, s.n), ALU.add).then_inc(sem["y_taken"], 1)

            def step(s, finish, front):
                for h in range(LH):
                    maximum(s, h)
                    if h == 0:
                        if finish:
                            take_probs(s - 1, LH - 1)
                    else:
                        take_probs(s, h - 1)
                    if h == 1 and finish:
                        normalise(s - 1)
                    if front:
                        if h == 1:
                            sums(s + 1, 0)
                        if h == 2:
                            turn_k(s + 1)
                            sums(s + 1, 1)
                        if h in (3, 4):
                            norms(s + 1, 2 * h - 6)
                            norms(s + 1, 2 * h - 5)
                        if h in (5, 6):
                            scale(s + 1, h - 5)
                    if finish and h == 5:
                        residual(s - 1)

            for r in range(2):
                dve.memset(shifted[r][0:1, :, D // 2:D], 0.0)
                dve.memset(probs[r][:, :], 0.0)
            dve.drain().then_inc(sem["zeroed"], 1)
            dve.wait_ge(sem["w_loaded"], 16 * len(loads))
            for c in range(2):
                q = scales[:, c, :].unsqueeze(1)
                dve.tensor_tensor(cos[c][:, :, :], cos[c][:, :, :], q.broadcast_to([P, TILES, LD]), ALU.mult)
                for a, b in ((0, LD // 2), (LD // 2, 0)):
                    dve.tensor_tensor(sin[c][:, :, a:a + LD // 2], sin[c][:, :, a:a + LD // 2],
                                      q[:, :, b:b + LD // 2].broadcast_to([P, TILES, LD // 2]), ALU.mult)
            dve.drain().then_inc(sem["zeroed"], 1)
            s0 = Turn(0, 0)
            turn_k(s0)
            sums(s0, 0)
            sums(s0, 1)
            for part in range(4):
                norms(s0, part)
            scale(s0, 0)
            scale(s0, 1)
            run_turns(dve, n_seq, step)
            take_probs(Turn(0, n_seq - 1), LH - 1)
            normalise(Turn(0, n_seq - 1))
            residual(Turn(0, n_seq - 1))



def post_ln_network(nc, x, consts, w, out):
    n_seq = x.shape[0]
    n_groups = n_seq * TILES // GROUP
    every = [P, P]
    with ExitStack() as stack:
        room = Room(nc, stack, "net")
        x_res = room.sb("x_res", [P, n_seq * TILES * D])
        x1_res = room.sb("x1_res", [P, n_seq * TILES * D])
        c = {k: room.sb(k, every) for k in ("ident", "neg_half", "ln_eps", "rms_eps", "eighth")}
        c["ident_bf"] = room.sb("ident_bf", every, BF16)
        c["mask_qk"] = room.sb("mask_qk", [P, TILES, P], BF16)
        c["mask_kq"] = room.sb("mask_kq", [P, TILES, P], BF16)
        c["pick"] = room.sb("pick", [P, HEADS // 2, P], BF16)
        c["band"] = room.sb("band", [P, 5 * WINDOW], BF16)
        c["cos"] = room.sb("cos", [P, TILES, HD])
        c["sin"] = room.sb("sin", [P, TILES, HD])
        c["tril"] = room.sb("tril", [P, 3 * P])
        gqa = {"eighth": c["eighth"]}
        mha = {}
        for k, width in (("qkv", 224), ("out", D), ("gate", D), ("ln1", 1), ("neg_bg", 1)):
            gqa[k] = room.sb(f"gqa_{k}", [D, width])
        for k, width in (("b_qkv", 224), ("bo", D), ("qk_norm", 24 * HD)):
            gqa[k] = room.sb(f"gqa_{k}", [P, width])
        for k, width in (("qkv", 384), ("out", D)):
            mha[k] = room.sb(f"mha_{k}", [D, width])
        g = w["gqa"]
        gqa["loads"] = [(gqa[k][:, :], g[k]) for k in ("qkv", "out", "ln1")]
        gqa["loads"] += [(gqa[k][:, :], g[k].broadcast_to([P, g[k].shape[1]])) for k in ("b_qkv", "bo", "qk_norm")]
        mha["loads"] = [(mha[k][:, :], w["mha"][k]) for k in ("qkv", "out")]
        for each in (gqa, mha):
            each["count"] = len(each["loads"])

        with ExitStack() as first:
            early = Room(nc, first, "setup")
            wide = {k: early.sb(k, [P, consts[k].shape[1]]) for k in ("mask_qk", "mask_kq", "pick", "band")}
            loaded, zeroed, filled = (early.sem(k) for k in ("loaded", "zeroed", "filled"))
            block = early.block()

            @block.sync
            def _(sp):
                loads = [(wide[k][:, :], consts[k]) for k in wide]
                loads += [(c["ident"][:, :], consts["ident"]), (c["tril"][:, :], consts["tril"]),
                          (c["cos"][:, :, :], consts["cos"]), (c["sin"][:, :, :], consts["sin"]),
                          (gqa["neg_bg"][:, :], g["bg"])]
                for dst, src in loads:
                    sp.dma_start(dst, src).then_inc(loaded, 16)
                sp.wait_ge(zeroed, 1)
                for h in range(HEADS):
                    at = slice(h * HD, (h + 1) * HD)
                    sp.dma_start(gqa["gate"][at, at], g["gate"]).then_inc(filled, 16)
                sp.wait_ge(filled, 16 * HEADS)

            @block.vector
            def _(dve):
                dve.memset(gqa["gate"][:, :], 0.0)
                dve.drain().then_inc(zeroed, 1)
                for k, value in (("neg_half", -0.5), ("ln_eps", LN_EPS), ("rms_eps", RMS_EPS), ("eighth", 1.0 / HD)):
                    dve.memset(c[k][:, :], value)
                dve.wait_ge(loaded, 16 * (len(wide) + 5))
                dve.tensor_copy(c["ident_bf"][:, :], c["ident"][:, :])
                for t in range(TILES):
                    dve.tensor_copy(c["mask_qk"][:, t, :], wide["mask_qk"][:, :])
                    dve.tensor_copy(c["mask_kq"][:, t, :], wide["mask_kq"][:, :])
                dve.tensor_copy(c["pick"][:, :, :], wide["pick"][:, :].rearrange("p (j k) -> p j k", k=P))
                dve.tensor_copy(c["band"][:, :], wide["band"][:, :])
                dve.tensor_scalar(gqa["neg_bg"][:, :], gqa["neg_bg"][:, :], -1.0, None, ALU.mult)

        single_head_attention(nc, x_res, x, w["sha"][0], w["sha"][1], w["sha"][2],
                              c["ident"], c["neg_half"], c["ln_eps"], c["tril"])
        many_head_attention(nc, n_seq, x_res, x1_res, c, gqa, True)
        mixture_of_experts(nc, n_groups, x_res, x1_res, c, w["moe"])
        many_head_attention(nc, n_seq, x_res, x_res, c, mha, False)
        for layer in range(2):
            windowed_attention(nc, n_seq, layer, x_res if layer == 0 else x1_res, x1_res, c, w["win"][layer])
            gated_feed_forward(nc, n_groups, layer, x1_res, c, w["ffn"][layer], first=x_res,
                               out_dram=out if layer == 1 else None)


def by_token_tile(table):
    n = table.shape[1]
    return np.ascontiguousarray(table.reshape(TILES, P, n).transpose(1, 0, 2)).astype(np.float32)


def rotation(width):
    f4 = np.float32
    inv = f4(1) / f4(10000.0) ** (np.arange(0, width, 2, dtype=f4) / f4(width))
    angle = np.arange(S, dtype=f4)[:, None] * inv[None, :]
    cos, sin = np.cos(angle), np.sin(angle)
    return np.concatenate([cos, cos], 1), np.concatenate([-sin, sin], 1)


def shape_constants():
    f4 = np.float32
    one = np.tril(np.ones((P, P), f4))
    late = np.where(one > 0, f4(0), f4(MASKED))
    pick = np.zeros((P, HEADS // 2, P), f4)
    for j in range(HEADS // 2):
        for half in (0, ROWS):
            pick[half + j, j, :] = 1
            pick[half + HEADS // 2 + j, j, :] = 1
    q = np.arange(P)[:, None]
    k0, k1 = np.arange(P)[None, :], np.arange(WINDOW, S)[None, :]
    near0 = (k0 <= q) & (k0 >= q - WINDOW)
    near1 = (k1 <= q + P) & (k1 >= q + P - WINDOW)
    cos, sin = rotation(HD)
    made = {
        "ident": np.eye(P, dtype=f4), "tril": np.concatenate([one, np.ones((P, P), f4), one], 1),
        "mask_qk": late, "mask_kq": late.T, "pick": pick.reshape(P, -1),
        "band": np.where(np.concatenate([near0, near1], 1), f4(0), f4(MASKED)),
        "cos": by_token_tile(cos), "sin": by_token_tile(sin),
        "experts": np.arange(EXPERTS, dtype=f4)[None, :],
    }
    cos, sin = rotation(LD)
    half = np.arange(0, LD, 2, dtype=f4)
    base = (half + f4(0.4 * LD)) / f4(1.4 * LD)
    power = (np.arange(S, dtype=f4) - S // 2) / f4(WINDOW // 2)
    grow = base[None, :] ** power[:, None]
    grow = np.concatenate([grow, grow], 1)
    for name, table in (("cos", cos), ("sin", sin)):
        made[f"{name}_q"] = by_token_tile(table * grow * f4(8))
        made[f"{name}_k"] = by_token_tile(table / grow)
    return made


def kernel(**inputs):
    import concourse.bacc as bacc
    from concourse.bass_utils import run_bass_kernel_spmd

    a = {k: np.asarray(v) for k, v in inputs.items()}

    def rope_halves(weights):
        return weights.reshape(HEADS, HD // 2, 2, D).transpose(0, 2, 1, 3).reshape(D, D).T

    def keys_twice(weights):
        return np.repeat(weights.reshape(-1, 4, 1, HD), 2, axis=2).reshape(weights.shape[0], -1)

    row = lambda k: a[k].reshape(1, -1)
    column = lambda k: a[k].reshape(-1, 1)
    arrays = {
        "x": a["L0_attn_x"],
        "sha_q": a["L0_attn_WQ"].T, "sha_k": a["L0_attn_WK"].T, "sha_v": a["L0_attn_WV"].T,
        "gqa_qkv": np.concatenate([a["L0_ffn_Wq"], keys_twice(a["L0_ffn_Wk"]), a["L0_ffn_Wv"]], 1),
        "gqa_b_qkv": np.concatenate([row("L0_ffn_bq"), keys_twice(row("L0_ffn_bk")), row("L0_ffn_bv")], 1),
        "gqa_qk_norm": np.concatenate([np.tile(row("L0_ffn_qn_w"), (1, HEADS)), np.tile(row("L0_ffn_kn_w"), (1, 8))], 1),
        "gqa_out": a["L0_ffn_Wo"], "gqa_bo": row("L0_ffn_bo"), "gqa_ln1": column("L0_ffn_ln1_w"),
        "gqa_gate": a["L0_ffn_Wg"], "gqa_bg": np.tile(a["L0_ffn_bg"], HEADS).reshape(-1, 1),
        "moe_W1": a["L0_ffn_W1"], "moe_W2": a["L0_ffn_W2"],
        "moe_b1": a["L0_ffn_b1"].reshape(EXPERTS, 2 * CHUNKS, P).transpose(2, 0, 1),
        "moe_b2": a["L0_ffn_b2"], "moe_Wr": a["L0_ffn_Wr"], "moe_br": row("L0_ffn_br"),
        "moe_ln2": column("L0_ffn_ln2_w"),
        "mha_qkv": np.concatenate([rope_halves(a["L1_attn_Wq"]), rope_halves(a["L1_attn_Wk"]), a["L1_attn_Wv"].T], 1),
        "mha_out": a["L1_attn_Wo"].T,
    }
    for n in range(2):
        arrays.update({
            f"win{n}_qkv": a["L1_ffn_wqkv"][n].reshape(D, 3, INNER), f"win{n}_out": a["L1_ffn_wo"][n],
            f"win{n}_scales": np.stack([a["L1_ffn_q_scale"][n], a["L1_ffn_k_scale"][n]])[None],
            f"ffn{n}_w1": a["L1_ffn_w1"][n], f"ffn{n}_w2": a["L1_ffn_w2"][n],
            f"ffn{n}_b1": a["L1_ffn_b1"][n].reshape(-1, 1), f"ffn{n}_b2": a["L1_ffn_b2"][n].reshape(1, -1),
            f"ffn{n}_ln_g": a["L1_ffn_ln_g"][n].reshape(-1, 1), f"ffn{n}_ln_b": a["L1_ffn_ln_b"][n].reshape(-1, 1),
        })
    arrays.update({f"const_{k}": v for k, v in shape_constants().items()})
    arrays = {f"in_{k}": np.ascontiguousarray(v) for k, v in arrays.items()}

    nc = bacc.Bacc("TRN2", target_bir_lowering=False, num_devices=1)
    t = {k[3:]: nc.dram_tensor(k, v.shape, mybir.dt.from_np(v.dtype), kind="ExternalInput").ap()
         for k, v in arrays.items()}
    out = nc.dram_tensor("out_0", a["L0_attn_x"].shape, F32, kind="ExternalOutput").ap()
    consts = {k[6:]: v for k, v in t.items() if k.startswith("const_")}
    weights = {
        "sha": [t["sha_q"], t["sha_k"], t["sha_v"]],
        "gqa": {k[4:]: v for k, v in t.items() if k.startswith("gqa_")},
        "mha": {k[4:]: v for k, v in t.items() if k.startswith("mha_")},
        "moe": {
            "W1": t["moe_W1"].rearrange("e d f -> d e f"), "b1": t["moe_b1"], "b2": t["moe_b2"],
            "W2": t["moe_W2"].rearrange("e (c p) d -> p e c d", p=P), "Wr": t["moe_Wr"],
            "br": t["moe_br"].broadcast_to([P, EXPERTS]), "ln2": t["moe_ln2"],
            "experts": consts["experts"].broadcast_to([P, EXPERTS]),
        },
        "win": [{
            "qkv": t[f"win{n}_qkv"], "out": t[f"win{n}_out"].rearrange("(c p) d -> p c d", p=P),
            "scales": t[f"win{n}_scales"].broadcast_to([P, 2, LD]),
            "cos": [consts["cos_q"], consts["cos_k"]], "sin": [consts["sin_q"], consts["sin_k"]],
        } for n in range(2)],
        "ffn": [{
            "w1": t[f"ffn{n}_w1"], "w2": t[f"ffn{n}_w2"], "b1": t[f"ffn{n}_b1"],
            "b2": t[f"ffn{n}_b2"].broadcast_to([P, D]), "ln_g": t[f"ffn{n}_ln_g"], "ln_b": t[f"ffn{n}_ln_b"],
        } for n in range(2)],
    }
    post_ln_network(nc, t["x"], consts, weights, out)
    result = run_bass_kernel_spmd(nc, [arrays], core_ids=[0])
    return result.results[0]["out_0"]
```

```python
from contextlib import ExitStack

import numpy as np
import concourse.bass as bass
from concourse import mybir

F32 = mybir.dt.float32
BF16 = mybir.dt.bfloat16
U32 = mybir.dt.uint32
I32 = mybir.dt.int32
ALU = mybir.AluOpType
ACT = mybir.ActivationFunctionType
AX_X = mybir.AxisListType.X

P = 128
D = 128
S = 256
TILES = S // P
LN_EPS = 1e-5
RMS_EPS = 1e-6
MASKED = -1e30


class Room:

    def __init__(self, nc, stack, stage):
        self.nc, self.stack, self.stage, self.sems = nc, stack, stage, []

    def sb(self, name, shape, dt=F32):
        return self.stack.enter_context(self.nc.sbuf_tensor(f"{self.stage}_{name}", shape, dt))

    def psum(self, name, shape, dt=F32):
        return self.stack.enter_context(self.nc.psum_tensor(f"{self.stage}_{name}", shape, dt))

    def sem(self, name):
        made = self.stack.enter_context(self.nc.semaphore(f"{self.stage}_{name}"))
        self.sems.append(made)
        return made

    def block(self):
        self.stack.callback(self.clear)
        return self.stack.enter_context(self.nc.Block())

    def clear(self):
        numbers = sorted(s.num for s in self.sems)
        starts = [a for a in numbers if a - 1 not in numbers]
        ends = [a + 1 for a in numbers if a + 1 not in numbers]
        with self.nc.Block() as block:
            @block.gpsimd
            def _(pool):
                for start, end in zip(starts, ends):
                    pool.sem_clear(range(start, end))


def inverse_root(dve, part, x, minus_half_x, guess, out):
    dve.drain()
    if part == 0:
        return dve.tensor_scalar(guess.bitcast(I32), x.bitcast(I32), -0.5, float(0x5F3759DF), ALU.mult, ALU.add)
    dve.tensor_tensor(x, guess, guess, ALU.mult)
    dve.drain()
    dve.tensor_tensor(x, x, minus_half_x, ALU.mult)
    dve.drain()
    return dve.scalar_tensor_tensor(out if part == 3 else guess, x, 1.5, guess, ALU.add, ALU.mult)


class Ahead:

    def __init__(self, room, loads):
        self.loads, self.loaded = loads, room.sem("ahead_loaded")

    def start(self, sp):
        for dst, src in self.loads:
            sp.dma_start(dst, src).then_inc(self.loaded, 16)

    def wait(self, sp):
        if self.loads:
            sp.wait_ge(self.loaded, 16 * len(self.loads))


def seq(x_res, n):
    return x_res[:, bass.ds(n * (TILES * D), TILES * D)].rearrange("p (t d) -> p t d", t=TILES)


def tile(x_res, n, t):
    return x_res[:, bass.ds(n * (TILES * D) + t * D, D)]


class Step:

    def __init__(self, third, offset):
        self.third, self.offset = third, offset
        self.n = third * 3 + offset
        self.slot = offset % 3
        self.turn = third + offset // 3

    def __add__(self, k):
        return Step(self.third, self.offset + k)

    def __sub__(self, k):
        return Step(self.third, self.offset - k)


def run_steps(eng, n_seq, step):
    step(Step(0, 0), True, False, False, True)
    step(Step(0, 1), True, True, False, True)
    step(Step(0, 2), True, True, True, True)
    assert (n_seq - 5) % 3 == 0
    with eng.Fori(0, (n_seq - 5) // 3) as i:
        for c in range(3):
            step(Step(i, 3 + c), True, True, True, True)
    step(Step(0, n_seq - 2), True, True, True, True)
    step(Step(0, n_seq - 1), True, True, True, False)
    step(Step(0, n_seq), False, True, True, False)
    step(Step(0, n_seq + 1), False, False, True, False)


def single_head_attention(nc, x_res, x_dram, wq_t, wk_t, wv_t, ident, neg_half, ln_eps, tril, ahead=()):
    n_seq = x_dram.shape[0]
    x_tiles = x_dram.rearrange("b (t p) d -> b p t d", p=P)
    scale = float(D) ** -0.5
    with ExitStack() as stack:
        room = Room(nc, stack, "sha")
        w = room.sb("w", [D, 3, D])
        x_in = [room.sb(f"x_in{r}", [P, TILES, D]) for r in range(3)]
        x_t = room.sb("x_t", [D, S])
        qk_t = room.sb("qk_t", [D, 2, S])
        v = [room.sb(f"v{r}", [P, TILES, D]) for r in range(3)]
        scores = [room.sb(f"scores{r}", [P, 3 * P]) for r in range(3)]
        dead = room.sb("dead", [P, 3 * P])
        probs = [room.sb(f"probs{r}", [P, 3 * P]) for r in range(3)]
        probs_t = room.sb("probs_t", [P, 3 * P])
        top = room.sb("top", [P, TILES])
        bias = [room.sb(f"bias{r}", [P, TILES]) for r in range(3)]
        total = [room.sb(f"total{r}", [P, TILES]) for r in range(3)]
        inv = room.sb("inv", [P, TILES])
        y = room.sb("y", [P, TILES, D])
        stats = room.sb("stats", [P, TILES, 6])
        mean_var = room.sb("mean_var", [P, TILES, 2])
        var_eps = room.sb("var_eps", [P, TILES])
        rstd = room.sb("rstd", [P, TILES])
        ps_a = [room.psum(f"ps_a{r}", [P, 512]) for r in range(3)]
        ps_p = [room.psum(f"ps_p{r}", [P, 512]) for r in range(3)]
        ps_qk = room.psum("ps_qk", [P, 2, S])
        ps_v = room.psum("ps_v", [P, TILES, D])
        names = ("w_loaded xt_done xt_copied qk_done qk_copied v_done v_copied scores_done bias_ready "
                 "probs_ready pt_done pt_copied out_done var_ready rstd_ready")
        sem = {k: room.sem(k) for k in names.split()}
        x_loaded = [room.sem(f"x_loaded{r}") for r in range(3)]
        row = [slice(0, P), slice(P, 3 * P)]
        next_weights = Ahead(room, ahead)
        block = room.block()

        @block.sync
        def _(sp):
            def load(s):
                src = x_tiles[bass.ds(s.n, 1)].rearrange("b p t d -> (b p) t d")
                sp.dma_start(x_in[s.slot][:, :, :], src).then_inc(x_loaded[s.slot], 16)
                sp.dma_start(seq(x_res, s.n), src).then_inc(x_loaded[s.slot], 16)

            load(Step(0, 0))
            for c, src in enumerate((wq_t, wk_t, wv_t)):
                sp.dma_start(w[:, c, :], src).then_inc(sem["w_loaded"], 16)
            load(Step(0, 1))
            load(Step(0, 2))
            next_weights.start(sp)
            with sp.Fori(0, (n_seq - 5) // 3) as i:
                for c in range(3):
                    s = Step(i, 3 + c)
                    sp.wait_ge(sem["xt_done"], (s - 2).n)
                    load(s)
            for n in range(n_seq - 2, n_seq):
                sp.wait_ge(sem["xt_done"], n - 2)
                load(Step(0, n))
            next_weights.wait(sp)

        @block.tensor
        def _(pe):
            def turn_x(s):
                pe.wait_ge(x_loaded[s.slot], s.turn * 32 + 32)
                for t in range(TILES):
                    last = pe.transpose(ps_a[s.slot][:, t * P:(t + 1) * P], x_in[s.slot][:, t, :], ident[:, :])
                last.then_inc(sem["xt_done"], 1)

            def project(s):
                pe.wait_ge(sem["xt_copied"], s.n + 1)
                for c in range(2):
                    last = pe.matmul(ps_qk[:, c, :], w[:, c, :], x_t[:, :], start=True, stop=True)
                last.then_inc(sem["qk_done"], 1)
                if not (isinstance(s.n, int) and s.n == 0):
                    pe.wait_ge(sem["v_copied"], s.n)
                for t in range(TILES):
                    last = pe.matmul(ps_v[:, t, :], x_t[:, t * P:(t + 1) * P], w[:, 2, :], start=True, stop=True)
                last.then_inc(sem["v_done"], 1)

            def score(s):
                pe.wait_ge(sem["qk_copied"], s.n + 1)
                out = ps_a[s.slot]
                pe.matmul(out[:, row[0]], qk_t[:, 0, 0:P], qk_t[:, 1, 0:P], start=True, stop=True)
                pe.matmul(out[:, row[1]], qk_t[:, 0, P:S], qk_t[:, 1, :], start=True, stop=True)\
                  .then_inc(sem["scores_done"], 1)

            def turn_probs(s):
                pe.wait_ge(sem["probs_ready"], s.n + 1)
                for b in range(3):
                    last = pe.transpose(ps_p[s.slot][:, b * P:(b + 1) * P], probs[s.slot][:, b * P:(b + 1) * P],
                                        ident[:, :])
                last.then_inc(sem["pt_done"], 1)

            def weigh(s):
                pe.wait_ge(sem["pt_copied"], s.n + 1)
                out = ps_p[s.slot]
                pe.matmul(out[:, 0:D], probs_t[:, 0:P], v[s.slot][:, 0, :], start=True, stop=True)
                for t in range(TILES):
                    last = pe.matmul(out[:, D:2 * D], probs_t[:, (1 + t) * P:(2 + t) * P], v[s.slot][:, t, :],
                                     start=t == 0, stop=t == 1)
                last.then_inc(sem["out_done"], 1)

            def step(s, project_s, attend, finish, more):
                if project_s:
                    turn_x(s)
                if finish:
                    turn_probs(s - 2)
                if project_s:
                    project(s)
                if finish:
                    weigh(s - 2)
                if project_s:
                    score(s)

            pe.wait_ge(sem["w_loaded"], 48)
            run_steps(pe, n_seq, step)

        @block.scalar
        def _(act):
            def step(s, project_s, attend, finish, more):
                if project_s:
                    act.wait_ge(sem["xt_done"], s.n + 1)
                    act.copy(x_t[:, :], ps_a[s.slot][:, 0:S]).then_inc(sem["xt_copied"], 1)
                if finish:
                    act.wait_ge(sem["pt_done"], (s - 1).n)
                    act.copy(probs_t[:, :], ps_p[(s - 2).slot][:, 0:3 * P]).then_inc(sem["pt_copied"], 1)
                if project_s:
                    act.wait_ge(sem["qk_done"], s.n + 1)
                    act.copy(qk_t[:, :, :], ps_qk[:, :, :]).then_inc(sem["qk_copied"], 1)
                    act.wait_ge(sem["v_done"], s.n + 1)
                    act.copy(v[s.slot][:, :, :], ps_v[:, :, :]).then_inc(sem["v_copied"], 1)
                if attend:
                    r = (s - 1).slot
                    act.wait_ge(sem["bias_ready"], s.n)
                    for t in range(TILES):
                        last = act.activation(probs[r][:, row[t]], scores[r][:, row[t]], ACT.Exp,
                                              bias=bias[r][:, t:t + 1], scale=scale, accum_out=total[r][:, t:t + 1])
                    last.then_inc(sem["probs_ready"], 1)

            run_steps(act, n_seq, step)

        @block.gpsimd
        def _(pool):
            def step(s, project_s, attend, finish, more):
                if finish:
                    pool.wait_ge(sem["var_ready"], (s - 1).n)
                    pool.tensor_tensor(var_eps[:, :], mean_var[:, :, 1], ln_eps[:, 0:TILES], ALU.add)
                    pool.drain()
                    pool.tensor_tensor(rstd[:, :], var_eps[:, :], neg_half[:, 0:TILES], ALU.pow)\
                        .then_inc(sem["rstd_ready"], 1)

            run_steps(pool, n_seq, step)

        @block.vector
        def _(dve):
            def invert_total(s):
                dve.wait_ge(sem["probs_ready"], s.n + 1)
                dve.reciprocal(inv[:, :], total[s.slot][:, :])

            def residual(s):
                dve.drain()
                dve.wait_ge(sem["out_done"], s.n + 1)
                for t in range(TILES):
                    dve.scalar_tensor_tensor(y[:, t, :], ps_p[s.slot][:, t * D:(t + 1) * D], inv[:, t:t + 1],
                                             tile(x_res, s.n, t), ALU.mult, ALU.add)
                dve.drain()
                for t in range(TILES):
                    dve.bn_stats(stats[:, t, :], y[:, t, :])
                dve.drain()
                for t in range(TILES):
                    last = dve.bn_aggr(mean_var[:, t, :], stats[:, t, :])
                last.then_inc(sem["var_ready"], 1)

            def layer_norm(s):
                dve.wait_ge(sem["rstd_ready"], s.n + 1)
                for t in range(TILES):
                    dve.tensor_scalar(tile(x_res, s.n, t), y[:, t, :], mean_var[:, t, 0:1], rstd[:, t:t + 1],
                                      ALU.subtract, ALU.mult)

            def step(s, project_s, attend, finish, more):
                r = (s - 1).slot
                dve.drain()
                if attend:
                    dve.wait_ge(sem["scores_done"], s.n)
                    dve.tensor_tensor(scores[r][:, :], ps_a[r][:, 0:3 * P], tril[:, :], ALU.mult)
                if finish:
                    invert_total(s - 2)
                if attend:
                    dve.drain()
                    dve.tensor_scalar(dead[:, :], scores[r][:, :], 0.0, MASKED, ALU.is_equal, ALU.mult)
                if finish and not (isinstance(s.n, int) and s.n == 2):
                    layer_norm(s - 3)
                if attend:
                    dve.drain()
                    for t in range(TILES):
                        dve.tensor_tensor_reduce(scores[r][:, row[t]], scores[r][:, row[t]], dead[:, row[t]],
                                                 1.0, -3e38, ALU.add, ALU.max, top[:, t:t + 1])
                    dve.drain()
                    dve.tensor_scalar(bias[r][:, :], top[:, :], -scale, None, ALU.mult)\
                        .then_inc(sem["bias_ready"], 1)
                if finish:
                    residual(s - 2)

            run_steps(dve, n_seq, step)
            dve.drain()
            layer_norm(Step(0, n_seq - 1))




HEADS = 16
HD = 8
ROWS = 64
QUADS = HEADS // 4


def many_head_attention(nc, n_seq, x_res, out_res, consts, w, gated, ahead=()):
    ident, ident_bf, neg_half, eps_ln, eps_rms = (consts[k] for k in ("ident", "ident_bf", "neg_half", "ln_eps", "rms_eps"))
    NK = 8 if gated else 16
    NV = 4 if gated else 16
    NQK = HEADS + NK
    W = NQK * HD + NV * HD
    scale = float(HD) ** -0.5
    with ExitStack() as stack:
        room = Room(nc, stack, "gqa" if gated else "mha")
        x_in = [room.sb(f"x_in{r}", [P, TILES, D]) for r in range(3)]
        x_t = [room.sb(f"x_t{r}", [D, S]) for r in range(3)]
        qk = room.sb("qk", [P, TILES * NQK, HD])
        turned = room.sb("turned", [P, TILES * NQK, HD])
        swapped = room.sb("swapped", [P, TILES * NQK, HD])
        squares = room.sb("squares", [P, TILES * NQK, HD])
        rope_cos = room.sb("rope_cos", [P, TILES * NQK, HD])
        rope_sin = room.sb("rope_sin", [P, TILES * NQK, HD])
        sq_sum = room.sb("sq_sum", [P, TILES * NQK])
        mean_eps = room.sb("mean_eps", [P, TILES * NQK])
        minus_half = room.sb("minus_half", [P, TILES * NQK])
        guess = room.sb("guess", [P, TILES * NQK])
        head_rms = room.sb("head_rms", [P, TILES * NQK])
        rest_q = room.sb("rest_q", [P, TILES * HEADS, HD])
        rest_k = room.sb("rest_k", [P, TILES * NK, HD])
        q_rows = room.sb("q_rows", [P, TILES * HEADS, ROWS], BF16)
        k_rows = room.sb("k_rows", [P, TILES * NK, ROWS], BF16)
        q_t = [room.sb(f"q_t{r}", [P, HEADS // 2, S], BF16) for r in range(3)]
        k_t = [room.sb(f"k_t{r}", [P, NK // 2, S], BF16) for r in range(3)]
        v_ext = [room.sb(f"v_ext{r}", [P, TILES, NV, 32]) for r in range(3)]
        neg_top = room.sb("neg_top", [P, TILES, HEADS])
        m_rows = room.sb("m_rows", [P, TILES, P], BF16)
        m_t = [room.sb(f"m_t{r}", [P, S], BF16) for r in range(3)]
        probs = room.sb("probs", [P, 8, 2 * S])
        o_t = room.sb("o_t", [P, QUADS, S])
        inv = room.sb("inv", [P, TILES, HEADS])
        attn = room.sb("attn", [P, TILES, D])
        attn_t = room.sb("attn_t", [D, S])
        gate_t = room.sb("gate_t", [D, S])
        x_ms = room.sb("x_ms", [P, TILES])
        x_ms_eps = room.sb("x_ms_eps", [P, TILES])
        x_rms = room.sb("x_rms", [P, TILES])
        sq = room.sb("sq", [P, D])
        y = room.sb("y", [P, TILES, D])
        stats = room.sb("stats", [P, TILES, 6])
        mean_var = room.sb("mean_var", [P, TILES, 2])
        rstd = room.sb("rstd", [P, TILES])
        ps_s = [room.psum(f"ps_s{r}", [P, 2 * S]) for r in range(2)]
        ps_st = [room.psum(f"ps_st{r}", [P, 2 * S]) for r in range(2)]
        ps_pv = room.psum("ps_pv", [P, QUADS, S])
        front = [room.psum(f"front{r}", [P, 512]) for r in range(2)]
        front_bf = [f[:, :].bitcast(BF16) for f in front]

        names = ("xt_done xt_copied x_ms_ready x_rms_ready qkv_done qkv_taken squared head_rms_ready "
                 "q_high_ready k_high_ready q_rest_ready k_rest_ready q_mid_ready k_mid_ready q_low_ready k_low_ready "
                 "cos_ready turned_ready q_top_ready k_top_ready qt_done qt_copied kt_done kt_copied s_done max_done "
                 "m_rows_ready mt_done mt_copied st_done exp_done pv_done ot_copied ot_done attn_ready at_done "
                 "at_copied z_done z_tanh_ready gated_ready y_done y_taken var_ready rstd_ready bias_added zeroed")
        sem = {k: room.sem(k) for k in names.split()}
        x_loaded = [room.sem(f"x_loaded{r}") for r in range(3)]
        next_weights = Ahead(room, ahead)
        block = room.block()

        def kgroup(h):
            return (h // 2) * NK // HEADS

        def vhead(h):
            return h * NV // HEADS

        def piece(rows, place):
            return rows[:, :, place * HD:(place + 1) * HD]

        def by_tile(a):
            return a.rearrange("p (t h) d -> p t h d", t=TILES)

        def turned_heads(rows):
            whole = by_tile(turned[:, :, :])
            return whole[:, :, 0:HEADS, :] if rows is q_rows else whole[:, :, HEADS:NQK, :]

        def copy_high(eng_copy, rows, place):
            return eng_copy(by_tile(piece(rows, place)), turned_heads(rows))

        @block.sync
        def _(sp):
            def load(s):
                sp.dma_start(x_in[s.slot][:, :, :], seq(x_res, s.n)).then_inc(x_loaded[s.slot], 16)

            for n in range(3):
                load(Step(0, n))
            next_weights.start(sp)
            with sp.Fori(0, (n_seq - 5) // 3) as i:
                for c in range(3):
                    s = Step(i, 3 + c)
                    sp.wait_ge(sem["xt_done"], (s - 2).n)
                    if gated:
                        sp.wait_ge(sem["x_ms_ready"], (s - 2).n)
                    load(s)
            for n in range(n_seq - 2, n_seq):
                sp.wait_ge(sem["xt_done"], n - 2)
                if gated:
                    sp.wait_ge(sem["x_ms_ready"], n - 2)
                load(Step(0, n))
            next_weights.wait(sp)

        @block.tensor
        def _(pe):
            def turn_x(s):
                pe.wait_ge(x_loaded[s.slot], s.turn * 16 + 16)
                for t in range(TILES):
                    last = pe.transpose(front[1][:, t * P:(t + 1) * P], x_in[s.slot][:, t, :], ident[:, :])
                last.then_inc(sem["xt_done"], 1)

            def project_qkv(s):
                pe.wait_ge(sem["xt_copied"], s.n + 1)
                for t in range(TILES):
                    pe.matmul(front[t][:, 0:W], x_t[s.slot][:, t * P:(t + 1) * P], w["qkv"][:, 0:W],
                              start=True, stop=True).then_inc(sem["qkv_done"], 1)

            def turn_rows(s, t, rows):
                is_q = rows is q_rows
                heads, kind = (HEADS, "q") if is_q else (NK, "k")
                if t == 0:
                    for made in ("high", "mid", "low"):
                        pe.wait_ge(sem[f"{kind}_{made}_ready"], s.n + 1)
                if not is_q:
                    pe.wait_ge(sem["qt_copied"], s.n * 2 + (t + 1))
                for j in range(heads // 2):
                    last = pe.transpose(front_bf[t][:, j * P:(j + 1) * P],
                                        rows[:, t * heads + 2 * j:t * heads + 2 * j + 2, :], ident_bf[:, :])
                last.then_inc(sem[f"{kind}t_done"], 1)

            def turn_m(s):
                pe.wait_ge(sem["m_rows_ready"], s.n + 1)
                for t in range(TILES):
                    last = pe.transpose(front_bf[0][:, t * P:(t + 1) * P], m_rows[:, t, :], ident_bf[:, :])
                last.then_inc(sem["mt_done"], 1)

            def scores(s, h):
                half = slice(ROWS * (h % 2), ROWS * (h % 2) + ROWS)
                q, k, out = q_t[s.slot][half, h // 2, :], k_t[s.slot][half, kgroup(h), :], ps_s[h % 2]
                if gated:
                    pe.matmul(out[:, 0:P], q[:, 0:P], k[:, 0:P], start=True, stop=False)
                    pe.matmul(out[:, P:3 * P], q[:, P:S], k[:, :], start=False, stop=False)
                    diagonal = out[:, :].rearrange("p (b c) -> p b c", c=S)[:, :, 0:P]
                    last = pe.matmul(diagonal, ident_bf[:, :], consts["mask_qk"][:, :, :], start=False, stop=True)
                else:
                    pe.matmul(out[:, 0:S], q[:, 0:P], k[:, :], start=True, stop=True)
                    last = pe.matmul(out[:, S:2 * S], q[:, P:S], k[:, :], start=True, stop=True)
                last.then_inc(sem["s_done"], 1)

            def scores_t(s, h):
                half = slice(ROWS * (h % 2), ROWS * (h % 2) + ROWS)
                q, k, out = q_t[s.slot][half, h // 2, :], k_t[s.slot][half, kgroup(h), :], ps_st[h % 2]
                pick, m = consts["pick"][half, h // 2, :], m_t[s.slot][half, :]
                pe.matmul(out[:, 0:S], pick, m, start=True, stop=False)
                if gated:
                    pe.matmul(out[:, S:3 * P], pick, m[:, P:S], start=False, stop=False)
                    pe.matmul(out[:, 0:S], k[:, 0:P], q, start=False, stop=False)
                    pe.matmul(out[:, S:3 * P], k[:, P:S], q[:, P:S], start=False, stop=False)
                    diagonal = out[:, :].rearrange("p (b c) -> p b c", c=S)[:, :, 0:P]
                    last = pe.matmul(diagonal, ident_bf[:, :], consts["mask_kq"][:, :, :], start=False, stop=True)
                else:
                    pe.matmul(out[:, S:2 * S], pick, m, start=False, stop=False)
                    pe.matmul(out[:, 0:S], k[:, 0:P], q, start=False, stop=False)
                    last = pe.matmul(out[:, S:2 * S], k[:, P:S], q, start=False, stop=True)
                last.then_inc(sem["st_done"], 1)

            def weigh_values(s, g):
                pe.wait_ge(sem["exp_done"], s.n * HEADS + 4 * (g + 1))
                for t in range(TILES):
                    for c in range(4):
                        h = 4 * g + c
                        slot = probs[:, h % 8, :]
                        if t == 0:
                            out, p = ps_pv[32 * c:32 * c + 32, g, :], slot[:, 0:S]
                        elif gated:
                            out, p = ps_pv[32 * c:32 * c + 32, g, P:S], slot[:, S:3 * P]
                        else:
                            out, p = ps_pv[32 * c:32 * c + 32, g, :], slot[:, S:2 * S]
                        last = pe.matmul(out, v_ext[s.slot][:, t, vhead(h), :], p, start=t == 0, stop=t == 1)
                last.then_inc(sem["pv_done"], 1)

            def turn_outputs(s, has_front):
                pe.wait_ge(sem["ot_copied"], s.n + 1)
                if has_front:
                    pe.wait_ge(sem["qkv_taken"], s.n + 4)
                else:
                    pe.wait_ge(sem["y_taken"], s.n)
                for t in range(TILES):
                    for g in range(QUADS):
                        last = pe.transpose(front[t][:, g * P:(g + 1) * P], o_t[:, g, t * P:(t + 1) * P], ident[:, :])
                last.then_inc(sem["ot_done"], 1)

            def turn_attn(s):
                pe.wait_ge(sem["attn_ready"], s.n + 1)
                for t in range(TILES):
                    last = pe.transpose(front[0][:, t * P:(t + 1) * P], attn[:, t, :], ident[:, :])
                last.then_inc(sem["at_done"], 1)

            def gate_logits(s):
                pe.wait_ge(sem["at_copied"], s.n + 1)
                pe.matmul(front[1][:, 0:S], w["gate"][:, :], attn_t[:, :], start=True, stop=True)\
                  .then_inc(sem["z_done"], 1)

            def project_out(s):
                pe.wait_ge(sem["gated_ready" if gated else "at_copied"], s.n + 1)
                for t in range(TILES):
                    last = pe.matmul(front[0][:, t * D:(t + 1) * D], attn_t[:, t * P:(t + 1) * P], w["out"][:, :],
                                     start=True, stop=True)
                last.then_inc(sem["y_done"], 1)

            def begin(s, slot, after_attend, after_finish):
                if slot == 0:
                    turn_x(s)
                if slot == 1:
                    if after_attend:
                        pe.wait_ge(sem["mt_copied"], (s - 1).n)
                    project_qkv(s)
                if slot == 11:
                    if after_finish:
                        pe.wait_ge(sem["y_taken"], (s - 2).n)
                        if gated:
                            pe.wait_ge(sem["z_tanh_ready"], (s - 2).n)
                    turn_rows(s, 0, q_rows)
                    turn_rows(s, 1, q_rows)
                if slot == 12:
                    turn_rows(s, 0, k_rows)
                if slot == 13:
                    turn_rows(s, 1, k_rows)

            def scores_of(s, h):
                if not (isinstance(s.n, int) and s.n == 0 and h < 2):
                    pe.wait_ge(sem["max_done"], s.n * HEADS + (h - 1))
                scores(s, h)

            def step(s, do_scores, attend, finish, do_front):
                for h in range(HEADS):
                    if do_scores and h != 1:
                        if h == 0:
                            pe.wait_ge(sem["kt_copied"], s.n * 2 + 2)
                        scores_of(s, h)
                    if h == 0:
                        if do_front:
                            begin(s + 1, 0, attend, finish)
                        if finish:
                            weigh_values(s - 2, 3)
                        if attend:
                            if not do_scores:
                                pe.wait_ge(sem["y_taken"], (s - 2).n)
                            turn_m(s - 1)
                        if do_scores:
                            scores_of(s, 1)
                        if attend:
                            pe.wait_ge(sem["mt_copied"], s.n)
                    if attend:
                        if not (isinstance(s.n, int) and s.n == 1 and h < 2):
                            pe.wait_ge(sem["exp_done"], (s - 1).n * HEADS + (h - 1))
                        scores_t(s - 1, h)
                    if attend and h in (5, 9, 13):
                        if h == 5 and finish:
                            pe.wait_ge(sem["ot_copied"], (s - 1).n)
                        weigh_values(s - 1, (h - 5) // 4)
                    if finish:
                        if h == 3:
                            turn_outputs(s - 2, do_front)
                        if h == 5:
                            turn_attn(s - 2)
                        if h == 6 and gated:
                            gate_logits(s - 2)
                        if h == 9:
                            project_out(s - 2)
                    if do_front and h > 0:
                        begin(s + 1, h, attend, finish)

            pe.wait_ge(sem["zeroed"], 1)
            for slot in range(HEADS):
                begin(Step(0, 0), slot, False, False)
            run_steps(pe, n_seq, step)

        @block.scalar
        def _(act):
            def take_x(s):
                act.wait_ge(sem["xt_done"], s.n + 1)
                if gated:
                    ins = act.activation(x_t[s.slot][:, :], front[1][:, 0:S], ACT.Copy, scale=w["ln1"][:, 0:1])
                else:
                    ins = act.copy(x_t[s.slot][:, :], front[1][:, 0:S])
                ins.then_inc(sem["xt_copied"], 1)

            def take_queries(s, t):
                act.wait_ge(sem["qt_done"], s.n * 2 + (t + 1))
                act.copy(q_t[s.slot][:, :, t * P:(t + 1) * P],
                         front_bf[t][:, 0:HEADS // 2 * P].rearrange("p (j c) -> p j c", c=P))\
                   .then_inc(sem["qt_copied"], 1)

            def take_m(s):
                act.wait_ge(sem["mt_done"], s.n + 1)
                act.copy(m_t[s.slot][:, :], front_bf[0][:, 0:S]).then_inc(sem["mt_copied"], 1)

            def copy_highs(s, rows, places, done):
                act.wait_ge(sem["turned_ready"], s.n + 1)
                for place in places:
                    last = copy_high(act.copy, rows, place)
                    if place == 0:
                        last.then_inc(sem["q_top_ready"], 1)
                last.then_inc(sem[done], 1)

            def begin(s, slot):
                if slot == 0:
                    take_x(s)
                if slot == 2 and gated:
                    act.wait_ge(sem["qkv_taken"], s.n + 1)
                    act.square(squares[:, :, :], qk[:, :, :]).then_inc(sem["squared"], 1)
                if slot == 8:
                    copy_highs(s, q_rows, (0, 1, 2), "q_high_ready")
                if slot == 9:
                    copy_highs(s, k_rows, (3, 4), "k_high_ready")
                if slot == 11:
                    take_queries(s, 0)
                if slot == 12:
                    take_queries(s, 1)

            def take_outputs(s):
                act.wait_ge(sem["pv_done"], s.n * QUADS + QUADS)
                for g in range(0, QUADS, 2):
                    last = act.copy(o_t[:, g:g + 2, :], ps_pv[:, g:g + 2, :])
                last.then_inc(sem["ot_copied"], 1)

            def take_attn(s):
                act.wait_ge(sem["at_done"], s.n + 1)
                act.copy(attn_t[:, :], front[0][:, 0:S]).then_inc(sem["at_copied"], 1)

            def gate_tanh(s):
                act.wait_ge(sem["z_done"], s.n + 1)
                act.activation(gate_t[:, :], front[1][:, 0:S], ACT.Tanh, bias=w["half_bg"][:, 0:1], scale=0.5)\
                   .then_inc(sem["z_tanh_ready"], 1)

            def step(s, do_scores, attend, finish, do_front):
                if do_front:
                    begin(s + 1, 0)
                if attend:
                    take_m(s - 1)
                for h in range(HEADS):
                    if attend:
                        a = s - 1
                        act.wait_ge(sem["st_done"], a.n * HEADS + (h + 1))
                        if not (isinstance(s.n, int) and s.n == 1 and h < 8):
                            act.wait_ge(sem["pv_done"], a.n * QUADS + (h // 4 - 1))
                        n_cols = 3 * P if gated else 4 * P
                        act.activation(probs[:, h % 8, 0:n_cols], ps_st[h % 2][:, 0:n_cols], ACT.Exp, scale=scale)\
                           .then_inc(sem["exp_done"], 1)
                    if finish:
                        if h == 0:
                            take_outputs(s - 2)
                        if h == 5:
                            take_attn(s - 2)
                        if h == 6 and gated:
                            gate_tanh(s - 2)
                    if do_front and h > 0:
                        begin(s + 1, h)

            for slot in range(HEADS):
                begin(Step(0, 0), slot)
            run_steps(act, n_seq, step)

        @block.gpsimd
        def _(pool):
            def x_norm(s):
                pool.wait_ge(sem["x_ms_ready"], s.n + 1)
                pool.tensor_tensor(x_ms_eps[:, :], x_ms[:, :], eps_rms[:, 0:TILES], ALU.add)
                pool.drain()
                pool.tensor_tensor(x_rms[:, :], x_ms_eps[:, :], neg_half[:, 0:TILES], ALU.pow)\
                    .then_inc(sem["x_rms_ready"], 1)

            def rotate(s):
                x, b = qk[:, :, :], swapped[:, :, :]
                if gated:
                    pool.tensor_tensor(turned[:, :, :], x, rope_cos[:, :, :], ALU.mult)
                pool.tensor_tensor(b[:, :, 0:4], x[:, :, 4:8], rope_sin[:, :, 0:4], ALU.mult)
                pool.tensor_tensor(b[:, :, 4:8], x[:, :, 0:4], rope_sin[:, :, 4:8], ALU.mult)
                pool.drain()
                if not gated:
                    pool.wait_ge(sem["cos_ready"], s.n + 1)
                last = pool.tensor_tensor(turned[:, :, :], turned[:, :, :], b, ALU.add)
                if gated:
                    pool.drain()
                    pool.wait_ge(sem["head_rms_ready"], s.n + 1)
                    last = pool.tensor_tensor(turned[:, :, :], turned[:, :, :],
                                              head_rms[:, :].unsqueeze(2).broadcast_to([P, TILES * NQK, HD]), ALU.mult)
                last.then_inc(sem["turned_ready"], 1)
                pool.drain()

            def split_queries(s):
                pool.wait_ge(sem["q_top_ready"], s.n + 1)
                pool.tensor_tensor(by_tile(rest_q[:, :, :]), turned_heads(q_rows), by_tile(piece(q_rows, 0)),
                                   ALU.subtract).then_inc(sem["q_rest_ready"], 1)
                pool.drain()
                pool.tensor_copy(piece(q_rows, 3), rest_q[:, :, :])
                pool.drain()
                pool.tensor_tensor(piece(q_rows, 4), rest_q[:, :, :], piece(q_rows, 3), ALU.subtract)\
                    .then_inc(sem["q_low_ready"], 1)

            def split_keys(s):
                pool.wait_ge(sem["k_top_ready"], s.n + 1)
                pool.tensor_tensor(by_tile(rest_k[:, :, :]), turned_heads(k_rows), by_tile(piece(k_rows, 0)),
                                   ALU.subtract).then_inc(sem["k_rest_ready"], 1)
                pool.wait_ge(sem["k_mid_ready"], s.n + 1)
                pool.tensor_tensor(piece(k_rows, 2), rest_k[:, :, :], piece(k_rows, 1), ALU.subtract)\
                    .then_inc(sem["k_low_ready"], 1)

            def begin(s):
                if gated:
                    x_norm(s)
                pool.wait_ge(sem["qkv_taken"], s.n + 1)
                rotate(s)
                split_queries(s)
                split_keys(s)

            def layer_norm(s):
                pool.wait_ge(sem["var_ready"], s.n + 1)
                pool.tensor_tensor(x_ms_eps[:, :], mean_var[:, :, 1], eps_ln[:, 0:TILES], ALU.add)
                pool.drain()
                pool.tensor_tensor(rstd[:, :], x_ms_eps[:, :], neg_half[:, 0:TILES], ALU.pow)\
                    .then_inc(sem["rstd_ready"], 1)

            def add_bias(s):
                pool.wait_ge(sem["y_taken"], s.n + 1)
                pool.tensor_tensor(seq(out_res, s.n), y[:, :, :],
                                   w["bo"][:, :].unsqueeze(1).broadcast_to([P, TILES, D]), ALU.add)\
                    .then_inc(sem["bias_added"], 1)

            def step(s, do_scores, attend, finish, do_front):
                if do_front:
                    begin(s + 1)
                if finish:
                    add_bias(s - 2) if gated else layer_norm(s - 2)

            begin(Step(0, 0))
            run_steps(pool, n_seq, step)

        @block.vector
        def _(dve):
            cos, sin = consts["cos"], consts["sin"]

            def x_squares(s):
                dve.wait_ge(x_loaded[s.slot], s.turn * 16 + 16)
                for t in range(TILES):
                    x = x_in[s.slot][:, t, :]
                    last = dve.tensor_tensor_reduce(sq[:, :], x, x, 1.0 / D, 0.0, ALU.mult, ALU.add, x_ms[:, t:t + 1])
                    dve.drain()
                last.then_inc(sem["x_ms_ready"], 1)

            def take_qkv(s):
                if gated:
                    dve.wait_ge(sem["x_rms_ready"], s.n + 1)
                for t in range(TILES):
                    dve.wait_ge(sem["qkv_done"], s.n * 2 + (t + 1))
                    made = qk[:, t * NQK:(t + 1) * NQK, :].rearrange("p h d -> p (h d)")
                    v_made = v_ext[s.slot][:, t, :, 0:HD]
                    v_from = front[t][:, NQK * HD:W].rearrange("p (h d) -> p h d", d=HD)
                    if gated:
                        dve.scalar_tensor_tensor(made, front[t][:, 0:NQK * HD], x_rms[:, t:t + 1],
                                                 w["b_qkv"][:, 0:NQK * HD], ALU.mult, ALU.add)
                        last = dve.scalar_tensor_tensor(
                            v_made, v_from, x_rms[:, t:t + 1],
                            w["b_qkv"][:, NQK * HD:W].rearrange("p (h d) -> p h d", d=HD), ALU.mult, ALU.add)
                    else:
                        dve.tensor_copy(made, front[t][:, 0:NQK * HD])
                        last = dve.tensor_copy(v_made, v_from)
                last.then_inc(sem["qkv_taken"], 1)

            def norm_heads(s, part):
                if part == 0:
                    dve.wait_ge(sem["squared"], s.n + 1)
                    dve.tensor_reduce(sq_sum[:, :], squares[:, :, :], AX_X, ALU.add)
                    dve.drain()
                    dve.tensor_scalar(mean_eps[:, :], sq_sum[:, :], 1.0 / HD, RMS_EPS, ALU.mult, ALU.add)
                    dve.tensor_scalar(minus_half[:, :], sq_sum[:, :], -0.5 / HD, -0.5 * RMS_EPS, ALU.mult, ALU.add)
                last = inverse_root(dve, part, mean_eps[:, :], minus_half[:, :], guess[:, :], head_rms[:, :])
                if part == 3:
                    last.then_inc(sem["head_rms_ready"], 1)

            def round_keys(s):
                dve.wait_ge(sem["turned_ready"], s.n + 1)
                copy_high(dve.tensor_copy, k_rows, 0).then_inc(sem["k_top_ready"], 1)

            def copy_mid(s, rows, rest, places, kind):
                dve.wait_ge(sem[f"{kind}_rest_ready"], s.n + 1)
                for place in places:
                    last = dve.tensor_copy(piece(rows, place), rest[:, :, :])
                last.then_inc(sem[f"{kind}_mid_ready"], 1)

            def take_keys(s, t):
                dve.wait_ge(sem["kt_done"], s.n * 2 + (t + 1))
                dve.tensor_copy(k_t[s.slot][:, :, t * P:(t + 1) * P],
                                front_bf[t][:, 0:NK // 2 * P].rearrange("p (j c) -> p j c", c=P))\
                   .then_inc(sem["kt_copied"], 1)

            def begin(s, slot):
                if slot == 1:
                    take_qkv(s)
                    if not gated:
                        dve.drain()
                        dve.tensor_tensor(turned[:, :, :], qk[:, :, :], rope_cos[:, :, :], ALU.mult)\
                            .then_inc(sem["cos_ready"], 1)
                for part, at in enumerate((3, 5, 5, 6)):
                    if slot == at and gated:
                        norm_heads(s, part)
                if slot == 8:
                    round_keys(s)
                if slot == 9:
                    copy_mid(s, q_rows, rest_q, (5,), "q")
                if slot == 10:
                    copy_mid(s, k_rows, rest_k, (1, 5), "k")
                if slot == 13:
                    take_keys(s, 0)
                if slot == 14:
                    take_keys(s, 1)

            def split_max(s):
                top = neg_top[:, :, :].rearrange("p t (j c) -> p t c j", c=2)
                m = m_rows[:, :, :].rearrange("p t (c r) -> p t c r", c=2)
                high, low = m[:, :, :, 0:HEADS // 2], m[:, :, :, HEADS // 2:HEADS]
                dve.tensor_copy(high, top)
                dve.drain()
                dve.tensor_tensor(low, top, high, ALU.subtract).then_inc(sem["m_rows_ready"], 1)

            def maximum(s, h):
                dve.wait_ge(sem["s_done"], s.n * HEADS + (h + 1))
                if gated:
                    dve.tensor_reduce(neg_top[:, 0, h:h + 1], ps_s[h % 2][:, 0:P], AX_X, ALU.max, negate=True)
                    last = dve.tensor_reduce(neg_top[:, 1, h:h + 1], ps_s[h % 2][:, P:3 * P], AX_X, ALU.max, negate=True)
                else:
                    last = dve.tensor_reduce(neg_top[:, :, h:h + 1],
                                             ps_s[h % 2][:, :].rearrange("p (t c) -> p t c", t=TILES),
                                             AX_X, ALU.max, negate=True)
                last.then_inc(sem["max_done"], 1)

            def normalise(s):
                dve.wait_ge(sem["ot_done"], s.n + 1)
                for t in range(TILES):
                    o = front[t][:, :].rearrange("p (h c) -> p h c", c=32)
                    dve.reciprocal(inv[:, t, :], o[:, :, HD])
                dve.drain()
                for t in range(TILES):
                    o = front[t][:, :].rearrange("p (h c) -> p h c", c=32)
                    last = dve.tensor_tensor(attn[:, t, :].rearrange("p (h d) -> p h d", d=HD), o[:, :, 0:HD],
                                             inv[:, t, :].unsqueeze(2).broadcast_to([P, HEADS, HD]), ALU.mult)
                last.then_inc(sem["attn_ready"], 1)

            def gate(s):
                dve.wait_ge(sem["z_tanh_ready"], s.n + 1)
                dve.scalar_tensor_tensor(attn_t[:, :], gate_t[:, :], 1.0, attn_t[:, :], ALU.add, ALU.mult)\
                   .then_inc(sem["gated_ready"], 1)

            def residual(s):
                if gated and not (isinstance(s.n, int) and s.n == 0):
                    dve.wait_ge(sem["bias_added"], s.n)
                dve.wait_ge(sem["y_done"], s.n + 1)
                dve.scalar_tensor_tensor(y[:, :, :], front[0][:, 0:S].rearrange("p (t d) -> p t d", t=TILES),
                                         0.5 if gated else 1.0, seq(x_res, s.n), ALU.mult, ALU.add)\
                   .then_inc(sem["y_taken"], 1)

            def statistics(s):
                dve.drain()
                for t in range(TILES):
                    dve.bn_stats(stats[:, t, :], y[:, t, :])
                dve.drain()
                for t in range(TILES):
                    last = dve.bn_aggr(mean_var[:, t, :], stats[:, t, :])
                last.then_inc(sem["var_ready"], 1)

            def layer_norm(s):
                dve.wait_ge(sem["rstd_ready"], s.n + 1)
                for t in range(TILES):
                    dve.tensor_scalar(tile(out_res, s.n, t), y[:, t, :], mean_var[:, t, 0:1],
                                      rstd[:, t:t + 1], ALU.subtract, ALU.mult)

            def step(s, do_scores, attend, finish, do_front):
                if do_front and gated:
                    x_squares(s + 1)
                for h in range(HEADS):
                    if do_scores:
                        maximum(s, h)
                    if h == 15 and do_scores:
                        dve.drain()
                        split_max(s)
                        dve.drain()
                    if finish:
                        if h == 4:
                            normalise(s - 2)
                        if h == 7 and gated:
                            gate(s - 2)
                        if h == 9:
                            residual(s - 2)
                        if h == 11 and not gated:
                            statistics(s - 2)
                        if h == 15 and not gated:
                            layer_norm(s - 2)
                    if do_front:
                        begin(s + 1, h)

            for table, angle in ((rope_cos, cos), (rope_sin, sin)):
                if gated:
                    for t in range(TILES):
                        dve.tensor_tensor(table[:, t * NQK:(t + 1) * NQK, :],
                                          angle[:, t:t + 1, :].broadcast_to([P, NQK, HD]),
                                          w["qk_norm"][:, :].rearrange("p (h d) -> p h d", d=HD), ALU.mult)
                else:
                    dve.tensor_copy(by_tile(table[:, :, :]),
                                    angle[:, :, :].unsqueeze(2).broadcast_to([P, TILES, NQK, HD]))
            dve.memset(q_rows[:, :, :].bitcast(U32), 0)
            dve.memset(k_rows[:, :, :].bitcast(U32), 0)
            dve.memset(m_rows[:, :, :].bitcast(U32), 0)
            for r in range(3):
                dve.memset(v_ext[r][:, :, :, :], 0.0)
            dve.drain()
            for r in range(3):
                last = dve.memset(v_ext[r][:, :, :, HD:HD + 1], 1.0)
            dve.drain()
            last.then_inc(sem["zeroed"], 1)
            if gated:
                x_squares(Step(0, 0))
            for slot in range(HEADS):
                begin(Step(0, 0), slot)
            run_steps(dve, n_seq, step)



class Turn:

    def __init__(self, half, offset):
        self.half, self.offset = half, offset
        self.n = half * 2 + offset
        self.slot = offset % 2
        self.turn = half + offset // 2

    def __add__(self, k):
        return Turn(self.half, self.offset + k)

    def __sub__(self, k):
        return Turn(self.half, self.offset - k)


def run_turns(eng, count, step):
    step(Turn(0, 0), False, True)
    step(Turn(0, 1), True, True)
    step(Turn(0, 2), True, True)
    assert count % 2 == 0
    with eng.Fori(0, (count - 4) // 2) as i:
        for c in range(2):
            step(Turn(i, 3 + c), True, True)
    step(Turn(0, count - 1), True, False)


GROUP = 4
COLS = GROUP * P
EXPERTS = 8
HID = 256
CHUNKS = HID // P


def group_of(x_res, n):
    return x_res[:, bass.ds(n * COLS, COLS)].rearrange("p (t d) -> p t d", t=GROUP)


def group_tile(x_res, n, t):
    return x_res[:, bass.ds(n * COLS + t * D, D)]


def expert_weights(room, src):
    w = {
        "w1": room.sb("w1", [D, EXPERTS, 2 * HID]), "w2": room.sb("w2", [P, EXPERTS, CHUNKS, D]),
        "b1": room.sb("b1", [P, EXPERTS, 2 * CHUNKS]), "b2": room.sb("b2", [EXPERTS, D]),
        "wr": room.sb("wr", [D, EXPERTS]), "br": room.sb("br", [P, EXPERTS]), "ln2": room.sb("ln2", [D, 1]),
        "experts": room.sb("experts", [P, EXPERTS]),
    }
    loads = [(w["w1"][:, :, :], src["W1"]), (w["w2"][:, :, :, :], src["W2"]), (w["b1"][:, :, :], src["b1"])]
    loads += [(w[k][:, :], src[of]) for k, of in (("b2", "b2"), ("wr", "Wr"), ("br", "br"), ("ln2", "ln2"),
                                                  ("experts", "experts"))]
    return w, loads


def mixture_of_experts(nc, n_groups, x_res, x1_res, consts, w):
    ident, neg_half, eps_ln, eps_rms = (consts[k] for k in ("ident", "neg_half", "ln_eps", "rms_eps"))
    UNITS = EXPERTS * CHUNKS
    with ExitStack() as stack:
        room = Room(nc, stack, "moe")
        w1, w2, b1, b2, wr, br, ln2, experts = (w[k] for k in ("w1", "w2", "b1", "b2", "wr", "br", "ln2", "experts"))
        x_in = [room.sb(f"x_in{r}", [P, GROUP, D]) for r in range(2)]
        h_t = [room.sb(f"h_t{r}", [D, COLS]) for r in range(2)]
        mask = [room.sb(f"mask{r}", [P, GROUP, EXPERTS]) for r in range(2)]
        mask_t = [room.sb(f"mask_t{r}", [EXPERTS, COLS]) for r in range(2)]
        acc = [room.sb(f"acc{r}", [P, GROUP, D]) for r in range(2)]
        h = room.sb("h", [P, GROUP, D])
        sq = room.sb("sq", [P, D])
        ms = room.sb("ms", [P, GROUP])
        ms_eps = room.sb("ms_eps", [P, GROUP])
        rms = room.sb("rms", [P, GROUP])
        logits = room.sb("logits", [P, GROUP, EXPERTS])
        best = room.sb("best", [P, GROUP, 8])
        index = room.sb("index", [P, GROUP, 8], U32)
        chosen = room.sb("chosen", [P, GROUP])
        sig = [room.sb(f"sig{r}", [P, COLS]) for r in range(2)]
        hidden = [room.sb(f"hidden{r}", [P, COLS]) for r in range(2)]
        stats = room.sb("stats", [P, GROUP, 6])
        mean_var = room.sb("mean_var", [P, GROUP, 2])
        var_eps = room.sb("var_eps", [P, GROUP])
        rstd = room.sb("rstd", [P, GROUP])
        ps_value = [room.psum(f"ps_value{r}", [P, COLS]) for r in range(2)]
        ps_gate = [room.psum(f"ps_gate{r}", [P, COLS]) for r in range(2)]
        ps_y = [room.psum(f"ps_y{r}", [P, GROUP, D]) for r in range(2)]
        ps_h = room.psum("ps_h", [P, COLS])
        ps_r = room.psum("ps_r", [P, COLS])
        names = ("ms_ready rms_ready h_ready ht_done ht_copied logits_done mask_ready "
                 "mask_turned mask_copied acc_ready value_done gate_done sig_ready hidden_ready y_done y_taken "
                 "var_ready rstd_ready finished")
        sem = {k: room.sem(k) for k in names.split()}
        x_loaded = [room.sem(f"x_loaded{r}") for r in range(2)]
        block = room.block()
        YS = EXPERTS + 1

        @block.sync
        def _(sp):
            def load(s):
                sp.dma_start(x_in[s.slot][:, :, :], group_of(x1_res, s.n)).then_inc(x_loaded[s.slot], 16)

            load(Turn(0, 0))
            load(Turn(0, 1))
            with sp.Fori(0, (n_groups - 2) // 2) as i:
                for c in range(2):
                    s = Turn(i, 2 + c)
                    sp.wait_ge(sem["h_ready"], (s - 1).n)
                    sp.wait_ge(sem["acc_ready"], (s - 1).n)
                    load(s)

        @block.tensor
        def _(pe):
            def turn_h(s):
                pe.wait_ge(sem["h_ready"], s.n + 1)
                for t in range(GROUP):
                    last = pe.transpose(ps_h[:, t * P:(t + 1) * P], h[:, t, :], ident[:, :])
                last.then_inc(sem["ht_done"], 1)

            def route(s):
                pe.wait_ge(sem["ht_copied"], s.n + 1)
                for t in range(GROUP):
                    last = pe.matmul(ps_r[:, t * EXPERTS:(t + 1) * EXPERTS], h_t[s.slot][:, t * P:(t + 1) * P],
                                     wr[:, :], start=True, stop=True)
                last.then_inc(sem["logits_done"], 1)

            def turn_mask(s):
                pe.wait_ge(sem["mask_ready"], s.n + 1)
                for t in range(GROUP):
                    last = pe.transpose(ps_r[0:EXPERTS, t * P:(t + 1) * P], mask[s.slot][:, t, :], ident[:, :])
                last.then_inc(sem["mask_turned"], 1)

            def biases(s):
                pe.wait_ge(sem["mask_copied"], s.n + 1)
                bank(s, 0)
                for t in range(GROUP):
                    last = pe.matmul(y_bank(s, 0)[:, t, :], mask_t[s.slot][:, t * P:(t + 1) * P], b2[:, :],
                                     start=True, stop=True)
                last.then_inc(sem["y_done"], 1)

            def y_bank(s, k):
                return ps_y[(s.slot * YS + k) % 2]

            def bank(s, k):
                if not (isinstance(s.n, int) and s.n * YS + k < 2):
                    pe.wait_ge(sem["y_taken"], s.n * YS + (k - 1))

            def up(s, k):
                e, c = k // CHUNKS, k % CHUNKS
                if not (isinstance(s.n, int) and s.n * UNITS + k < 2):
                    pe.wait_ge(sem["hidden_ready"], s.n * UNITS + (k - 1))
                pe.matmul(ps_gate[k % 2][:, :], w1[:, e, HID + c * P:HID + (c + 1) * P], h_t[s.slot][:, :],
                          start=True, stop=True).then_inc(sem["gate_done"], 1)
                pe.matmul(ps_value[k % 2][:, :], w1[:, e, c * P:(c + 1) * P], h_t[s.slot][:, :],
                          start=True, stop=True).then_inc(sem["value_done"], 1)

            def down(s, k):
                e, c = k // CHUNKS, k % CHUNKS
                pe.wait_ge(sem["hidden_ready"], s.n * UNITS + (k + 1))
                if c == 0:
                    bank(s, 1 + e)
                for t in range(GROUP):
                    last = pe.matmul(y_bank(s, 1 + e)[:, t, :], hidden[k % 2][:, t * P:(t + 1) * P],
                                     w2[:, e, c, :], start=c == 0 and t == 0, stop=c == CHUNKS - 1 and t == GROUP - 1)
                if c == CHUNKS - 1:
                    last.then_inc(sem["y_done"], 1)

            def step(s, finish, front):
                biases(s)
                for k in range(UNITS + 1):
                    if k < UNITS:
                        up(s, k)
                    if k >= 1:
                        down(s, k - 1)
                    if front:
                        if k == 6:
                            turn_h(s + 1)
                        if k == 8:
                            route(s + 1)
                        if k == 12:
                            turn_mask(s + 1)

            turn_h(Turn(0, 0))
            route(Turn(0, 0))
            turn_mask(Turn(0, 0))
            run_turns(pe, n_groups, step)

        @block.scalar
        def _(act):
            def take_h(s):
                act.wait_ge(sem["ht_done"], s.n + 1)
                act.activation(h_t[s.slot][:, :], ps_h[:, :], ACT.Copy, scale=ln2[:, 0:1])\
                   .then_inc(sem["ht_copied"], 1)

            def take_mask(s):
                act.wait_ge(sem["mask_turned"], s.n + 1)
                act.copy(mask_t[s.slot][:, :], ps_r[0:EXPERTS, :]).then_inc(sem["mask_copied"], 1)

            def step(s, finish, front):
                for k in range(UNITS):
                    e, c = k // CHUNKS, k % CHUNKS
                    act.wait_ge(sem["gate_done"], s.n * UNITS + (k + 1))
                    if not (isinstance(s.n, int) and s.n * UNITS + k < 2):
                        act.wait_ge(sem["hidden_ready"], s.n * UNITS + (k - 1))
                    act.activation(sig[k % 2][:, :], ps_gate[k % 2][:, :], ACT.Sigmoid,
                                   bias=b1[:, e, CHUNKS + c:CHUNKS + c + 1]).then_inc(sem["sig_ready"], 1)
                    if front:
                        if k == 7:
                            take_h(s + 1)
                        if k == 13:
                            take_mask(s + 1)

            take_h(Turn(0, 0))
            take_mask(Turn(0, 0))
            run_turns(act, n_groups, step)

        @block.gpsimd
        def _(pool):
            def x_norm(s):
                pool.wait_ge(sem["ms_ready"], s.n + 1)
                pool.tensor_tensor(ms_eps[:, :], ms[:, :], eps_rms[:, 0:GROUP], ALU.add)
                pool.drain()
                pool.tensor_tensor(rms[:, :], ms_eps[:, :], neg_half[:, 0:GROUP], ALU.pow)\
                    .then_inc(sem["rms_ready"], 1)

            def start_sum(s):
                pool.wait_ge(x_loaded[s.slot], s.turn * 16 + 16)
                if not (isinstance(s.n, int) and s.n < 2):
                    pool.wait_ge(sem["finished"], (s - 1).n)
                pool.tensor_tensor(acc[s.slot][:, :, :], x_in[s.slot][:, :, :], group_of(x_res, s.n), ALU.add)\
                    .then_inc(sem["acc_ready"], 1)

            def layer_norm(s):
                pool.wait_ge(sem["var_ready"], s.n + 1)
                pool.tensor_tensor(var_eps[:, :], mean_var[:, :, 1], eps_ln[:, 0:GROUP], ALU.add)
                pool.drain()
                pool.tensor_tensor(rstd[:, :], var_eps[:, :], neg_half[:, 0:GROUP], ALU.pow)\
                    .then_inc(sem["rstd_ready"], 1)

            def step(s, finish, front):
                if finish:
                    layer_norm(s - 1)
                if front:
                    x_norm(s + 1)
                    start_sum(s + 1)

            x_norm(Turn(0, 0))
            start_sum(Turn(0, 0))
            run_turns(pool, n_groups, step)
            layer_norm(Turn(0, n_groups - 1))

        @block.vector
        def _(dve):
            def squares(s):
                dve.wait_ge(x_loaded[s.slot], s.turn * 16 + 16)
                for t in range(GROUP):
                    x = x_in[s.slot][:, t, :]
                    last = dve.tensor_tensor_reduce(sq[:, :], x, x, 1.0 / D, 0.0, ALU.mult, ALU.add, ms[:, t:t + 1])
                    dve.drain()
                last.then_inc(sem["ms_ready"], 1)

            def scale_h(s):
                dve.wait_ge(sem["rms_ready"], s.n + 1)
                for t in range(GROUP):
                    last = dve.tensor_scalar(h[:, t, :], x_in[s.slot][:, t, :], rms[:, t:t + 1], None, ALU.mult)
                last.then_inc(sem["h_ready"], 1)

            def choose(s):
                dve.wait_ge(sem["logits_done"], s.n + 1)
                dve.tensor_tensor(logits[:, :, :], ps_r[:, 0:GROUP * EXPERTS].rearrange("p (t e) -> p t e", t=GROUP),
                                  br[:, :].unsqueeze(1).broadcast_to([P, GROUP, EXPERTS]), ALU.add)
                dve.drain()
                for t in range(GROUP):
                    dve.max(best[:, t, :], logits[:, t, :])
                dve.drain()
                for t in range(GROUP):
                    dve.max_index(index[:, t, :], best[:, t, :], logits[:, t, :])
                dve.drain()
                dve.tensor_copy(chosen[:, :], index[:, :, 0])
                dve.drain()
                for t in range(GROUP):
                    last = dve.tensor_scalar(mask[s.slot][:, t, :], experts[:, :], chosen[:, t:t + 1], None, ALU.is_equal)
                last.then_inc(sem["mask_ready"], 1)

            def take_biases(s):
                dve.wait_ge(sem["y_done"], s.n * YS + 1)
                dve.wait_ge(sem["acc_ready"], s.n + 1)
                a, y = acc[s.slot], ps_y[(s.slot * YS) % 2]
                dve.tensor_tensor(a[:, :, :], y[:, :, :], a[:, :, :], ALU.add).then_inc(sem["y_taken"], 1)

            def take(s, e):
                dve.drain()
                dve.wait_ge(sem["y_done"], s.n * YS + (e + 2))
                a, y = acc[s.slot], ps_y[(s.slot * YS + 1 + e) % 2]
                for t in range(GROUP):
                    last = dve.scalar_tensor_tensor(a[:, t, :], y[:, t, :], mask[s.slot][:, t, e:e + 1], a[:, t, :],
                                                    ALU.mult, ALU.add)
                last.then_inc(sem["y_taken"], 1)

            def statistics(s):
                dve.drain()
                for t in range(GROUP):
                    dve.bn_stats(stats[:, t, :], acc[s.slot][:, t, :])
                dve.drain()
                for t in range(GROUP):
                    last = dve.bn_aggr(mean_var[:, t, :], stats[:, t, :])
                last.then_inc(sem["var_ready"], 1)

            def normalise(s):
                dve.wait_ge(sem["rstd_ready"], s.n + 1)
                for t in range(GROUP):
                    last = dve.tensor_scalar(group_tile(x_res, s.n, t), acc[s.slot][:, t, :], mean_var[:, t, 0:1],
                                             rstd[:, t:t + 1], ALU.subtract, ALU.mult)
                last.then_inc(sem["finished"], 1)

            def step(s, finish, front):
                take_biases(s)
                for k in range(UNITS):
                    e, c = k // CHUNKS, k % CHUNKS
                    dve.wait_ge(sem["sig_ready"], s.n * UNITS + (k + 1))
                    dve.wait_ge(sem["value_done"], s.n * UNITS + (k + 1))
                    dve.scalar_tensor_tensor(hidden[k % 2][:, :], ps_value[k % 2][:, :], b1[:, e, c:c + 1],
                                             sig[k % 2][:, :], ALU.add, ALU.mult).then_inc(sem["hidden_ready"], 1)
                    if k >= 2 and k % 2 == 0:
                        take(s, k // 2 - 1)
                    if finish and k == 1:
                        normalise(s - 1)
                    if front:
                        if k == 3:
                            squares(s + 1)
                        if k == 5:
                            scale_h(s + 1)
                        if k == 9:
                            choose(s + 1)
                take(s, EXPERTS - 1)
                statistics(s)

            squares(Turn(0, 0))
            scale_h(Turn(0, 0))
            choose(Turn(0, 0))
            run_turns(dve, n_groups, step)
            normalise(Turn(0, n_groups - 1))


def shift_loads(eng, src, dst, n, count, done):
    half = D // 2
    v = src[:, bass.ds(n * count * D, count * D)].rearrange("p (t d) -> p t d", t=count)
    eng.dma_start(dst[:, :, 0:half], v[:, :, 0:half]).then_inc(done, 16)
    eng.dma_start(dst[1:P, :, half:D], v[0:P - 1, :, half:D]).then_inc(done, 16)
    eng.dma_start(dst[0:1, 1:count:2, half:D], v[P - 1:P, 0:count:2, half:D]).then_inc(done, 16)


FF = 341
FF_CHUNKS = [(c, min(P, FF - c)) for c in range(0, FF, P)]


def feed_forward_weights(room, src):
    N = len(FF_CHUNKS)
    w = {
        "w1": room.sb("w1", [D, 2 * FF]), "w2": room.sb("w2", [P, N, D]), "b1": room.sb("b1", [P, 2 * N]),
        "b2": room.sb("b2", [P, D]), "ln_g": room.sb("ln_g", [D, 1]), "ln_b": room.sb("ln_b", [D, 1]),
    }
    loads = [(w[k][:, :], src[k]) for k in ("w1", "b2", "ln_g", "ln_b")]
    for k, (c, m) in enumerate(FF_CHUNKS):
        loads += [(w["w2"][0:m, k, :], src["w2"][c:c + m, :]), (w["b1"][0:m, k:k + 1], src["b1"][c:c + m, :]),
                  (w["b1"][0:m, N + k:N + k + 1], src["b1"][FF + c:FF + c + m, :])]
    return w, loads


def gated_feed_forward(nc, n_groups, layer, x_res, consts, w, first=None, out_dram=None, ahead=()):
    ident, neg_half, eps_ln = (consts[k] for k in ("ident", "neg_half", "ln_eps"))
    N = len(FF_CHUNKS)
    final = out_dram is not None
    with ExitStack() as stack:
        room = Room(nc, stack, f"ffn{layer}")
        w1, w2, b1, b2, ln_g, ln_b = (w[k] for k in ("w1", "w2", "b1", "b2", "ln_g", "ln_b"))
        shifted = [room.sb(f"shifted{r}", [P, GROUP, D]) for r in range(2)]
        h_t = [room.sb(f"h_t{r}", [D, COLS]) for r in range(2)]
        h = room.sb("h", [P, GROUP, D])
        x_b = [room.sb(f"x_b{r}", [P, GROUP, D]) for r in range(2)]
        result = [room.sb(f"result{r}", [P, GROUP, D]) for r in range(2)]
        gelu = [room.sb(f"gelu{r}", [P, COLS]) for r in range(3)]
        hidden = [room.sb(f"hidden{r}", [P, COLS]) for r in range(3)]
        stats = room.sb("stats", [P, GROUP, 6])
        mean_var = room.sb("mean_var", [P, GROUP, 2])
        var_eps = room.sb("var_eps", [P, GROUP])
        rstd = room.sb("rstd", [P, GROUP])
        stats2 = room.sb("stats2", [P, GROUP, 6])
        mean_var2 = room.sb("mean_var2", [P, GROUP, 2])
        rstd2 = room.sb("rstd2", [P, GROUP])
        var_eps2 = room.sb("var_eps2", [P, GROUP])
        ps_value = [room.psum(f"ps_value{r}", [P, COLS]) for r in range(2)]
        ps_gate = [room.psum(f"ps_gate{r}", [P, COLS]) for r in range(2)]
        ps_y = [room.psum(f"ps_y{r}", [P, GROUP, D]) for r in range(2)]
        ps_h = room.psum("ps_h", [P, COLS])
        names = ("zeroed var_ready rstd_ready h_ready ht_done ht_copied xb_ready value_done gate_done "
                 "gelu_ready hidden_ready y_done y_taken var2_ready rstd2_ready result_ready")
        sem = {k: room.sem(k) for k in names.split()}
        loaded = [room.sem(f"loaded{r}") for r in range(2)]
        stored = [room.sem(f"stored{r}") for r in range(2)]
        next_weights = Ahead(room, ahead)
        block = room.block()

        @block.sync
        def _(sp):
            def load(s):
                shift_loads(sp, x_res, shifted[s.slot], s.n, GROUP, loaded[s.slot])

            def store(s):
                sp.wait_ge(sem["result_ready"], s.n + 1)
                sp.dma_start(out_dram[bass.ds(s.n * 2, 2)].rearrange("b (t p) d -> p (b t) d", p=P),
                             result[s.slot][:, :, :]).then_inc(stored[s.slot], 16)

            sp.wait_ge(sem["zeroed"], 1)
            load(Turn(0, 0))
            load(Turn(0, 1))
            next_weights.start(sp)
            def later(s, storing):
                sp.wait_ge(sem["h_ready"], (s - 1).n)
                load(s)
                if final and storing:
                    store(s - 3)

            later(Turn(0, 2), False)
            later(Turn(0, 3), True)
            with sp.Fori(0, (n_groups - 4) // 2) as i:
                for c in range(2):
                    later(Turn(i, 4 + c), True)
            if final:
                for n in range(n_groups - 3, n_groups):
                    store(Turn(0, n))
                for r in range(2):
                    sp.wait_ge(stored[r], 16 * (n_groups // 2))
            next_weights.wait(sp)

        @block.tensor
        def _(pe):
            def turn_h(s):
                pe.wait_ge(sem["h_ready"], s.n + 1)
                for t in range(GROUP):
                    last = pe.transpose(ps_h[:, t * P:(t + 1) * P], h[:, t, :], ident[:, :])
                last.then_inc(sem["ht_done"], 1)

            def up(s, k):
                c, m = FF_CHUNKS[k]
                r = (s.slot * N + k) % 2
                if k == 0:
                    pe.wait_ge(sem["ht_copied"], s.n + 1)
                if not (isinstance(s.n, int) and s.n * N + k < 2):
                    pe.wait_ge(sem["hidden_ready"], s.n * N + (k - 1))
                pe.matmul(ps_gate[r][0:m, :], w1[:, FF + c:FF + c + m], h_t[s.slot][:, :],
                          start=True, stop=True).then_inc(sem["gate_done"], 1)
                pe.matmul(ps_value[r][0:m, :], w1[:, c:c + m], h_t[s.slot][:, :],
                          start=True, stop=True).then_inc(sem["value_done"], 1)

            def down(s, k):
                c, m = FF_CHUNKS[k]
                pe.wait_ge(sem["hidden_ready"], s.n * N + (k + 1))
                if k == 0 and not (isinstance(s.n, int) and s.n < 2):
                    pe.wait_ge(sem["y_taken"], (s - 1).n)
                for t in range(GROUP):
                    last = pe.matmul(ps_y[s.slot][:, t, :], hidden[k][0:m, t * P:(t + 1) * P], w2[0:m, k, :],
                                     start=k == 0 and t == 0, stop=k == N - 1 and t == GROUP - 1)
                if k == N - 1:
                    last.then_inc(sem["y_done"], 1)

            def step(s, finish, front):
                for k in range(N):
                    up(s, k)
                    if k == 0 and finish:
                        down(s - 1, N - 1)
                    if front and k == 2:
                        turn_h(s + 1)
                    if k >= 1:
                        down(s, k - 1)

            turn_h(Turn(0, 0))
            run_turns(pe, n_groups, step)
            down(Turn(0, n_groups - 1), N - 1)

        @block.scalar
        def _(act):
            def take_h(s):
                act.wait_ge(sem["ht_done"], s.n + 1)
                act.activation(h_t[s.slot][:, :], ps_h[:, :], ACT.Identity, bias=ln_b[:, 0:1], scale=ln_g[:, 0:1])\
                   .then_inc(sem["ht_copied"], 1)

            def step(s, finish, front):
                for k, (c, m) in enumerate(FF_CHUNKS):
                    r = (s.slot * N + k) % 2
                    act.wait_ge(sem["gate_done"], s.n * N + (k + 1))
                    if not (isinstance(s.n, int) and s.n == 0):
                        act.wait_ge(sem["hidden_ready"], s.n * N + (k + 1 - N))
                    act.activation(gelu[k][0:m, :], ps_gate[r][0:m, :], ACT.Gelu,
                                   bias=b1[0:m, N + k:N + k + 1]).then_inc(sem["gelu_ready"], 1)
                    if front and k == 2:
                        take_h(s + 1)

            take_h(Turn(0, 0))
            run_turns(act, n_groups, step)

        @block.gpsimd
        def _(pool):
            def layer_norm(s):
                pool.wait_ge(sem["var_ready"], s.n + 1)
                pool.tensor_tensor(var_eps[:, :], mean_var[:, :, 1], eps_ln[:, 0:GROUP], ALU.add)
                pool.drain()
                pool.tensor_tensor(rstd[:, :], var_eps[:, :], neg_half[:, 0:GROUP], ALU.pow)\
                    .then_inc(sem["rstd_ready"], 1)

            def last_norm(s):
                pool.wait_ge(sem["var2_ready"], s.n + 1)
                pool.tensor_tensor(var_eps2[:, :], mean_var2[:, :, 1], eps_ln[:, 0:GROUP], ALU.add)
                pool.drain()
                pool.tensor_tensor(rstd2[:, :], var_eps2[:, :], neg_half[:, 0:GROUP], ALU.pow)\
                    .then_inc(sem["rstd2_ready"], 1)

            def add_bias(s):
                if not (isinstance(s.n, int) and s.n < 2):
                    pool.wait_ge(sem["y_taken"], (s - 1).n)
                pool.tensor_tensor(x_b[s.slot][:, :, :], group_of(x_res, s.n),
                                   b2[:, :].unsqueeze(1).broadcast_to([P, GROUP, D]), ALU.add)\
                    .then_inc(sem["xb_ready"], 1)
                if final:
                    pool.wait_ge(sem["xb_ready"], s.n * 2 + 1)
                    pool.tensor_tensor(x_b[s.slot][:, :, :], x_b[s.slot][:, :, :], group_of(first, s.n), ALU.add)\
                        .then_inc(sem["xb_ready"], 1)

            def step(s, finish, front):
                if front:
                    layer_norm(s + 1)
                if finish and final:
                    last_norm(s - 1)
                add_bias(s)

            layer_norm(Turn(0, 0))
            run_turns(pool, n_groups, step)
            if final:
                last_norm(Turn(0, n_groups - 1))

        @block.vector
        def _(dve):
            def statistics(s):
                dve.wait_ge(loaded[s.slot], s.turn * 48 + 48)
                for t in range(GROUP):
                    dve.bn_stats(stats[:, t, :], shifted[s.slot][:, t, :])
                dve.drain()
                for t in range(GROUP):
                    last = dve.bn_aggr(mean_var[:, t, :], stats[:, t, :])
                last.then_inc(sem["var_ready"], 1)

            def normalise(s):
                dve.wait_ge(sem["rstd_ready"], s.n + 1)
                if not (isinstance(s.n, int) and s.n == 0):
                    dve.wait_ge(sem["ht_done"], s.n)
                for t in range(GROUP):
                    last = dve.tensor_scalar(h[:, t, :], shifted[s.slot][:, t, :], mean_var[:, t, 0:1],
                                             rstd[:, t:t + 1], ALU.subtract, ALU.mult)
                last.then_inc(sem["h_ready"], 1)

            def take(s):
                dve.wait_ge(sem["y_done"], s.n + 1)
                dve.wait_ge(sem["xb_ready"], s.n * 2 + 2 if final else s.n + 1)
                out = x_b[s.slot][:, :, :] if final else group_of(x_res, s.n)
                ins = dve.tensor_tensor(out, ps_y[s.slot][:, :, :], x_b[s.slot][:, :, :], ALU.add)
                if not final:
                    ins.then_inc(sem["y_taken"], 1)
                    return
                dve.drain()
                for t in range(GROUP):
                    dve.bn_stats(stats2[:, t, :], x_b[s.slot][:, t, :])
                dve.drain()
                for t in range(GROUP):
                    last = dve.bn_aggr(mean_var2[:, t, :], stats2[:, t, :])
                last.then_inc(sem["var2_ready"], 1)

            def last_normalise(s):
                dve.wait_ge(sem["rstd2_ready"], s.n + 1)
                if not (isinstance(s.n, int) and s.n < 2):
                    dve.wait_ge(stored[s.slot], s.turn * 16)
                for t in range(GROUP):
                    last = dve.tensor_scalar(result[s.slot][:, t, :], x_b[s.slot][:, t, :], mean_var2[:, t, 0:1],
                                             rstd2[:, t:t + 1], ALU.subtract, ALU.mult)
                last.then_inc(sem["result_ready"], 1)
                dve.drain().then_inc(sem["y_taken"], 1)

            def step(s, finish, front):
                if front:
                    statistics(s + 1)
                for k, (c, m) in enumerate(FF_CHUNKS):
                    r = (s.slot * N + k) % 2
                    dve.wait_ge(sem["gelu_ready"], s.n * N + (k + 1))
                    dve.wait_ge(sem["value_done"], s.n * N + (k + 1))
                    dve.scalar_tensor_tensor(hidden[k][0:m, :], ps_value[r][0:m, :], b1[0:m, k:k + 1],
                                             gelu[k][0:m, :], ALU.add, ALU.mult).then_inc(sem["hidden_ready"], 1)
                    if finish and k == 0:
                        take(s - 1)
                    if front and k == 1:
                        normalise(s + 1)
                    if finish and k == 2 and final:
                        last_normalise(s - 1)

            for r in range(2):
                last = dve.memset(shifted[r][0:1, :, D // 2:D], 0.0)
            dve.drain().then_inc(sem["zeroed"], 1)
            statistics(Turn(0, 0))
            normalise(Turn(0, 0))
            run_turns(dve, n_groups, step)
            take(Turn(0, n_groups - 1))
            if final:
                last_normalise(Turn(0, n_groups - 1))



LH = 8
LD = 64
WINDOW = 64
INNER = LH * LD


def window_weights(room, src):
    w = {
        "qkv": room.sb("w_qkv", [D, 3, INNER]), "out": room.sb("w_out", [P, INNER // P, D]),
        "scales": room.sb("scales", [P, 2, LD]),
        "cos": [room.sb(f"cos{c}", [P, TILES, LD]) for c in range(2)],
        "sin": [room.sb(f"sin{c}", [P, TILES, LD]) for c in range(2)],
    }
    loads = [(w[k][:, :, :], src[k]) for k in ("qkv", "out", "scales")]
    loads += [(w[k][c][:, :, :], src[k][c]) for k in ("cos", "sin") for c in range(2)]
    return w, loads


def windowed_attention(nc, n_seq, layer, src, dst, consts, w, ahead=()):
    ident, ident_bf, neg_half, band = (consts[k] for k in ("ident", "ident_bf", "neg_half", "band"))
    FIRST, SECOND = slice(0, P), slice(P + WINDOW, 3 * P)
    with ExitStack() as stack:
        room = Room(nc, stack, f"win{layer}")
        w_qkv, w_out, scales, cos, sin = (w[k] for k in ("qkv", "out", "scales", "cos", "sin"))
        shifted = [room.sb(f"shifted{r}", [P, TILES, D]) for r in range(2)]
        h_t = room.sb("h_t", [D, S])
        raw = [room.sb(f"raw{c}", [P, TILES * LH, LD]) for c in range(2)]
        turned = [room.sb(f"turned{c}", [P, TILES * LH, LD]) for c in range(2)]
        swapped = [room.sb(f"swapped{c}", [P, TILES * LH, LD]) for c in range(2)]
        squares = [room.sb(f"squares{c}", [P, TILES * LH, LD]) for c in range(2)]
        sq_sum = room.sb("sq_sum", [P, 2, TILES * LH])
        minus_half = room.sb("minus_half", [P, 2, TILES * LH])
        guess = room.sb("guess", [P, 2, TILES * LH])
        inv_norm = room.sb("inv_norm", [P, 2, TILES * LH])
        v = [room.sb(f"v{r}", [P, TILES, INNER]) for r in range(2)]
        qk_t = [[room.sb(f"qk_t{r}{c}", [P, LH // 2, S]) for c in range(2)] for r in range(2)]
        neg_top = room.sb("neg_top", [P, 2, TILES])
        probs = [room.sb(f"probs{r}", [P, 3 * P]) for r in range(2)]
        probs_t = [room.sb(f"probs_t{r}", [P, 3 * P]) for r in range(2)]
        total = [room.sb(f"total{r}", [P, TILES, LH]) for r in range(2)]
        inv = room.sb("inv", [P, TILES, LH])
        attn = room.sb("attn", [P, TILES, INNER])
        attn_t = room.sb("attn_t", [P, INNER // P, S])
        ps_s = [room.psum(f"ps_s{r}", [P, 512]) for r in range(2)]
        ps_p = [room.psum(f"ps_p{r}", [P, 512]) for r in range(2)]
        ps_o = [room.psum(f"ps_o{r}", [P, INNER]) for r in range(2)]
        bank = [room.psum(f"bank{r}", [P, 512]) for r in range(2)]
        names = ("zeroed ht_done ht_copied qkv_done raw_ready v_ready sq_ready "
                 "k_cos_ready rotated qk_ready qkt_done qkt_copied s_done max_ready exp_done pt_done pt_copied "
                 "o_done attn_ready at_done at_copied y_done y_taken")
        sem = {k: room.sem(k) for k in names.split()}
        loaded = [room.sem(f"loaded{r}") for r in range(2)]
        next_weights = Ahead(room, ahead)
        block = room.block()

        @block.sync
        def _(sp):
            def load(s):
                shift_loads(sp, src, shifted[s.slot], s.n, TILES, loaded[s.slot])

            sp.wait_ge(sem["zeroed"], 1)
            load(Turn(0, 0))
            load(Turn(0, 1))
            next_weights.start(sp)
            with sp.Fori(0, (n_seq - 2) // 2) as i:
                for c in range(2):
                    s = Turn(i, 2 + c)
                    sp.wait_ge(sem["ht_done"], (s - 1).n)
                    load(s)
            next_weights.wait(sp)

        @block.tensor
        def _(pe):
            def turn_h(s):
                pe.wait_ge(loaded[s.slot], s.turn * 48 + 48)
                for t in range(TILES):
                    last = pe.transpose(bank[0][:, t * P:(t + 1) * P], shifted[s.slot][:, t, :], ident[:, :])
                last.then_inc(sem["ht_done"], 1)

            def project(s, c):
                pe.wait_ge(sem["ht_copied"], s.n + 1)
                for t in range(TILES):
                    if c >= 1:
                        pe.wait_ge(sem["raw_ready"], s.n * 4 + ((c - 1) * 2 + t + 1))
                    pe.matmul(bank[t][:, :], h_t[:, t * P:(t + 1) * P], w_qkv[:, c, :],
                              start=True, stop=True).then_inc(sem["qkv_done"], 1)

            def turn_qk(s, c):
                pe.wait_ge(sem["qk_ready"], s.n * 2 + (c + 1))
                for t in range(TILES):
                    if c == 1:
                        pe.wait_ge(sem["qkt_copied"], s.n * 4 + (t + 1))
                    for j in range(LH // 2):
                        at = t * LH + 2 * j
                        last = pe.transpose(bank[t][:, j * P:(j + 1) * P], raw[c][:, at:at + 2, :], ident[:, :])
                    last.then_inc(sem["qkt_done"], 1)

            def scores(s, h):
                half = slice(LD * (h % 2), LD * (h % 2) + LD)
                q, k = (qk_t[s.slot][c][half, h // 2, :] for c in range(2))
                if not (isinstance(s.n, int) and s.n == 0 and h < 2):
                    pe.wait_ge(sem["exp_done"], s.n * LH + (h - 1))
                out = ps_s[h % 2]
                pe.matmul(out[:, 0:P], q[:, 0:P], k[:, 0:P], start=True, stop=False)
                pe.matmul(out[:, P:5 * WINDOW], q[:, P:S], k[:, WINDOW:S], start=False, stop=False)
                pe.matmul(out[:, 0:5 * WINDOW], ident_bf[:, :], band[:, :], start=False, stop=True)\
                  .then_inc(sem["s_done"], 1)

            def turn_probs(s, h):
                pe.wait_ge(sem["exp_done"], s.n * LH + (h + 1))
                if not (isinstance(s.n, int) and s.n == 0 and h < 2):
                    pe.wait_ge(sem["pt_copied"], s.n * LH + (h - 1))
                for b in range(3):
                    last = pe.transpose(ps_p[h % 2][:, b * P:(b + 1) * P], probs[h % 2][:, b * P:(b + 1) * P],
                                        ident[:, :])
                last.then_inc(sem["pt_done"], 1)

            def weigh(s, h):
                pe.wait_ge(sem["pt_copied"], s.n * LH + (h + 1))
                if h == 0 and not (isinstance(s.n, int) and s.n == 0):
                    pe.wait_ge(sem["attn_ready"], s.n)
                cols = slice(h * LD, (h + 1) * LD)
                p = probs_t[h % 2]
                pe.matmul(ps_o[0][:, cols], p[:, 0:P], v[s.slot][:, 0, cols], start=True, stop=True)
                pe.matmul(ps_o[1][:, cols], p[:, P:2 * P], v[s.slot][:, 0, cols], start=True, stop=False)
                pe.matmul(ps_o[1][:, cols], p[:, 2 * P:3 * P], v[s.slot][:, 1, cols],
                          start=False, stop=True).then_inc(sem["o_done"], 1)

            def turn_attn(s):
                pe.wait_ge(sem["attn_ready"], s.n + 1)
                for t in range(TILES):
                    for c in range(INNER // P):
                        last = pe.transpose(bank[t][:, c * P:(c + 1) * P], attn[:, t, c * P:(c + 1) * P], ident[:, :])
                    last.then_inc(sem["at_done"], 1)

            def project_out(s):
                pe.wait_ge(sem["at_copied"], s.n * 2 + 2)
                for t in range(TILES):
                    for c in range(INNER // P):
                        last = pe.matmul(bank[0][:, t * D:(t + 1) * D], attn_t[:, c, t * P:(t + 1) * P],
                                         w_out[:, c, :], start=c == 0, stop=c == INNER // P - 1)
                last.then_inc(sem["y_done"], 1)

            def step(s, finish, front):
                if finish:
                    turn_probs(s - 1, LH - 1)
                    weigh(s - 1, LH - 2)
                pe.wait_ge(sem["qkt_copied"], s.n * 4 + 4)
                if front:
                    turn_h(s + 1)
                for h in range(LH):
                    scores(s, h)
                    if h > 0:
                        turn_probs(s, h - 1)
                        if h == 1 and finish:
                            weigh(s - 1, LH - 1)
                        if h >= 2:
                            weigh(s, h - 2)
                    if front and h < 3:
                        project(s + 1, h)
                    if h == 3 and finish:
                        if front:
                            pe.wait_ge(sem["v_ready"], (s + 1).n + 1)
                        turn_attn(s - 1)
                    if h == 5 and finish:
                        project_out(s - 1)
                    if front and h >= 6:
                        if h == 6:
                            if finish:
                                pe.wait_ge(sem["y_taken"], s.n)
                            pe.wait_ge(sem["v_ready"], (s + 1).n + 1)
                        turn_qk(s + 1, h - 6)

            def tail(s):
                turn_probs(s, LH - 1)
                weigh(s, LH - 2)
                weigh(s, LH - 1)
                turn_attn(s)
                project_out(s)

            pe.wait_ge(sem["zeroed"], 2)
            s0 = Turn(0, 0)
            turn_h(s0)
            for c in range(3):
                project(s0, c)
            pe.wait_ge(sem["v_ready"], 1)
            turn_qk(s0, 0)
            turn_qk(s0, 1)
            run_turns(pe, n_seq, step)
            tail(Turn(0, n_seq - 1))

        @block.scalar
        def _(act):
            def take_h(s):
                act.wait_ge(sem["ht_done"], s.n + 1)
                act.copy(h_t[:, :], bank[0][:, 0:S]).then_inc(sem["ht_copied"], 1)

            def take(s, c):
                if c < 2 and not (isinstance(s.n, int) and s.n == 0):
                    act.wait_ge(sem["qkt_done"], s.n * 4)
                for t in range(TILES):
                    act.wait_ge(sem["qkv_done"], s.n * 6 + (c * 2 + t + 1))
                    if c < 2:
                        act.copy(raw[c][:, t * LH:(t + 1) * LH, :],
                                 bank[t][:, :].rearrange("p (h d) -> p h d", d=LD)).then_inc(sem["raw_ready"], 1)
                    else:
                        last = act.copy(v[s.slot][:, t, :], bank[t][:, :])
                if c == 2:
                    last.then_inc(sem["v_ready"], 1)

            def square(s, c):
                act.drain()
                act.square(squares[c][:, :, :], raw[c][:, :, :]).then_inc(sem["sq_ready"], 1)

            def take_qkt(s, c):
                for t in range(TILES):
                    act.wait_ge(sem["qkt_done"], s.n * 4 + (c * 2 + t + 1))
                    act.copy(qk_t[s.slot][c][:, :, t * P:(t + 1) * P],
                             bank[t][:, :].rearrange("p (j c) -> p j c", c=P)).then_inc(sem["qkt_copied"], 1)

            def take_attn(s, t):
                act.wait_ge(sem["at_done"], s.n * 2 + (t + 1))
                act.copy(attn_t[:, :, t * P:(t + 1) * P],
                         bank[t][:, :].rearrange("p (c k) -> p c k", k=P)).then_inc(sem["at_copied"], 1)

            def exponentials(s, h):
                act.wait_ge(sem["max_ready"], s.n * LH + (h + 1))
                if not (isinstance(s.n, int) and s.n == 0 and h < 2):
                    act.wait_ge(sem["pt_done"], s.n * LH + (h - 1))
                out = probs[h % 2]
                act.activation(out[:, FIRST], ps_s[h % 2][:, 0:P], ACT.Exp, bias=neg_top[:, h % 2, 0:1],
                               accum_out=total[s.slot][:, 0, h:h + 1])
                act.activation(out[:, SECOND], ps_s[h % 2][:, P:5 * WINDOW], ACT.Exp, bias=neg_top[:, h % 2, 1:2],
                               accum_out=total[s.slot][:, 1, h:h + 1]).then_inc(sem["exp_done"], 1)

            def step(s, finish, front):
                if front:
                    take_h(s + 1)
                for h in range(LH):
                    exponentials(s, h)
                    if front and h < 3:
                        take(s + 1, h)
                        if h < 2:
                            square(s + 1, h)
                    if finish and h in (3, 4):
                        take_attn(s - 1, h - 3)
                    if front and h >= 6:
                        take_qkt(s + 1, h - 6)

            s0 = Turn(0, 0)
            take_h(s0)
            for c in range(3):
                take(s0, c)
                if c < 2:
                    square(s0, c)
            take_qkt(s0, 0)
            take_qkt(s0, 1)
            run_turns(act, n_seq, step)
            for t in range(TILES):
                take_attn(Turn(0, n_seq - 1), t)

        def by_tile(a):
            return a[:, :, :].rearrange("p (t h) d -> p t h d", t=TILES)

        def times_cos(eng, c):
            return eng.tensor_tensor(by_tile(turned[c]), by_tile(raw[c]),
                                     cos[c][:, :, :].unsqueeze(2).broadcast_to([P, TILES, LH, LD]), ALU.mult)

        @block.gpsimd
        def _(pool):
            def times_sin(c):
                half = [P, TILES, LH, LD // 2]
                x, b = by_tile(raw[c]), by_tile(swapped[c])
                for a, other in ((0, LD // 2), (LD // 2, 0)):
                    pool.tensor_tensor(b[:, :, :, a:a + LD // 2], x[:, :, :, other:other + LD // 2],
                                       sin[c][:, :, a:a + LD // 2].unsqueeze(2).broadcast_to(half), ALU.mult)

            def rotate(s, c):
                pool.wait_ge(sem["raw_ready"], s.n * 4 + (c * 2 + 2))
                times_sin(c)
                if c == 0:
                    times_cos(pool, 0)
                pool.drain()
                if c == 1:
                    pool.wait_ge(sem["k_cos_ready"], s.n + 1)
                pool.tensor_tensor(turned[c][:, :, :], turned[c][:, :, :], swapped[c][:, :, :], ALU.add)\
                    .then_inc(sem["rotated"], 1)

            def step(s, finish, front):
                if front:
                    rotate(s + 1, 0)
                    rotate(s + 1, 1)

            pool.wait_ge(sem["zeroed"], 2)
            rotate(Turn(0, 0), 0)
            rotate(Turn(0, 0), 1)
            run_turns(pool, n_seq, step)

        @block.vector
        def _(dve):
            def sums(s, c):
                dve.wait_ge(sem["sq_ready"], s.n * 2 + (c + 1))
                dve.tensor_reduce(sq_sum[:, c, :], squares[c][:, :, :], AX_X, ALU.add)

            def norms(s, part):
                if part == 0:
                    dve.drain()
                    dve.tensor_scalar(minus_half[:, :, :], sq_sum[:, :, :], 1e-24, -0.5, ALU.max, ALU.mult)
                    dve.tensor_scalar(sq_sum[:, :, :], sq_sum[:, :, :], 1e-24, None, ALU.max)
                inverse_root(dve, part, sq_sum[:, :, :], minus_half[:, :, :], guess[:, :, :], inv_norm[:, :, :])

            def turn_k(s):
                dve.wait_ge(sem["raw_ready"], s.n * 4 + 4)
                times_cos(dve, 1).then_inc(sem["k_cos_ready"], 1)

            def scale(s, c):
                dve.drain()
                dve.wait_ge(sem["rotated"], s.n * 2 + (c + 1))
                dve.tensor_tensor(raw[c][:, :, :], turned[c][:, :, :],
                                  inv_norm[:, c, :].unsqueeze(2).broadcast_to([P, TILES * LH, LD]), ALU.mult)\
                   .then_inc(sem["qk_ready"], 1)

            def maximum(s, h):
                dve.wait_ge(sem["s_done"], s.n * LH + (h + 1))
                dve.tensor_reduce(neg_top[:, h % 2, 0:1], ps_s[h % 2][:, 0:P], AX_X, ALU.max, negate=True)
                dve.tensor_reduce(neg_top[:, h % 2, 1:2], ps_s[h % 2][:, P:5 * WINDOW], AX_X, ALU.max, negate=True)\
                   .then_inc(sem["max_ready"], 1)

            def take_probs(s, h):
                dve.wait_ge(sem["pt_done"], s.n * LH + (h + 1))
                dve.tensor_copy(probs_t[h % 2][:, :], ps_p[h % 2][:, 0:3 * P]).then_inc(sem["pt_copied"], 1)

            def normalise(s):
                dve.reciprocal(inv[:, :, :], total[s.slot][:, :, :])
                dve.drain()
                dve.wait_ge(sem["o_done"], s.n * LH + LH)
                for t in range(TILES):
                    last = dve.tensor_tensor(attn[:, t, :].rearrange("p (h d) -> p h d", d=LD),
                                             ps_o[t][:, :].rearrange("p (h d) -> p h d", d=LD),
                                             inv[:, t, :].unsqueeze(2).broadcast_to([P, LH, LD]), ALU.mult)
                last.then_inc(sem["attn_ready"], 1)

            def residual(s):
                dve.wait_ge(sem["y_done"], s.n + 1)
                dve.tensor_tensor(seq(dst, s.n), bank[0][:, 0:S].rearrange("p (t d) -> p t d", t=TILES),
                                  seq(src, s.n), ALU.add).then_inc(sem["y_taken"], 1)

            def step(s, finish, front):
                if finish:
                    take_probs(s - 1, LH - 1)
                for h in range(LH):
                    maximum(s, h)
                    if h > 0:
                        take_probs(s, h - 1)
                    if h == 1 and finish:
                        normalise(s - 1)
                    if front:
                        if h == 1:
                            sums(s + 1, 0)
                        if h == 2:
                            turn_k(s + 1)
                            sums(s + 1, 1)
                        if h in (3, 4):
                            norms(s + 1, 2 * h - 6)
                            norms(s + 1, 2 * h - 5)
                        if h in (5, 6):
                            scale(s + 1, h - 5)
                    if finish and h == 5:
                        residual(s - 1)

            for r in range(2):
                dve.memset(shifted[r][0:1, :, D // 2:D], 0.0)
                dve.memset(probs[r][:, :], 0.0)
            dve.drain().then_inc(sem["zeroed"], 1)
            for c in range(2):
                q = scales[:, c, :].unsqueeze(1)
                dve.tensor_tensor(cos[c][:, :, :], cos[c][:, :, :], q.broadcast_to([P, TILES, LD]), ALU.mult)
                for a, b in ((0, LD // 2), (LD // 2, 0)):
                    dve.tensor_tensor(sin[c][:, :, a:a + LD // 2], sin[c][:, :, a:a + LD // 2],
                                      q[:, :, b:b + LD // 2].broadcast_to([P, TILES, LD // 2]), ALU.mult)
            dve.drain().then_inc(sem["zeroed"], 1)
            s0 = Turn(0, 0)
            turn_k(s0)
            sums(s0, 0)
            sums(s0, 1)
            for part in range(4):
                norms(s0, part)
            scale(s0, 0)
            scale(s0, 1)
            run_turns(dve, n_seq, step)
            take_probs(Turn(0, n_seq - 1), LH - 1)
            normalise(Turn(0, n_seq - 1))
            residual(Turn(0, n_seq - 1))



def post_ln_network(nc, x, consts, w, out):
    n_seq = x.shape[0]
    n_groups = n_seq * TILES // GROUP
    every = [P, P]
    with ExitStack() as stack:
        room = Room(nc, stack, "net")
        x_res = room.sb("x_res", [P, n_seq * TILES * D])
        x1_res = room.sb("x1_res", [P, n_seq * TILES * D])
        c = {k: room.sb(k, every) for k in ("ident", "neg_half", "ln_eps", "rms_eps", "eighth")}
        c["ident_bf"] = room.sb("ident_bf", every, BF16)
        c["mask_qk"] = room.sb("mask_qk", [P, TILES, P], BF16)
        c["mask_kq"] = room.sb("mask_kq", [P, TILES, P], BF16)
        c["pick"] = room.sb("pick", [P, HEADS // 2, P], BF16)
        c["band"] = room.sb("band", [P, 5 * WINDOW], BF16)
        c["cos"] = room.sb("cos", [P, TILES, HD])
        c["sin"] = room.sb("sin", [P, TILES, HD])
        c["tril"] = room.sb("tril", [P, 3 * P])
        gqa = {"eighth": c["eighth"]}
        mha = {}
        for k, width in (("qkv", 224), ("out", D), ("gate", D), ("ln1", 1), ("half_bg", 1)):
            gqa[k] = room.sb(f"gqa_{k}", [D, width])
        for k, width in (("b_qkv", 224), ("bo", D), ("qk_norm", 24 * HD)):
            gqa[k] = room.sb(f"gqa_{k}", [P, width])
        for k, width in (("qkv", 384), ("out", D)):
            mha[k] = room.sb(f"mha_{k}", [D, width])
        g = w["gqa"]
        gqa["loads"] = [(gqa[k][:, :], g[k]) for k in ("qkv", "out", "ln1")]
        gqa["loads"] += [(gqa[k][:, :], g[k].broadcast_to([P, g[k].shape[1]])) for k in ("b_qkv", "bo", "qk_norm")]
        for h in range(HEADS):
            at = slice(h * HD, (h + 1) * HD)
            gqa["loads"].append((gqa["gate"][at, at], g["gate"]))
        mha["loads"] = [(mha[k][:, :], w["mha"][k]) for k in ("qkv", "out")]

        with ExitStack() as first:
            early = Room(nc, first, "setup")
            wide = {k: early.sb(k, [P, consts[k].shape[1]]) for k in ("mask_qk", "mask_kq", "pick", "band")}
            loaded = early.sem("loaded")
            block = early.block()

            @block.sync
            def _(sp):
                loads = [(wide[k][:, :], consts[k]) for k in wide]
                loads += [(c["ident"][:, :], consts["ident"]), (c["tril"][:, :], consts["tril"]),
                          (c["cos"][:, :, :], consts["cos"]), (c["sin"][:, :, :], consts["sin"]),
                          (gqa["half_bg"][:, :], g["bg"])]
                for dst, src in loads:
                    sp.dma_start(dst, src).then_inc(loaded, 16)

            @block.vector
            def _(dve):
                dve.memset(gqa["gate"][:, :], 0.0)
                for k, value in (("neg_half", -0.5), ("ln_eps", LN_EPS), ("rms_eps", RMS_EPS), ("eighth", 1.0 / HD)):
                    dve.memset(c[k][:, :], value)
                dve.wait_ge(loaded, 16 * (len(wide) + 5))
                dve.tensor_copy(c["ident_bf"][:, :], c["ident"][:, :])
                for t in range(TILES):
                    dve.tensor_copy(c["mask_qk"][:, t, :], wide["mask_qk"][:, :])
                    dve.tensor_copy(c["mask_kq"][:, t, :], wide["mask_kq"][:, :])
                dve.tensor_copy(c["pick"][:, :, :], wide["pick"][:, :].rearrange("p (j k) -> p j k", k=P))
                dve.tensor_copy(c["band"][:, :], wide["band"][:, :])
                dve.tensor_scalar(gqa["half_bg"][:, :], gqa["half_bg"][:, :], 0.5, None, ALU.mult)

        single_head_attention(nc, x_res, x, w["sha"][0], w["sha"][1], w["sha"][2], c["ident"], c["neg_half"],
                              c["ln_eps"], c["tril"], ahead=gqa["loads"] + mha["loads"])
        with ExitStack() as weights:
            moe, loads = expert_weights(Room(nc, weights, "moe_w"), w["moe"])
            many_head_attention(nc, n_seq, x_res, x1_res, c, gqa, True, ahead=loads)
            mixture_of_experts(nc, n_groups, x_res, x1_res, c, moe)
        with ExitStack() as weights:
            win, win_loads = zip(*(window_weights(Room(nc, weights, f"win_w{n}"), w["win"][n]) for n in range(2)))
            ffn, ffn_loads = zip(*(feed_forward_weights(Room(nc, weights, f"ffn_w{n}"), w["ffn"][n]) for n in range(2)))
            many_head_attention(nc, n_seq, x_res, x_res, c, mha, False, ahead=win_loads[0])
            windowed_attention(nc, n_seq, 0, x_res, x1_res, c, win[0], ahead=ffn_loads[0])
            gated_feed_forward(nc, n_groups, 0, x1_res, c, ffn[0], first=x_res, ahead=win_loads[1])
            windowed_attention(nc, n_seq, 1, x1_res, x1_res, c, win[1], ahead=ffn_loads[1])
            gated_feed_forward(nc, n_groups, 1, x1_res, c, ffn[1], first=x_res, out_dram=out)


def by_token_tile(table):
    n = table.shape[1]
    return np.ascontiguousarray(table.reshape(TILES, P, n).transpose(1, 0, 2)).astype(np.float32)


def rotation(width):
    f4 = np.float32
    inv = f4(1) / f4(10000.0) ** (np.arange(0, width, 2, dtype=f4) / f4(width))
    angle = np.arange(S, dtype=f4)[:, None] * inv[None, :]
    cos, sin = np.cos(angle), np.sin(angle)
    return np.concatenate([cos, cos], 1), np.concatenate([-sin, sin], 1)


def shape_constants():
    f4 = np.float32
    one = np.tril(np.ones((P, P), f4))
    late = np.where(one > 0, f4(0), f4(MASKED))
    pick = np.zeros((P, HEADS // 2, P), f4)
    for j in range(HEADS // 2):
        for half in (0, ROWS):
            pick[half + j, j, :] = 1
            pick[half + HEADS // 2 + j, j, :] = 1
    q = np.arange(P)[:, None]
    k0, k1 = np.arange(P)[None, :], np.arange(WINDOW, S)[None, :]
    near0 = (k0 <= q) & (k0 >= q - WINDOW)
    near1 = (k1 <= q + P) & (k1 >= q + P - WINDOW)
    cos, sin = rotation(HD)
    made = {
        "ident": np.eye(P, dtype=f4), "tril": np.concatenate([one, np.ones((P, P), f4), one], 1),
        "mask_qk": late, "mask_kq": late.T, "pick": pick.reshape(P, -1),
        "band": np.where(np.concatenate([near0, near1], 1), f4(0), f4(MASKED)),
        "cos": by_token_tile(cos), "sin": by_token_tile(sin),
        "experts": np.arange(EXPERTS, dtype=f4)[None, :],
    }
    cos, sin = rotation(LD)
    half = np.arange(0, LD, 2, dtype=f4)
    base = (half + f4(0.4 * LD)) / f4(1.4 * LD)
    power = (np.arange(S, dtype=f4) - S // 2) / f4(WINDOW // 2)
    grow = base[None, :] ** power[:, None]
    grow = np.concatenate([grow, grow], 1)
    for name, table in (("cos", cos), ("sin", sin)):
        made[f"{name}_q"] = by_token_tile(table * grow * f4(8))
        made[f"{name}_k"] = by_token_tile(table / grow)
    return made


def kernel(**inputs):
    import concourse.bacc as bacc
    from concourse.bass_utils import run_bass_kernel_spmd

    a = {k: np.asarray(v) for k, v in inputs.items()}

    def rope_halves(weights):
        return weights.reshape(HEADS, HD // 2, 2, D).transpose(0, 2, 1, 3).reshape(D, D).T

    def keys_twice(weights):
        return np.repeat(weights.reshape(-1, 4, 1, HD), 2, axis=2).reshape(weights.shape[0], -1)

    row = lambda k: a[k].reshape(1, -1)
    column = lambda k: a[k].reshape(-1, 1)
    arrays = {
        "x": a["L0_attn_x"],
        "sha_q": a["L0_attn_WQ"].T, "sha_k": a["L0_attn_WK"].T, "sha_v": a["L0_attn_WV"].T,
        "gqa_qkv": np.concatenate([a["L0_ffn_Wq"], keys_twice(a["L0_ffn_Wk"]), a["L0_ffn_Wv"]], 1),
        "gqa_b_qkv": np.concatenate([row("L0_ffn_bq"), keys_twice(row("L0_ffn_bk")), row("L0_ffn_bv")], 1),
        "gqa_qk_norm": np.concatenate([np.tile(row("L0_ffn_qn_w"), (1, HEADS)), np.tile(row("L0_ffn_kn_w"), (1, 8))], 1),
        "gqa_out": a["L0_ffn_Wo"], "gqa_bo": row("L0_ffn_bo"), "gqa_ln1": column("L0_ffn_ln1_w"),
        "gqa_gate": a["L0_ffn_Wg"], "gqa_bg": np.tile(a["L0_ffn_bg"], HEADS).reshape(-1, 1),
        "moe_W1": a["L0_ffn_W1"], "moe_W2": a["L0_ffn_W2"],
        "moe_b1": a["L0_ffn_b1"].reshape(EXPERTS, 2 * CHUNKS, P).transpose(2, 0, 1),
        "moe_b2": a["L0_ffn_b2"], "moe_Wr": a["L0_ffn_Wr"], "moe_br": row("L0_ffn_br"),
        "moe_ln2": column("L0_ffn_ln2_w"),
        "mha_qkv": np.concatenate([rope_halves(a["L1_attn_Wq"]), rope_halves(a["L1_attn_Wk"]), a["L1_attn_Wv"].T], 1),
        "mha_out": a["L1_attn_Wo"].T,
    }
    for n in range(2):
        arrays.update({
            f"win{n}_qkv": a["L1_ffn_wqkv"][n].reshape(D, 3, INNER), f"win{n}_out": a["L1_ffn_wo"][n],
            f"win{n}_scales": np.stack([a["L1_ffn_q_scale"][n], a["L1_ffn_k_scale"][n]])[None],
            f"ffn{n}_w1": a["L1_ffn_w1"][n], f"ffn{n}_w2": a["L1_ffn_w2"][n],
            f"ffn{n}_b1": a["L1_ffn_b1"][n].reshape(-1, 1), f"ffn{n}_b2": a["L1_ffn_b2"][n].reshape(1, -1),
            f"ffn{n}_ln_g": a["L1_ffn_ln_g"][n].reshape(-1, 1), f"ffn{n}_ln_b": a["L1_ffn_ln_b"][n].reshape(-1, 1),
        })
    arrays.update({f"const_{k}": v for k, v in shape_constants().items()})
    arrays = {f"in_{k}": np.ascontiguousarray(v) for k, v in arrays.items()}

    nc = bacc.Bacc("TRN2", target_bir_lowering=False, num_devices=1)
    t = {k[3:]: nc.dram_tensor(k, v.shape, mybir.dt.from_np(v.dtype), kind="ExternalInput").ap()
         for k, v in arrays.items()}
    out = nc.dram_tensor("out_0", a["L0_attn_x"].shape, F32, kind="ExternalOutput").ap()
    consts = {k[6:]: v for k, v in t.items() if k.startswith("const_")}
    weights = {
        "sha": [t["sha_q"], t["sha_k"], t["sha_v"]],
        "gqa": {k[4:]: v for k, v in t.items() if k.startswith("gqa_")},
        "mha": {k[4:]: v for k, v in t.items() if k.startswith("mha_")},
        "moe": {
            "W1": t["moe_W1"].rearrange("e d f -> d e f"), "b1": t["moe_b1"], "b2": t["moe_b2"],
            "W2": t["moe_W2"].rearrange("e (c p) d -> p e c d", p=P), "Wr": t["moe_Wr"],
            "br": t["moe_br"].broadcast_to([P, EXPERTS]), "ln2": t["moe_ln2"],
            "experts": consts["experts"].broadcast_to([P, EXPERTS]),
        },
        "win": [{
            "qkv": t[f"win{n}_qkv"], "out": t[f"win{n}_out"].rearrange("(c p) d -> p c d", p=P),
            "scales": t[f"win{n}_scales"].broadcast_to([P, 2, LD]),
            "cos": [consts["cos_q"], consts["cos_k"]], "sin": [consts["sin_q"], consts["sin_k"]],
        } for n in range(2)],
        "ffn": [{
            "w1": t[f"ffn{n}_w1"], "w2": t[f"ffn{n}_w2"], "b1": t[f"ffn{n}_b1"],
            "b2": t[f"ffn{n}_b2"].broadcast_to([P, D]), "ln_g": t[f"ffn{n}_ln_g"], "ln_b": t[f"ffn{n}_ln_b"],
        } for n in range(2)],
    }
    post_ln_network(nc, t["x"], consts, weights, out)
    result = run_bass_kernel_spmd(nc, [arrays], core_ids=[0])
    return result.results[0]["out_0"]
```
